# Optimizing a Trainium2 kernel written in Bass

```python
import numpy as np
import jax
import jax.numpy as jnp

def _softmax(x, axis=-1):
    return jax.nn.softmax(x, axis=axis)

def _gelu(x):
    return jax.nn.gelu(x, approximate=True)

def _silu(x):
    return jax.nn.silu(x)

def _sigmoid(x):
    return jax.nn.sigmoid(x)

def _layernorm(x, axis=-1, eps=1e-05):
    m = jnp.mean(x, axis=axis, keepdims=True)
    v = jnp.var(x, axis=axis, keepdims=True)
    return (x - m) / jnp.sqrt(v + eps)

def _scatter_add(tgt, idx, src, axis=0):
    return tgt.at[idx].add(src)

def _segment_sum(src, seg, n):
    return jax.ops.segment_sum(src, seg, n)
kernel_name = 'mk_xattn_ffn_d2_seqx_r4_a9679f'

def setup_inputs(seed: int=0):
    np.random.seed(seed)
    _w = jnp.asarray

    def _rec_inputs():
        import jax
        import jax.numpy as jnp
        _rk = jax.random.key(seed)
        x = -0.000929 + 1 * jax.random.normal(jax.random.fold_in(_rk, 1), (8, 100, 512), jnp.float32)
        _lenS = 100 - jax.random.randint(jax.random.fold_in(_rk, 7), (8,), 0, max(1, 100 // 4) + 1, jnp.int32)
        _lenS2 = 361 - jax.random.randint(jax.random.fold_in(_rk, 8), (8,), 0, max(1, 361 // 4) + 1, jnp.int32)
        _ctx_2048P = jax.random.normal(jax.random.fold_in(_rk, 11), (8, 16, 512), jnp.float32)
        _ctx_2048c = jax.random.dirichlet(jax.random.fold_in(_rk, 511), 0.3 * jnp.ones((16,), jnp.float32), (8, 361))
        _ctx_2048t = jnp.einsum('bsk,bkd->bsd', _ctx_2048c, _ctx_2048P)
        _ctx_2048t = _ctx_2048t * jax.lax.rsqrt(jnp.mean(jnp.square(_ctx_2048t)) + 1e-12) * 0.953939
        ctx_2048 = 2.81802e-05 + 1.00001 * (_ctx_2048t + 0.3 * jax.random.normal(jax.random.fold_in(_rk, 611), (8, 361, 512), jnp.float32))
        _validS = jnp.arange(100)[None, :] < _lenS[:, None]
        _validS2 = jnp.arange(361)[None, :] < _lenS2[:, None]
        _causal = jnp.tril(jnp.ones((100, 100), dtype=bool))
        mask_BxSxS2_ff0 = jnp.where(jnp.ones((8, 100, 361), dtype=bool), 0.0, -1000000000.0).astype(jnp.float32)
        return (x, ctx_2048, mask_BxSxS2_ff0)
    x, ctx_2048, mask_BxSxS2_ff0 = _rec_inputs()

    def _L0_xattn_setup():
        import jax, jax.numpy as jnp
        import numpy as np
        from jax import lax
        LN_EPS = 1e-05
        key = jax.random.key(seed)
        ks = jax.random.split(key, 8)
        B, S, T, D = (4, 128, 512, 512)
        scale = 0.02
        return {'Z': jax.random.normal(ks[0], (B, S, D), dtype=jnp.float32), 'kv': jax.random.normal(ks[1], (B, T, D), dtype=jnp.float32), 'decay': jnp.float32(0.9), 'W_in': jax.random.normal(ks[2], (D, D), dtype=jnp.float32) * scale, 'b_in': jnp.zeros((D,), dtype=jnp.float32), 'W_out': jax.random.normal(ks[3], (D, D), dtype=jnp.float32) * scale, 'b_out': jnp.zeros((D,), dtype=jnp.float32), 'gamma': jnp.ones((D,), dtype=jnp.float32), 'beta': jnp.zeros((D,), dtype=jnp.float32)}
    _L0_xattn_all = _L0_xattn_setup()
    _L0_xattn_in = {k: v for k, v in _L0_xattn_all.items() if k in ('decay', 'W_in', 'b_in', 'W_out', 'b_out', 'gamma', 'beta')}
    del _L0_xattn_all

    def _L0_ffn_setup():
        import jax, jax.numpy as jnp
        import numpy as np
        DIM = 512
        HIDDEN = 2048
        EPS = 1e-06

        def rms_norm(x, gamma):
            var = jnp.mean(x * x, axis=-1, keepdims=True)
            return x * jax.lax.rsqrt(var + EPS) * gamma

        def activation_quant(x):
            scale = 127.0 / jnp.maximum(jnp.max(jnp.abs(x), axis=-1, keepdims=True), 1e-05)
            return jnp.clip(jnp.round(x * scale), -128.0, 127.0) / scale

        def weight_quant(w):
            scale = 1.0 / jnp.maximum(jnp.mean(jnp.abs(w)), 1e-05)
            return jnp.clip(jnp.round(w * scale), -1.0, 1.0) / scale

        def bit_linear(x, w):
            xq = x + jax.lax.stop_gradient(activation_quant(x) - x)
            wq = w + jax.lax.stop_gradient(weight_quant(w) - w)
            return jnp.einsum('bsi,oi->bso', xq, wq)
        key = jax.random.key(seed)
        k_x, k_w1, k_w2 = jax.random.split(key, 3)
        x = jax.random.normal(k_x, (4, 512, DIM), dtype=jnp.float32)
        b1 = 1.0 / np.sqrt(DIM)
        b2 = 1.0 / np.sqrt(HIDDEN)
        w1 = jax.random.uniform(k_w1, (HIDDEN, DIM), dtype=jnp.float32, minval=-b1, maxval=b1)
        w2 = jax.random.uniform(k_w2, (DIM, HIDDEN), dtype=jnp.float32, minval=-b2, maxval=b2)
        gamma = jnp.ones((DIM,), dtype=jnp.float32)
        return {'x': x, 'w1': w1, 'w2': w2, 'gamma': gamma}
    _L0_ffn_all = _L0_ffn_setup()
    _L0_ffn_in = {k: v for k, v in _L0_ffn_all.items() if k in ('w1', 'w2', 'gamma')}
    del _L0_ffn_all

    def _L1_xattn_setup():
        import jax, jax.numpy as jnp
        import numpy as np
        NUM_HEADS = 16
        EPS = 1e-08

        def _dyn_quant(x):
            s = jnp.maximum(jnp.max(jnp.abs(x), axis=-1, keepdims=True) / 127.0, EPS)
            q = jnp.clip(jnp.round(x / s), -127.0, 127.0)
            return (q, s)

        def _quant_weight(w):
            s = jnp.maximum(jnp.max(jnp.abs(w), axis=1, keepdims=True) / 127.0, EPS)
            q = jnp.clip(jnp.round(w / s), -127.0, 127.0)
            return (q, s)

        def _w8a8_linear(x, w, b):
            qx, sx = _dyn_quant(x)
            qw, sw = _quant_weight(w)
            y = jnp.einsum('bnc,oc->bno', qx, qw) * (sx * sw[:, 0])
            return y + b
        key = jax.random.key(seed)
        ks = jax.random.split(key, 9)
        B, N, L, C = (2, 1024, 128, 512)
        sc = 0.02
        return {'x': jax.random.normal(ks[0], (B, N, C), jnp.float32), 'cond': jax.random.normal(ks[1], (B, L, C), jnp.float32), 'mask': jnp.zeros((B, N, L), jnp.float32), 'wq': jax.random.normal(ks[2], (C, C), jnp.float32) * sc, 'bq': jnp.zeros((C,), jnp.float32), 'wk': jax.random.normal(ks[3], (C, C), jnp.float32) * sc, 'bk': jnp.zeros((C,), jnp.float32), 'wv': jax.random.normal(ks[4], (C, C), jnp.float32) * sc, 'bv': jnp.zeros((C,), jnp.float32), 'wo': jax.random.normal(ks[5], (C, C), jnp.float32) * sc, 'bo': jnp.zeros((C,), jnp.float32)}
    _L1_xattn_all = _L1_xattn_setup()
    _L1_xattn_in = {k: v for k, v in _L1_xattn_all.items() if k in ('wq', 'bq', 'wk', 'bk', 'wv', 'bv', 'wo', 'bo')}
    del _L1_xattn_all

    def _L1_ffn_setup():
        import jax, jax.numpy as jnp
        import numpy as np
        E, TOP_K, D, H = (8, 2, 512, 352)
        B, S = (2, 512)
        key = jax.random.key(seed)
        ks = jax.random.split(key, 8)
        x = jax.random.normal(ks[0], (B, S, D), dtype=jnp.float32)
        gate_w = jax.random.normal(ks[1], (E, D), dtype=jnp.float32) * (1.0 / np.sqrt(D))
        gate_b = jax.random.normal(ks[2], (E,), dtype=jnp.float32) * 0.01
        bias = jnp.zeros((E,), dtype=jnp.float32)
        w1 = jax.random.normal(ks[3], (E, H, D), dtype=jnp.float32) * (1.0 / np.sqrt(D))
        b1 = jax.random.normal(ks[4], (E, H), dtype=jnp.float32) * 0.01
        w2 = jax.random.normal(ks[5], (E, D, H), dtype=jnp.float32) * (1.0 / np.sqrt(H))
        b2 = jax.random.normal(ks[6], (E, D), dtype=jnp.float32) * 0.01
        return {'x': x, 'gate_w': gate_w, 'gate_b': gate_b, 'bias': bias, 'w1': w1, 'b1': b1, 'w2': w2, 'b2': b2}
    _L1_ffn_all = _L1_ffn_setup()
    _L1_ffn_in = {k: v for k, v in _L1_ffn_all.items() if k in ('gate_w', 'gate_b', 'bias', 'w1', 'b1', 'w2', 'b2')}
    del _L1_ffn_all
    return {'x': x, 'ctx_2048': ctx_2048, 'mask_BxSxS2_ff0': mask_BxSxS2_ff0, 'L0_xattn_decay': _L0_xattn_in['decay'], 'L0_xattn_W_in': _L0_xattn_in['W_in'], 'L0_xattn_b_in': _L0_xattn_in['b_in'], 'L0_xattn_W_out': _L0_xattn_in['W_out'], 'L0_xattn_b_out': _L0_xattn_in['b_out'], 'L0_xattn_gamma': _L0_xattn_in['gamma'], 'L0_xattn_beta': _L0_xattn_in['beta'], 'L0_ffn_w1': _L0_ffn_in['w1'], 'L0_ffn_w2': _L0_ffn_in['w2'], 'L0_ffn_gamma': _L0_ffn_in['gamma'], 'L1_xattn_wq': _L1_xattn_in['wq'], 'L1_xattn_bq': _L1_xattn_in['bq'], 'L1_xattn_wk': _L1_xattn_in['wk'], 'L1_xattn_bk': _L1_xattn_in['bk'], 'L1_xattn_wv': _L1_xattn_in['wv'], 'L1_xattn_bv': _L1_xattn_in['bv'], 'L1_xattn_wo': _L1_xattn_in['wo'], 'L1_xattn_bo': _L1_xattn_in['bo'], 'L1_ffn_gate_w': _L1_ffn_in['gate_w'], 'L1_ffn_gate_b': _L1_ffn_in['gate_b'], 'L1_ffn_bias': _L1_ffn_in['bias'], 'L1_ffn_w1': _L1_ffn_in['w1'], 'L1_ffn_b1': _L1_ffn_in['b1'], 'L1_ffn_w2': _L1_ffn_in['w2'], 'L1_ffn_b2': _L1_ffn_in['b2']}

def reference(x, ctx_2048, mask_BxSxS2_ff0, L0_xattn_decay, L0_xattn_W_in, L0_xattn_b_in, L0_xattn_W_out, L0_xattn_b_out, L0_xattn_gamma, L0_xattn_beta, L0_ffn_w1, L0_ffn_w2, L0_ffn_gamma, L1_xattn_wq, L1_xattn_bq, L1_xattn_wk, L1_xattn_bk, L1_xattn_wv, L1_xattn_bv, L1_xattn_wo, L1_xattn_bo, L1_ffn_gate_w, L1_ffn_gate_b, L1_ffn_bias, L1_ffn_w1, L1_ffn_b1, L1_ffn_w2, L1_ffn_b2):
    import jax
    import jax.numpy as jnp

    def _L0_xattn_ref(Z, kv, decay, W_in, b_in, W_out, b_out, gamma, beta):
        import jax, jax.numpy as jnp
        import numpy as np
        from jax import lax
        LN_EPS = 1e-05
        B, T, D = kv.shape
        K = jax.nn.sigmoid(decay)
        x = jnp.einsum('btd,ed->bte', kv, W_in) + b_in

        def scan_fn(s, xt):
            s = K * s + xt
            return (s, s)
        s0 = jnp.zeros((B, D), dtype=kv.dtype)
        _, states = lax.scan(scan_fn, s0, jnp.swapaxes(x, 0, 1))
        states = jnp.swapaxes(states, 0, 1)
        proj = jnp.einsum('btd,ed->bte', states, W_out) + b_out
        summary = jnp.mean(proj, axis=1, keepdims=True)
        y = Z + summary
        mu = jnp.mean(y, axis=-1, keepdims=True)
        var = jnp.mean((y - mu) ** 2, axis=-1, keepdims=True)
        return (y - mu) / jnp.sqrt(var + LN_EPS) * gamma + beta

    def _L0_ffn_ref(x, w1, w2, gamma):
        import jax, jax.numpy as jnp
        import numpy as np
        DIM = 512
        HIDDEN = 2048
        EPS = 1e-06

        def rms_norm(x, gamma):
            var = jnp.mean(x * x, axis=-1, keepdims=True)
            return x * jax.lax.rsqrt(var + EPS) * gamma

        def activation_quant(x):
            scale = 127.0 / jnp.maximum(jnp.max(jnp.abs(x), axis=-1, keepdims=True), 1e-05)
            return jnp.clip(jnp.round(x * scale), -128.0, 127.0) / scale

        def weight_quant(w):
            scale = 1.0 / jnp.maximum(jnp.mean(jnp.abs(w)), 1e-05)
            return jnp.clip(jnp.round(w * scale), -1.0, 1.0) / scale

        def bit_linear(x, w):
            xq = x + jax.lax.stop_gradient(activation_quant(x) - x)
            wq = w + jax.lax.stop_gradient(weight_quant(w) - w)
            return jnp.einsum('bsi,oi->bso', xq, wq)
        h = bit_linear(rms_norm(x, gamma), w1)
        h = jax.nn.gelu(h, approximate=False)
        return bit_linear(h, w2)

    def _L1_xattn_ref(x, cond, mask, wq, bq, wk, bk, wv, bv, wo, bo):
        import jax, jax.numpy as jnp
        import numpy as np
        NUM_HEADS = 16
        EPS = 1e-08

        def _dyn_quant(x):
            s = jnp.maximum(jnp.max(jnp.abs(x), axis=-1, keepdims=True) / 127.0, EPS)
            q = jnp.clip(jnp.round(x / s), -127.0, 127.0)
            return (q, s)

        def _quant_weight(w):
            s = jnp.maximum(jnp.max(jnp.abs(w), axis=1, keepdims=True) / 127.0, EPS)
            q = jnp.clip(jnp.round(w / s), -127.0, 127.0)
            return (q, s)

        def _w8a8_linear(x, w, b):
            qx, sx = _dyn_quant(x)
            qw, sw = _quant_weight(w)
            y = jnp.einsum('bnc,oc->bno', qx, qw) * (sx * sw[:, 0])
            return y + b
        B, N, C = x.shape
        L = cond.shape[1]
        H = NUM_HEADS
        D = C // H
        inv_sqrt_d = np.float32(1.0 / np.sqrt(D))
        q = _w8a8_linear(x, wq, bq).reshape(B, N, H, D).transpose(0, 2, 1, 3)
        k = (cond @ wk.T + bk).reshape(B, L, H, D).transpose(0, 2, 1, 3)
        v = (cond @ wv.T + bv).reshape(B, L, H, D).transpose(0, 2, 1, 3)
        scores = jnp.einsum('bhnd,bhld->bhnl', q, k) * inv_sqrt_d + mask[:, None]
        attn = jax.nn.softmax(scores, axis=-1)
        o = jnp.einsum('bhnl,bhld->bhnd', attn, v)
        o = o.transpose(0, 2, 1, 3).reshape(B, N, C)
        return _w8a8_linear(o, wo, bo)

    def _L1_ffn_ref(x, gate_w, gate_b, bias, w1, b1, w2, b2):
        import jax, jax.numpy as jnp
        import numpy as np
        E, TOP_K, D, H = (8, 2, 512, 352)
        B, S = (2, 512)
        b, s, d = x.shape
        xf = x.reshape(-1, d)
        scores = xf @ gate_w.T + gate_b + bias
        top_scores, top_idx = jax.lax.top_k(scores, TOP_K)
        gates = jax.nn.softmax(top_scores, axis=-1)
        comb = jnp.sum(jax.nn.one_hot(top_idx, E, dtype=gates.dtype) * gates[..., None], axis=1)
        h = jax.nn.silu(jnp.einsum('td,ehd->teh', xf, w1) + b1)
        y = jnp.einsum('teh,edh->ted', h, w2) + b2
        out = jnp.einsum('ted,te->td', y, comb)
        return out.reshape(b, s, d)
    x = x + _L0_xattn_ref(_layernorm(x, axis=-1), ctx_2048, L0_xattn_decay, L0_xattn_W_in, L0_xattn_b_in, L0_xattn_W_out, L0_xattn_b_out, L0_xattn_gamma, L0_xattn_beta)
    x = x + _L0_ffn_ref(_layernorm(x, axis=-1), L0_ffn_w1, L0_ffn_w2, L0_ffn_gamma)
    x = x + _L1_xattn_ref(_layernorm(x, axis=-1), ctx_2048, mask_BxSxS2_ff0, L1_xattn_wq, L1_xattn_bq, L1_xattn_wk, L1_xattn_bk, L1_xattn_wv, L1_xattn_bv, L1_xattn_wo, L1_xattn_bo)
    x = x + _L1_ffn_ref(_layernorm(x, axis=-1), L1_ffn_gate_w, L1_ffn_gate_b, L1_ffn_bias, L1_ffn_w1, L1_ffn_b1, L1_ffn_w2, L1_ffn_b2)
    return x

_drawn_inputs = setup_inputs


def setup_inputs(seed=0):
    import zlib

    import numpy as np

    out = dict(_drawn_inputs(seed))
    spreads = {'L0_xattn_b_in': (0.0, 0.1),
     'L0_xattn_b_out': (0.0, 0.1),
     'L0_xattn_gamma': (1.0, 0.2),
     'L0_xattn_beta': (0.0, 0.1),
     'L0_ffn_gamma': (1.0, 0.6),
     'L1_xattn_bq': (0.0, 0.8),
     'L1_xattn_bk': (0.0, 2.0),
     'L1_xattn_bv': (0.0, 0.1),
     'L1_xattn_bo': (0.0, 0.1),
     'L1_ffn_bias': (0.0, 0.1)}
    factors = {'L1_xattn_wq': 6.785,
     'L1_xattn_wk': 8.0,
     'L1_ffn_gate_b': 5.858,
     'L1_ffn_b1': 25.192,
     'L1_ffn_b2': 8.0}
    for name, (base, spread) in spreads.items():
        noise = np.random.default_rng([zlib.crc32(name.encode()), seed]).standard_normal(out[name].shape)
        drawn = base * np.exp(spread * noise) if base else spread * noise
        out[name] = jnp.asarray(drawn.astype(out[name].dtype))
    for name, factor in factors.items():
        out[name] = (out[name] * factor).astype(out[name].dtype)
    return out
```

```python
from contextlib import ExitStack

import concourse.bass as bass
from concourse import mybir

ALU = mybir.AluOpType
ACT = mybir.ActivationFunctionType
AX = mybir.AxisListType
F32 = mybir.dt.float32
F32R = mybir.dt.float32r
BF16 = mybir.dt.bfloat16
FP8 = mybir.dt.float8e4
U32 = mybir.dt.uint32

B, S, D = 8, 100, 512
T = 361
P = 128
KC = D // P
NT = 3
TC = -(-T // NT)
TP = 364
HEADS, HD = 16, 32
HPC = P // HD
VW = HEADS * (HD + 1)
FF = 2048
FC = FF // P
NW = 4
WP = D * FF // P // NW
E, EH = 8, 352
EC = 118
EHP = 3 * EC
LN_EPS, RMS_EPS = 1e-5, 1e-6
MAGIC = 1.5 * 2.0 ** 23
QMAX = 127.0


def block_kernel(nc, x, ctxT, mask, decay, win, b_in, wout, b_out, gamma0, beta0, w1, w2, gammaf,
                 wq, bq, wk, bk, wv, bv, wo, bo, gate_w, gate_b, gate_bias, ew1, eb1, ew2, out):
    with ExitStack() as whole:
        def sb(stack, name, shape, dt=F32):
            return stack.enter_context(nc.sbuf_tensor(name, shape, dt))

        sems = {}

        def sem(name):
            if name not in sems:
                sems[name] = whole.enter_context(nc.semaphore(name))
            return sems[name]

        credited = ("g1", "g2", "gelu", "h_t", "hq0", "hq1", "hqT0", "hs", "k_copied", "moe_done", "oQT", "oQb",
                    "o_norm", "summ_used", "t1", "t2", "v_copied", "v_mm", "x1", "x2", "x3",
                    *(f"{name}{r}" for name in ("exp", "masked", "p_copied", "p_turned", "pv", "score")
                      for r in range(2)))

        def after(count):
            return count + 1

        summ_dram = nc.dram_tensor("summary_rows", [B, D], F32, kind="Internal").ap()
        swo_dram = nc.dram_tensor("wo_scales", [D], F32, kind="Internal").ap()

        CT = sb(whole, "CT", [P, B, KC * TP])
        VS = sb(whole, "VS", [P, B * NT * VW])
        XR = sb(whole, "XR", [P, B, D])
        ident = sb(whole, "ident", [P, P])
        identb = sb(whole, "identb", [P, P], BF16)
        ones = sb(whole, "ones", [P, P])
        cols = sb(whole, "cols", [P, 48])
        ps = whole.enter_context(nc.psum_tensor("ps", [P, 8, 512], F32))

        def vs(b):
            return VS[:, bass.ds(b * (NT * VW), NT * VW)]

        a = ExitStack()
        wkH, wkL = sb(a, "wkH", [P, KC, D], F32R), sb(a, "wkL", [P, KC, D], F32R)
        wvH, wvL = sb(a, "wvH", [P, KC, D], F32R), sb(a, "wvL", [P, KC, D], F32R)
        cxH, cxL = sb(a, "cxH", [P, KC, TP], F32R), sb(a, "cxL", [P, KC, TP], F32R)
        w1s = sb(a, "w1s", [P, KC * D])
        w2s = sb(a, "w2s", [P, KC * D])
        w1q = w1s[:].bitcast(FP8)
        w2q = w2s[:].bitcast(FP8)
        h = sb(a, "h", [P, FF])
        hq = sb(a, "hq", [P, FF], BF16)
        hqT = sb(a, "hqT", [P, FC, S], BF16)
        xq, y, xb = sb(a, "xq", [P, D]), sb(a, "y", [P, D]), sb(a, "xb", [P, D])
        xqb = sb(a, "xqb", [P, D], BF16)
        xqT = sb(a, "xqT", [P, KC, S], BF16)
        summB = sb(a, "summB", [P, D])
        gamma0B, beta0B, gammafB = sb(a, "gamma0B", [P, D]), sb(a, "beta0B", [P, D]), sb(a, "gammafB", [P, D])
        kvw, xm = sb(a, "kvw", [P, KC, B]), sb(a, "xm", [P, KC, B])
        biases = sb(a, "biases", [P, 3, KC])
        st6 = sb(a, "st6", [P, 6])
        mv = sb(a, "mv", [P, 2])
        mv0 = sb(a, "mv0", [P, B, 2])
        st0 = sb(a, "st0", [P, B, 6])
        rs0 = sb(a, "rs0", [P, B])
        tk = sb(a, "tk", [P, 24])
        asum = sb(a, "asum", [P, 2, NW])
        wsc = sb(a, "wsc", [P, 2, 4])
        cw, krow = h[:, 0:TP], h[:, TP:2 * TP]
        junk = [h[:, (2 + i) * TP:(2 + i) * TP + T] for i in range(3)]
        summ, boutB = xq[0:B, :], y[0:B, :]
        a.close()

        def stage(i):
            at = 2 * NT * VW + (i % NW) * WP
            return VS[:, at:at + WP]

        bb = ExitStack()
        staging = ExitStack()
        wst = sb(staging, "wst", [P, 2, KC, D])
        wstb = sb(staging, "wstb", [P, 2, KC, D], BF16)
        staging.close()
        KH = [sb(bb, f"KH{i}", [P, KC, TP], F32R) for i in range(2)]
        KL = [sb(bb, f"KL{i}", [P, KC, TP], F32R) for i in range(2)]
        qH = [sb(bb, f"qH{i}", [P, KC, S], F32R) for i in range(2)]
        qL = [sb(bb, f"qL{i}", [P, KC, S], F32R) for i in range(2)]
        maskS = sb(bb, "maskS", [P, 2, T + 1])
        sN = sb(bb, "sN", [P, 2, TP])
        pE = sb(bb, "pE", [P, 2, NT * TC + 1])
        pT = sb(bb, "pT", [P, 2, NT, S])
        nmx = sb(bb, "nmx", [P, HEADS])
        oN, oQ = sb(bb, "oN", [P, D]), sb(bb, "oQ", [P, D])
        oQb = sb(bb, "oQb", [P, D], BF16)
        oQT = sb(bb, "oQT", [P, KC, S], BF16)
        g2, xq2 = sb(bb, "g2", [P, D]), sb(bb, "xq2", [P, D])
        xq2b = sb(bb, "xq2b", [P, D], BF16)
        xq2T = sb(bb, "xq2T", [P, KC, S], BF16)
        xbo, y2 = sb(bb, "xbo", [P, D]), sb(bb, "y2", [P, D])
        sxB = sb(bb, "sxB", [P, S])
        t1, t2, t3 = (sb(bb, f"qt{i}", [P, KC, S]) for i in range(3))
        swqB, bqB = sb(bb, "swqB", [P, KC, S]), sb(bb, "bqB", [P, KC, S])
        bvB, boB, swoB = sb(bb, "bvB", [P, D]), sb(bb, "boB", [P, D]), sb(bb, "swoB", [P, D])
        wqT = sb(bb, "wqT", [P, 2, KC, D], BF16)
        wsm = sb(bb, "wsm", [P, 4, 2, KC])
        bqS = sb(bb, "bqS", [P, KC])
        st6b, mvb = sb(bb, "st6b", [P, 6]), sb(bb, "mvb", [P, 2])
        tb = sb(bb, "tb", [P, 24])
        rinv = sb(bb, "rinv", [P, HEADS])
        bb.close()

        cc = ExitStack()
        z, zT = sb(cc, "z", [P, 2, D]), sb(cc, "zT", [P, 2, KC, S])
        st6c, mvc, tc_ = sb(cc, "st6c", [P, 6]), sb(cc, "mvc", [P, 2]), sb(cc, "tc", [P, 8])
        gwT, gbB = sb(cc, "gwT", [P, KC, E]), sb(cc, "gbB", [P, 2, E])
        sc, top, idx = sb(cc, "sc", [P, E]), sb(cc, "top", [P, E]), sb(cc, "idx", [P, E], U32)
        idf, iot, comb, comb2 = sb(cc, "idf", [P, E]), sb(cc, "iot", [P, E]), sb(cc, "comb", [P, E]), sb(cc, "comb2", [P, E])
        b1B = sb(cc, "b1B", [P, E, EH])
        hb, hs, hTe = sb(cc, "hb", [P, EH]), sb(cc, "hs", [P, 2, EHP]), sb(cc, "hTe", [P, 3, S])
        cc.close()

        C_MAGIC, C_NMAGIC, C_HALF, C_DEC, C_K, C_SUM = 0, 1, 2, 3, 4, 5
        C_EXP = 6

        def batches(eng, body):
            body(0, 0, 0, True, False)
            with eng.Fori(0, B // 2 - 1) as it:
                body(it * 2 + 1, 1, it, False, False)
                body(it * 2 + 2, 0, it + 1, False, False)
            body(B - 1, 1, B // 2 - 1, False, True)

        def chain(eng, name, per):
            class Chain:
                def turn(self, t):
                    self.base, self.k = t * per, 0

                def __call__(self, ins, by_itself=False):
                    self.k += 1
                    ins.then_inc(sem(name), 1)
                    if by_itself:
                        alone(eng, (name, self.base + self.k))
                    else:
                        eng.wait_ge(sem(name), self.base + self.k)

                def end(self):
                    assert self.k == per, (name, self.k)
            return Chain()

        def scores_done(eng, b):
            if not isinstance(b, int) or b > 0:
                for r in range(2):
                    eng.wait_ge(sem(f"score{r}"), after(b * 8))

        def alone(eng, *waits):
            for name, v in waits:
                eng.wait_ge(sem(name), v)
            eng.sem_inc(sem("gone_on"), 1)

        def copies_on_act(h_):
            return h_ % 3 != 2

        def copy_p(eng, copy, b, h_):
            r, n = h_ % 2, b * 8 + h_ // 2
            eng.wait_ge(sem(f"p_turned{r}"), after(n + 1))
            eng.wait_ge(sem(f"pv{r}"), after(n))
            copy(pT[0:TC, r].rearrange("p c s -> p (c s)"), ps[0:TC, 2 + r, 0:NT * S]).then_inc(sem(f"p_copied{r}"), 1)

        block = whole.enter_context(nc.Block())

        @block.sync
        def _(sp):
            sp.dma_start(cols[:, C_DEC:C_DEC + 1], decay.partition_broadcast(P)).then_inc(sem("decay_in"), 16)
            sp.dma_start(biases[:, 0, :], b_in).then_inc(sem("biases_in"), 16)
            sp.dma_start(biases[:, 1, :], bk).then_inc(sem("biases_in"), 16)
            sp.dma_start(CT[:, 0, :], ctxT[0]).then_inc(sem("ctx_in0"), 16)
            sp.dma_start(stage(0), wk).then_inc(sem("stage_in0"), 16)
            sp.dma_start(stage(1), wv).then_inc(sem("stage_in1"), 16)
            for c in range(2):
                sp.dma_start(stage(2 + c), w1[c]).then_inc(sem(f"stage_in{2 + c}"), 16)
            for b in range(1, B):
                sp.dma_start(CT[:, b, :], ctxT[b]).then_inc(sem(f"ctx_in{b}"), 16)
            for c in range(2, NW):
                sp.wait_ge(sem("wkvL"), c - 1)
                sp.dma_start(stage(2 + c), w1[c]).then_inc(sem(f"stage_in{c - 2}"), 16)
            sp.dma_start(w1s[:], win).then_inc(sem("win_in"), 16)
            sp.dma_start(w2s[:], wout).then_inc(sem("win_in"), 16)
            sp.dma_start(boutB, b_out.partition_broadcast(B)).then_inc(sem("bout_in"), 16)
            sp.dma_start(XR[0:S], x).then_inc(sem("x_in"), 16)
            for t, src in ((gamma0B, gamma0), (beta0B, beta0), (gammafB, gammaf)):
                sp.dma_start(t[0:S, :], src.partition_broadcast(S)).then_inc(sem("vec_in"), 16)
            for c in range(NW):
                sp.wait_ge(sem("ternary"), c + 1)
                sp.dma_start(stage(2 + c), w2[c]).then_inc(sem(f"stage_in{(2 + c) % NW}"), 16)
            sp.wait_ge(sem("summ_ready"), 1)
            sp.dma_start(summ_dram, summ).then_inc(sem("summ_out"), 16)
            sp.wait_ge(sem("summ_out"), 16)
            with sp.Fori(0, B) as b:
                sp.wait_ge(sem("summ_used"), after(b))
                sp.dma_start(summB[0:S], summ_dram[b].partition_broadcast(S)).then_inc(sem("summ_in"), 16)
            for e in ("dve", "act", "pe", "pool"):
                sp.wait_ge(sem(f"a_done_{e}"), 1)
            sp.dma_start(wst[:, 0], wq).then_inc(sem("wqo_in"), 16)
            sp.dma_start(wst[:, 1], wo).then_inc(sem("wqo_in"), 16)
            sp.dma_start(bqS[:], bq).then_inc(sem("bq_in"), 16)
            for t, src in ((bvB, bv), (boB, bo)):
                sp.dma_start(t[0:S, :], src.partition_broadcast(S)).then_inc(sem("bvo_in"), 16)
            sp.wait_ge(sem("wscale"), 1)
            sp.dma_start(swo_dram.rearrange("(j p) -> p j", p=P), wsm[:, 1, 1, :], allow_slow_non_contiguous=True)\
              .then_inc(sem("swo_out"), 16)
            sp.wait_ge(sem("swo_out"), 16)
            sp.dma_start(swoB[0:S, :], swo_dram.partition_broadcast(S)).then_inc(sem("bvo_in"), 16)
            for j in range(2):
                sp.dma_start(maskS[0:S, j, 0:T], mask[j]).then_inc(sem(f"mask_in{j}"), 16)

            def expert_loads(b, j, more):
                sp.wait_ge(sem("kL"), b + 1)
                sp.dma_start(CT[:, b, 0:KC * EH], ew1[b]).then_inc(sem("ew1_in"), 16)
                sp.wait_ge(sem("o_norm"), after(b + 1))
                sp.dma_start(vs(b)[0:EC, 0:3 * D], ew2[b]).then_inc(sem("ew2_in"), 16)
                if more:
                    sp.wait_ge(sem("mask_used"), b + 1)
                    sp.dma_start(maskS[0:S, j, 0:T], mask[b + 2]).then_inc(sem(f"mask_in{j}"), 16)

            with sp.Fori(0, B // 2 - 1) as it:
                for j in range(2):
                    expert_loads(it * 2 + j, j, True)
            expert_loads(B - 2, 0, False)
            expert_loads(B - 1, 1, False)
            for e in ("dve", "act", "pe", "pool"):
                sp.wait_ge(sem(f"b_done_{e}"), 1)
            sp.dma_start(gwT[:], gate_w).then_inc(sem("c_in"), 16)
            sp.dma_start(gbB[0:S, 0, :], gate_b.partition_broadcast(S)).then_inc(sem("c_in"), 16)
            sp.dma_start(gbB[0:S, 1, :], gate_bias.partition_broadcast(S)).then_inc(sem("c_in"), 16)
            sp.dma_start(b1B[0:S], eb1.partition_broadcast(S)).then_inc(sem("c_in"), 16)
            with sp.Fori(0, B) as b:
                sp.wait_ge(sem("moe_done"), after((b + 1) * E))
                sp.dma_start(out[b], XR[0:S, b, :]).then_inc(sem("out"), 16)
            sp.wait_ge(sem("out"), 16 * B)

        @block.gpsimd
        def _(g):
            n = [0]

            def step(ins):
                n[0] += 1
                ins.then_inc(sem("pool_setup"), 1)
                g.wait_ge(sem("pool_setup"), n[0])

            step(g.iota(ident[:], [[1, P]], base=0, channel_multiplier=-1, allow_small_or_imprecise_dtypes=True))
            step(g.tensor_scalar(ident[:], ident[:], 0.0, None, ALU.is_equal))
            step(g.tensor_copy(identb[:], ident[:]))
            step(g.memset(ones[:], 1.0))
            g.memset(cols[:, C_MAGIC:C_MAGIC + 1], MAGIC)
            g.memset(cols[:, C_NMAGIC:C_NMAGIC + 1], -MAGIC)
            g.memset(cols[:, C_HALF:C_HALF + 1], -0.5).then_inc(sem("consts"), 1)
            g.wait_ge(sem("consts"), 1)

            def rsqrt(dst, src, tmp, eps, tag, count, width=1):
                g.tensor_scalar(tmp, src, eps, None, ALU.add).then_inc(sem(tag + "_t"), 1)
                g.wait_ge(sem(tag + "_t"), count)
                half = cols[0:S, C_HALF:C_HALF + 1]
                half = half if width == 1 else half.to_broadcast([S, width])
                return g.tensor_tensor(dst, tmp, half, ALU.pow)

            g.wait_ge(sem("mv0"), B)
            rsqrt(rs0[0:S, :], mv0[0:S, :, 1], rs0[0:S, :], LN_EPS, "rs0", 1, B).then_inc(sem("rs0"), 1)
            with g.Fori(0, B) as b:
                g.wait_ge(sem("cxH"), b + 1)
                g.tensor_tensor(cxL[:].rearrange("p k t -> p (k t)"), CT[:, b, :],
                                cxH[:].rearrange("p k t -> p (k t)").bitcast(F32), ALU.subtract)\
                 .then_inc(sem("cxL"), 1)
                g.wait_ge(sem("x1"), after(b))
                g.wait_ge(sem("vec_in"), 48)
                g.tensor_tensor(xb[0:S], XR[0:S, b, :], beta0B[0:S], ALU.add).then_inc(sem("xb"), 1)
                alone(g, ("mvA", b * 2 + 1))
                rsqrt(tk[0:S, 1:2], mv[0:S, 1:2], tk[0:S, 0:1], LN_EPS, "rsA", b * 2 + 1).then_inc(sem("rsA"), 1)
                alone(g, ("mvA", b * 2 + 2))
                rsqrt(tk[0:S, 3:4], mv[0:S, 1:2], tk[0:S, 2:3], LN_EPS, "rsA", b * 2 + 2).then_inc(sem("rsF"), 1)
                alone(g, ("rsF", b + 1))
                g.tensor_scalar(tk[0:S, 4:5], mv[0:S, 1:2], tk[0:S, 3:4], tk[0:S, 3:4], ALU.mult, ALU.mult)\
                 .then_inc(sem("msF"), 1)
                alone(g, ("msF", b + 1))
                rsqrt(tk[0:S, 6:7], tk[0:S, 4:5], tk[0:S, 5:6], RMS_EPS, "rms", b + 1).then_inc(sem("rms"), 1)
                alone(g, ("rms", b + 1))
                g.tensor_tensor(tk[0:S, 7:8], tk[0:S, 3:4], tk[0:S, 6:7], ALU.mult).then_inc(sem("uscale"), 1)
                g.wait_ge(sem("v_copied"), after((b + 1) * NT))
                g.tensor_copy(vs(b)[0:TC, :].rearrange("p (c h w) -> p c h w", c=NT, h=HEADS)[:, :, :, HD],
                              ones[0:TC, 0:NT * HEADS].rearrange("p (c h) -> p c h", c=NT))\
                 .then_inc(sem("v_ones"), 1)
                alone(g, ("h_round", b + 1), ("t2", after(b * 2)))
                g.tensor_scalar(hq[0:S, FF // 2:], h[0:S, FF // 2:], -MAGIC, 1.0, ALU.add, ALU.mult)\
                 .then_inc(sem("hq1"), 1)
            g.wait_ge(sem("hq1"), after(B))
            g.wait_ge(sem("v_ones"), B)
            g.tensor_copy(cols[:, 20:21], cols[:, 0:1]).then_inc(sem("a_done_pool"), 1)
            for e in ("dve", "act", "pe"):
                g.wait_ge(sem(f"a_done_{e}"), 1)
            for i in range(2):
                g.memset(pE[0:S, i, T:NT * TC + 1], 0.0).then_inc(sem("p_pad"), 1)

            def low_keys(b, j, u):
                g.wait_ge(sem("kH"), b + 1)
                scores_done(g, b - 1)
                g.tensor_tensor(KL[j][:].rearrange("p k t -> p (k t)"), CT[:, b, :],
                                KH[j][:].rearrange("p k t -> p (k t)").bitcast(F32), ALU.subtract)\
                 .then_inc(sem("kL"), 1)

            def rstd_b(b):
                alone(g, ("mvB", b + 1))
                rsqrt(tb[0:S, 1:2], mvb[0:S, 1:2], tb[0:S, 0:1], LN_EPS, "rsB_t", b + 1).then_inc(sem("rsB"), 1)

            def with_bo(b):
                g.wait_ge(sem("x3"), after(b))
                g.tensor_tensor(xbo[0:S], XR[0:S, b, :], boB[0:S], ALU.add).then_inc(sem("xbo"), 1)

            def body(b, j, u, first, last):
                if not first:
                    with_bo(b - 1)
                if not last:
                    low_keys(b + 1, 1 - j, u + j)
                    rstd_b(b + 1)

            g.wait_ge(sem("bvo_in"), 48)
            low_keys(0, 0, 0)
            rstd_b(0)
            batches(g, body)
            with_bo(B - 1)
            g.wait_ge(sem("xbo"), B)
            g.tensor_copy(cols[:, 20:21], cols[:, 1:2]).then_inc(sem("b_done_pool"), 1)
            for e in ("dve", "act", "pe"):
                g.wait_ge(sem(f"b_done_{e}"), 1)
            g.iota(iot[0:S], [[1, E]], base=0, channel_multiplier=0, allow_small_or_imprecise_dtypes=True)\
             .then_inc(sem("c_setup"), 1)
            for j in range(2):
                g.memset(hs[0:S, j, EH:EH + 1], 1.0).then_inc(sem("c_setup"), 1)
                g.memset(hs[0:S, j, EH + 1:EHP], 0.0).then_inc(sem("c_setup"), 1)
            with g.Fori(0, B) as b:
                alone(g, ("mvC", b + 1))
                rsqrt(tc_[0:S, 1:2], mvc[0:S, 1:2], tc_[0:S, 0:1], LN_EPS, "rsC", b + 1).then_inc(sem("rsC"), 1)


        @block.scalar
        def _(act):
            act.wait_ge(sem("decay_in"), 16)
            act.activation(cols[:, C_EXP:C_EXP + 1], cols[:, C_DEC:C_DEC + 1], ACT.Exp, scale=-1.0)\
               .then_inc(sem("decay_exp"), 1)
            act.wait_ge(sem("stage_in0"), 16)
            act.copy(wkH[:].rearrange("p k n -> p (k n)"), stage(0)).then_inc(sem("wkvH"), 1)
            act.wait_ge(sem("stage_in1"), 16)
            act.copy(wvH[:].rearrange("p k n -> p (k n)"), stage(1)).then_inc(sem("wkvH"), 1)
            act.wait_ge(sem("consts"), 1)
            for w in range(2):
                for c in range(NW):
                    slot = (2 + c) % NW
                    act.wait_ge(sem(f"stage_in{slot}"), 16 * (w + 1 + (slot < 2)))
                    if w + c:
                        act.wait_ge(sem("abs_sum"), NW * w + c)
                    act.activation(hq[:, 0:WP], stage(slot), ACT.Abs, accum_out=asum[:, w, c:c + 1])\
                       .then_inc(sem("abs_sum"), 1)
                act.wait_ge(sem("w_scale"), w + 1)
                for c in range(NW):
                    act.activation(stage(2 + c), stage(2 + c), ACT.Identity, bias=cols[:, C_MAGIC:C_MAGIC + 1],
                                   scale=wsc[:, w, 2:3]).then_inc(sem("w_round"), 1)
            for b in range(B):
                act.wait_ge(sem(f"ctx_in{b}"), 16)

            with act.Fori(0, B) as b:
                alone(act, ("v_mm", after(b * NT)))
                act.copy(cxH[:].rearrange("p k t -> p (k t)"), CT[:, b, :]).then_inc(sem("cxH"), 1)
                for m in range(KC):
                    alone(act, ("k_mm", b * KC + m + 1))
                    act.activation(CT[:, b, m * TP:(m + 1) * TP], ps[:, m % 2, 0:TP], ACT.Identity,
                                   bias=biases[:, 1, m:m + 1]).then_inc(sem("k_copied"), 1)
                act.wait_ge(sem("t1"), after(b + 1))
                act.wait_ge(sem("g1"), after(b * 4))
                act.copy(xqT[:].rearrange("p k s -> p (k s)"), ps[:, 6, 0:KC * S // 2].bitcast(BF16))\
                   .then_inc(sem("xqT"), 1)
                act.wait_ge(sem("dq1"), b + 1)
                act.wait_ge(sem("hq0"), after(b))
                act.wait_ge(sem("hq1"), after(b))
                for m in range(4):
                    act.wait_ge(sem("g1"), after(b * 4 + m + 1))
                    act.activation(h[0:S, m * 512:(m + 1) * 512], ps[0:S, 2 + m, :], ACT.Gelu,
                                   scale=tk[0:S, 12:13]).then_inc(sem("gelu"), 1)
                act.wait_ge(sem("t2"), after(b * 2 + 1))
                act.wait_ge(sem("g2"), after(b))
                act.copy(hqT[:, 0:8, :].rearrange("p k s -> p (k s)"), ps[:, 6, 0:4 * S].bitcast(BF16))\
                   .then_inc(sem("hqT0"), 1)
            act.wait_ge(sem("hqT0"), after(B))
            act.copy(cols[:, 21:22], cols[:, 0:1]).then_inc(sem("a_done_act"), 1)
            for e in ("dve", "pe", "pool"):
                act.wait_ge(sem(f"a_done_{e}"), 1)
            act.wait_ge(sem("wscale"), 2)
            for w in range(2):
                for j in range(KC):
                    act.activation(wst[:, w, j, :], wst[:, w, j, :], ACT.Identity, bias=cols[:, C_MAGIC:C_MAGIC + 1],
                                   scale=wsm[:, 2, w, j:j + 1]).then_inc(sem("wq_round"), 1)
            for i in range(0, 8, 2):
                act.wait_ge(sem("wq_t"), i + 1)
                act.copy(wqT[:, i // KC, i % KC, :], ps[:, i, 0:D // 2].bitcast(BF16)).then_inc(sem("wqT_act"), 1)

            def high_keys(b, j, u):
                scores_done(act, b - 1)
                act.copy(KH[j][:].rearrange("p k t -> p (k t)"), CT[:, b, :]).then_inc(sem("kH"), 1)

            def turned_x(b):
                act.wait_ge(sem("xq2_t"), b + 1)
                act.copy(xq2T[:].rearrange("p k s -> p (k s)"), ps[:, 7, 0:KC * S // 2].bitcast(BF16))\
                   .then_inc(sem("xq2T"), 1)

            def turned_o(b):
                act.wait_ge(sem("oq_t"), b + 1)
                act.copy(oQT[:].rearrange("p k s -> p (k s)"), ps[:, 7, 0:KC * S // 2].bitcast(BF16))\
                   .then_inc(sem("oQT"), 1)

            def body(b, j, u, first, last):
                for h_ in range(HEADS + 1):
                    if h_ < HEADS:
                        r, n = h_ % 2, b * 8 + h_ // 2
                        act.wait_ge(sem(f"masked{r}"), after(n + 1))
                        act.wait_ge(sem(f"p_turned{r}"), after(n))
                        act.activation(pE[0:S, r, 0:T], sN[0:S, r, 0:T], ACT.Exp, scale=-1.0,
                                       bias=nmx[0:S, h_:h_ + 1]).then_inc(sem(f"exp{r}"), 1)
                    if h_ and copies_on_act(h_ - 1):
                        copy_p(act, act.copy, b, h_ - 1)
                    if h_ == 3 and not last:
                        high_keys(b + 1, 1 - j, u + j)
                    if h_ == 7 and not first:
                        turned_o(b - 1)
                    if h_ == 13 and not last:
                        turned_x(b + 1)

            act.wait_ge(sem("wq_t"), 8)
            high_keys(0, 0, 0)
            turned_x(0)
            batches(act, body)
            turned_o(B - 1)
            act.wait_ge(sem("oQT"), after(B))
            act.copy(cols[:, 21:22], cols[:, 1:2]).then_inc(sem("b_done_act"), 1)
            for e in ("dve", "pe", "pool"):
                act.wait_ge(sem(f"b_done_{e}"), 1)
            with act.Fori(0, B) as b:
                act.wait_ge(sem("z_t"), b + 1)
                act.copy(zT[:, 0].rearrange("p k s -> p (k s)"), ps[:, 0, 0:KC * S]).then_inc(sem("zT"), 1)
                act.wait_ge(sem("gap"), b + 1)
                act.activation(tc_[0:S, 3:4], tc_[0:S, 2:3], ACT.Exp).then_inc(sem("gap_exp"), 1)
                with act.Fori(0, E) as e:
                    act.wait_ge(sem("hb"), b * E + e + 1)
                    act.wait_ge(sem("h_t"), after(b * E + e))
                    act.activation(hs[0:S, 0, 0:EH], hb[0:S], ACT.Silu).then_inc(sem("hs"), 1)
                    act.wait_ge(sem("h_t"), after(b * E + e + 1))
                    act.copy(hTe[0:EC].rearrange("p c s -> p (c s)"), ps[0:EC, 3, 0:3 * S]).then_inc(sem("hTe"), 1)

        @block.tensor
        def _(pe):
            for name in credited:
                pe.sem_inc(sem(name), 1)
            pe.wait_ge(sem("consts"), 1)
            pe.wait_ge(sem("kvw"), KC * B)
            pe.wait_ge(sem("win_in"), 32)
            for m in range(KC):
                for k in range(KC):
                    mm = pe.matmul(ps[:, 7, m * B:(m + 1) * B], w1s[:, k * D + m * P:k * D + (m + 1) * P], kvw[:, k, :],
                                   start=(k == 0), stop=(k == KC - 1))
            mm.then_inc(sem("xm_mm"), 1)
            pe.wait_ge(sem("xm"), 1)
            for k in range(KC):
                mm = pe.matmul(ps[0:B, 6, :], xm[:, k, :], w2s[:, k * D:(k + 1) * D], start=(k == 0), stop=(k == KC - 1))
            mm.then_inc(sem("summ_mm"), 1)
            for w in range(2):
                pe.wait_ge(sem("abs_sum"), NW * (w + 1))
                pe.matmul(ps[:, 5, 0:NW], ones[:, :], asum[:, w, :], start=True, stop=True).then_inc(sem("w_total"), 1)
            pe.wait_ge(sem("w_scale"), 2)
            pe.wait_ge(sem("summ_ready"), 1)
            pe.wait_ge(sem("wkvL"), 2)
            with pe.Fori(0, B) as b:
                pe.wait_ge(sem("cxL"), b + 1)
                for m in range(KC):
                    if m < 2:
                        pe.wait_ge(sem("v_copied"), after(b * NT))
                    else:
                        pe.wait_ge(sem("k_copied"), after(b * KC + m - 1))
                    n = 0
                    for wt, cx in ((wkH, cxH), (wkH, cxL), (wkL, cxH)):
                        for k in range(KC):
                            mm = pe.matmul(ps[:, m % 2, 0:TP], wt[:, k, m * P:(m + 1) * P], cx[:, k, :],
                                           start=(n == 0), stop=(n == 3 * KC - 1))
                            n += 1
                    mm.then_inc(sem("k_mm"), 1)
                pe.wait_ge(sem("xqb"), b + 1)
                pe.wait_ge(sem("hqT0"), after(b))
                for k in range(KC):
                    mm = pe.transpose(ps[:, 6, k * S // 2:(k + 1) * S // 2].bitcast(BF16), xqb[0:S, k * P:(k + 1) * P],
                                      identb[0:S, 0:S])
                mm.then_inc(sem("t1"), 1)
                alone(pe, ("xqT", b + 1), ("ternary", NW), ("gelu", after(b * 4)))
                for m in range(4):
                    for k in range(KC):
                        mm = pe.matmul(ps[0:S, 2 + m, :], xqT[:, k, :], w1q[:, k * FF + m * 512:k * FF + (m + 1) * 512],
                                       start=(k == 0), stop=(k == KC - 1))
                    mm.then_inc(sem("g1"), 1)
                for c in range(NT):
                    if c < 2:
                        pe.wait_ge(sem("k_copied"), after(b * KC + c + 3))
                    else:
                        pe.wait_ge(sem("v_copied"), after(b * NT + 1))
                    n = 0
                    for cx, wt in ((cxH, wvH), (cxH, wvL), (cxL, wvH)):
                        for k in range(KC):
                            mm = pe.matmul(ps[0:TC, c % 2, :], cx[:, k, c * TC:(c + 1) * TC], wt[:, k, :],
                                           start=(n == 0), stop=(n == 3 * KC - 1))
                            n += 1
                    mm.then_inc(sem("v_mm"), 1)
                pe.wait_ge(sem("hq0"), after(b + 1))
                pe.wait_ge(sem("hq1"), after(b + 1))
                pe.wait_ge(sem("x2"), after(b))
                for half in range(2):
                    for k in range(8):
                        mm = pe.transpose(ps[:, 6 + half, k * S // 2:(k + 1) * S // 2].bitcast(BF16),
                                          hq[0:S, (half * 8 + k) * P:(half * 8 + k + 1) * P], identb[0:S, 0:S])
                    mm.then_inc(sem("t2"), 1)
                alone(pe, ("hqT0", after(b + 1)), ("hqT1", b + 1), ("ternary", 2 * NW))
                for k in range(FC):
                    mm = pe.matmul(ps[0:S, 7, :], hqT[:, k, :], w2q[:, k * D:(k + 1) * D],
                                   start=(k == 0), stop=(k == FC - 1))
                mm.then_inc(sem("g2"), 1)
            pe.wait_ge(sem("x2"), after(B))
            pe.matmul(ps[:, 0, 0:1], ones[:, :], ones[:, 0:1], start=True, stop=True).then_inc(sem("a_done_pe"), 1)
            for e in ("dve", "act", "pool"):
                pe.wait_ge(sem(f"a_done_{e}"), 1)
            pe.wait_ge(sem("a_done_pe"), 1)
            for i in range(8):
                w, k = divmod(i, KC)
                pe.wait_ge(sem("wq_b"), (w + 1) * KC)
                for j in range(KC):
                    mm = pe.transpose(ps[:, i, j * P // 2:(j + 1) * P // 2].bitcast(BF16),
                                      wstb[:, w, j, k * P:(k + 1) * P], identb[:, :])
                mm.then_inc(sem("wq_t"), 1)
            pe.wait_ge(sem("wqT_act"), 4)
            pe.wait_ge(sem("wqT_dve"), 4)

            def turn_rows(src, name, b):
                for k in range(KC):
                    mm = pe.transpose(ps[:, 7, k * S // 2:(k + 1) * S // 2].bitcast(BF16), src[0:S, k * P:(k + 1) * P],
                                      identb[0:S, 0:S])
                mm.then_inc(sem(name), 1)

            def queries(b):
                pe.wait_ge(sem("xq2T"), b + 1)
                pe.transpose(ps[:, 6, KC * S:(KC + 1) * S], tb[0:S, 4:5].to_broadcast([S, P]), ident[0:S, 0:S])
                for m in range(KC):
                    for k in range(KC):
                        mm = pe.matmul(ps[:, 6, m * S:(m + 1) * S], wqT[:, 0, k, m * P:(m + 1) * P], xq2T[:, k, :],
                                       start=(k == 0), stop=(k == KC - 1))
                mm.then_inc(sem("q_mm"), 1)

            def out_rows(b):
                pe.wait_ge(sem("oQT"), after(b + 1))
                for k in range(KC):
                    mm = pe.matmul(ps[0:S, 6, :], oQT[:, k, :], wqT[:, 1, k, :], start=(k == 0), stop=(k == KC - 1))
                mm.then_inc(sem("wo_mm"), 1)

            def body(b, j, u, first, last):
                pe.wait_ge(sem("q_ready"), b + 1)
                pe.wait_ge(sem("kL"), b + 1)
                for h_ in range(HEADS + 2):
                    if h_ < HEADS:
                        r, n, m, at = h_ % 2, b * 8 + h_ // 2, h_ // HPC, h_ % HPC * HD
                        pe.wait_ge(sem(f"masked{r}"), after(n))
                        for i, (q, kk) in enumerate(((qH[j], KH[j]), (qH[j], KL[j]), (qL[j], KH[j]))):
                            mm = pe.matmul(ps[0:S, r, 0:TP], q[at:at + HD, m, :], kk[at:at + HD, m, :],
                                           start=(i == 0), stop=(i == 2))
                        mm.then_inc(sem(f"score{r}"), 1)
                    if 1 <= h_ <= HEADS:
                        r, n = (h_ - 1) % 2, b * 8 + (h_ - 1) // 2
                        pe.wait_ge(sem(f"exp{r}"), after(n + 1))
                        pe.wait_ge(sem(f"p_copied{r}"), after(n))
                        for c in range(NT):
                            mm = pe.transpose(ps[0:TC, 2 + r, c * S:(c + 1) * S], pE[0:S, r, c * TC:(c + 1) * TC],
                                              ident[0:S, 0:S])
                        mm.then_inc(sem(f"p_turned{r}"), 1)
                    if h_ >= 2:
                        hh = h_ - 2
                        r, n = hh % 2, b * 8 + hh // 2
                        pe.wait_ge(sem(f"p_copied{r}"), after(n + 1))
                        if hh == 0:
                            pe.wait_ge(sem("o_norm"), after(b))
                        for c in range(NT):
                            at = c * VW + hh * (HD + 1)
                            mm = pe.matmul(ps[0:S, 4 + hh // 8, hh % 8 * (HD + 1):(hh % 8 + 1) * (HD + 1)],
                                           pT[0:TC, r, c, :], vs(b)[0:TC, at:at + HD + 1],
                                           start=(c == 0), stop=(c == NT - 1))
                        mm.then_inc(sem(f"pv{r}"), 1)
                    if h_ == 6 and not first:
                        pe.wait_ge(sem("oQb"), after(b))
                        turn_rows(oQb, "oq_t", b - 1)
                    if h_ == 8 and not first:
                        out_rows(b - 1)
                    if h_ == 12 and not last:
                        pe.wait_ge(sem("xq2b"), b + 2)
                        pe.wait_ge(sem("oQT"), after(b))
                        turn_rows(xq2b, "xq2_t", b + 1)
                    if h_ == 14 and not last:
                        pe.wait_ge(sem("x3"), after(b))
                        queries(b + 1)

            pe.wait_ge(sem("xq2b"), 1)
            turn_rows(xq2b, "xq2_t", 0)
            queries(0)
            batches(pe, body)
            pe.wait_ge(sem("oQb"), after(B))
            turn_rows(oQb, "oq_t", B - 1)
            out_rows(B - 1)
            pe.wait_ge(sem("x3"), after(B))
            pe.matmul(ps[:, 0, 0:1], ones[:, :], ones[:, 0:1], start=True, stop=True).then_inc(sem("b_done_pe"), 1)
            for e in ("dve", "act", "pool"):
                pe.wait_ge(sem(f"b_done_{e}"), 1)
            pe.wait_ge(sem("b_done_pe"), 1)
            pe.wait_ge(sem("ew1_in"), 16 * E)
            pe.wait_ge(sem("ew2_in"), 16 * E)
            pe.wait_ge(sem("c_in"), 64)
            with pe.Fori(0, B) as b:
                pe.wait_ge(sem("z"), b + 1)
                for k in range(KC):
                    mm = pe.transpose(ps[:, 0, k * S:(k + 1) * S], z[0:S, 0, k * P:(k + 1) * P], ident[0:S, 0:S])
                mm.then_inc(sem("z_t"), 1)
                pe.wait_ge(sem("zT"), b + 1)
                for k in range(KC):
                    mm = pe.matmul(ps[0:S, 1, 0:E], zT[:, 0, k, :], gwT[:, k, :], start=(k == 0), stop=(k == KC - 1))
                mm.then_inc(sem("logit"), 1)
                with pe.Fori(0, E) as e:
                    for k in range(KC):
                        mm = pe.matmul(ps[0:S, 2, 0:EH], zT[:, 0, k, :], CT[:, e, k * EH:(k + 1) * EH],
                                       start=(k == 0), stop=(k == KC - 1))
                    mm.then_inc(sem("h_mm"), 1)
                    pe.wait_ge(sem("hs"), after(b * E + e + 1))
                    for c in range(3):
                        mm = pe.transpose(ps[0:EC, 3, c * S:(c + 1) * S], hs[0:S, 0, c * EC:(c + 1) * EC],
                                          ident[0:S, 0:S])
                    mm.then_inc(sem("h_t"), 1)
                    pe.wait_ge(sem("hTe"), b * E + e + 1)
                    pe.wait_ge(sem("moe_done"), after(b * E + e))
                    for c in range(3):
                        mm = pe.matmul(ps[0:S, 4, :], hTe[0:EC, c, :], vs(e)[0:EC, c * D:(c + 1) * D],
                                       start=(c == 0), stop=(c == 2))
                    mm.then_inc(sem("y_mm"), 1)

        @block.vector
        def _(dve):
            ch = chain(dve, "dve_setup", 0)
            ch.turn(0)
            ch(dve.memset(krow, 1.0))
            dve.wait_ge(sem("decay_exp"), 1)
            ch(dve.tensor_scalar(cols[:, C_K:C_K + 1], cols[:, C_EXP:C_EXP + 1], 1.0, None, ALU.add))
            ch(dve.reciprocal(cols[:, C_K + 2:C_K + 3], cols[:, C_K:C_K + 1]))
            ch(dve.tensor_scalar(y[:, 0:T], krow[:, 0:T], cols[:, C_K + 2:C_K + 3], None, ALU.mult))
            ch(dve.tensor_tensor_scan(out=xq[:, T - 1::-1], data0=y[:, 0:T], data1=krow[:, 0:T],
                                      initial=0.0, op0=ALU.mult, op1=ALU.add))
            ch(dve.tensor_scalar(cw[:, 0:T], xq[:, 0:T], 1.0 / T, None, ALU.mult))
            ch(dve.tensor_reduce(cols[:, C_SUM:C_SUM + 1], cw[:, 0:T], AX.X, ALU.add))
            dve.wait_ge(sem("biases_in"), 32)
            ch(dve.tensor_scalar(biases[:, 2, :], biases[:, 0, :], cols[:, C_SUM:C_SUM + 1], None, ALU.mult))
            for i, (hi, lo) in enumerate(((wkH, wkL), (wvH, wvL))):
                dve.wait_ge(sem("wkvH"), i + 1)
                dve.tensor_tensor(lo[:].rearrange("p k n -> p (k n)"), stage(i),
                                  hi[:].rearrange("p k n -> p (k n)").bitcast(F32), ALU.subtract)\
                   .then_inc(sem("wkvL"), 1)
            for b in range(B):
                dve.wait_ge(sem(f"ctx_in{b}"), 16)
                for k in range(KC):
                    i = b * KC + k
                    if i >= 3:
                        dve.wait_ge(sem("kvw"), i - 2)
                    dve.tensor_tensor_reduce(out=junk[i % 3], in0=CT[:, b, k * TP:k * TP + T], in1=cw[:, 0:T],
                                             scale=1.0, scalar=0.0, op0=ALU.mult, op1=ALU.add,
                                             accum_out=kvw[:, k, b:b + 1]).then_inc(sem("kvw"), 1)
            dve.wait_ge(sem("xm_mm"), 1)
            dve.tensor_tensor(xm[:], ps[:, 7, 0:KC * B].rearrange("p (k b) -> p k b", k=KC),
                              biases[:, 2, :].unsqueeze(2).to_broadcast([P, KC, B]), ALU.add).then_inc(sem("xm"), 1)
            dve.wait_ge(sem("summ_mm"), 1)
            dve.wait_ge(sem("bout_in"), 16)
            dve.tensor_tensor(summ, ps[0:B, 6, :], boutB, ALU.add).then_inc(sem("summ_ready"), 1)

            def w_scale(w):
                dve.wait_ge(sem("w_total"), w + 1)
                ch(dve.tensor_reduce(wsc[:, w, 0:1], ps[:, 5, 0:NW], AX.X, ALU.add))
                ch(dve.tensor_scalar(wsc[:, w, 1:2], wsc[:, w, 0:1], 1.0 / (D * FF), 1e-5, ALU.mult, ALU.max))
                dve.reciprocal(wsc[:, w, 2:3], wsc[:, w, 1:2]).then_inc(sem("w_scale"), 1)

            def ternary(w):
                dst = (w1q, w2q)[w]
                for c in range(NW):
                    dve.wait_ge(sem("w_round"), NW * w + c + 1)
                    ch(dve.tensor_scalar(stage(2 + c), stage(2 + c), MAGIC - 1.0, MAGIC + 1.0, ALU.max, ALU.min))
                    dve.tensor_scalar(dst[:, c * WP:(c + 1) * WP], stage(2 + c), MAGIC, None, ALU.subtract,
                                      saturate=False).then_inc(sem("ternary"), 1)

            w_scale(0)
            ternary(0)
            w_scale(1)
            ternary(1)
            dve.wait_ge(sem("w_scale"), 2)
            dve.wait_ge(sem("x_in"), 16)
            for b in range(B):
                ch(dve.bn_stats(st0[0:S, b, :], XR[0:S, b, :]))
                dve.bn_aggr(mv0[0:S, b, :], st0[0:S, b, :]).then_inc(sem("mv0"), 1)
            dve.wait_ge(sem("rs0"), 1)
            dve.wait_ge(sem("vec_in"), 48)

            ch = chain(dve, "dve_a", 16)
            with dve.Fori(0, B) as b:
                ch.turn(b)
                xr = XR[0:S, b, :]
                dve.wait_ge(sem("summ_in"), 16 * b + 16)
                dve.scalar_tensor_tensor(out=y[0:S], in0=xr, scalar=rs0[0:S, bass.ds(b, 1)], in1=summB[0:S],
                                         op0=ALU.mult, op1=ALU.add).then_inc(sem("summ_used"), 1)
                dve.wait_ge(sem("summ_used"), after(b + 1))
                ch(dve.bn_stats(st6[0:S], y[0:S]), True)
                dve.bn_aggr(mv[0:S], st6[0:S]).then_inc(sem("mvA"), 1)
                dve.wait_ge(sem("mvA"), b * 2 + 1)
                ch(dve.scalar_tensor_tensor(out=xq[0:S], in0=y[0:S], scalar=mv[0:S, 0:1], in1=gamma0B[0:S],
                                            op0=ALU.subtract, op1=ALU.mult))
                dve.wait_ge(sem("rsA"), b + 1)
                dve.wait_ge(sem("xb"), b + 1)
                dve.scalar_tensor_tensor(out=xr, in0=xq[0:S], scalar=tk[0:S, 1:2], in1=xb[0:S],
                                         op0=ALU.mult, op1=ALU.add).then_inc(sem("x1"), 1)
                alone(dve, ("x1", after(b + 1)))
                ch(dve.bn_stats(st6[0:S], xr), True)
                dve.bn_aggr(mv[0:S], st6[0:S]).then_inc(sem("mvA"), 1)
                dve.wait_ge(sem("mvA"), b * 2 + 2)
                ch(dve.scalar_tensor_tensor(out=y[0:S], in0=xr, scalar=mv[0:S, 0:1], in1=gammafB[0:S],
                                            op0=ALU.subtract, op1=ALU.mult))
                ch(dve.tensor_reduce(tk[0:S, 8:9], y[0:S], AX.X, ALU.max, apply_absolute_value=True))
                dve.wait_ge(sem("uscale"), b + 1)
                ch(dve.tensor_scalar(tk[0:S, 9:10], tk[0:S, 8:9], tk[0:S, 7:8], 1e-5, ALU.mult, ALU.max))
                ch(dve.reciprocal(tk[0:S, 10:11], tk[0:S, 9:10]))
                ch(dve.tensor_scalar(tk[0:S, 11:12], tk[0:S, 10:11], tk[0:S, 7:8], QMAX, ALU.mult, ALU.mult))
                ch(dve.tensor_scalar(xq[0:S], y[0:S], tk[0:S, 11:12], MAGIC, ALU.mult, ALU.add))
                dve.wait_ge(sem("t1"), after(b))
                dve.tensor_scalar(xqb[0:S], xq[0:S], MAGIC, None, ALU.subtract).then_inc(sem("xqb"), 1)
                dve.wait_ge(sem("gelu"), after(b * 4))
                dve.tensor_scalar(tk[0:S, 12:13], tk[0:S, 9:10], wsc[0:S, 0, 1:2], 1.0 / QMAX, ALU.mult, ALU.mult)\
                   .then_inc(sem("dq1"), 1)
                for m in range(4):
                    dve.wait_ge(sem("gelu"), after(b * 4 + m + 1))
                    ins = dve.tensor_reduce(tk[0:S, 14 + m:15 + m], h[0:S, m * 512:(m + 1) * 512], AX.X, ALU.max,
                                            apply_absolute_value=True)
                ch(ins)
                ch(dve.tensor_reduce(tk[0:S, 18:19], tk[0:S, 14:18], AX.X, ALU.max))
                ch(dve.tensor_scalar(tk[0:S, 19:20], tk[0:S, 18:19], 1e-5, None, ALU.max))
                ch(dve.reciprocal(tk[0:S, 20:21], tk[0:S, 19:20]))
                ch(dve.tensor_scalar(tk[0:S, 21:22], tk[0:S, 20:21], QMAX, None, ALU.mult))
                dve.tensor_scalar(h[0:S, FF // 2:], h[0:S, FF // 2:], tk[0:S, 21:22], MAGIC, ALU.mult, ALU.add)\
                   .then_inc(sem("h_round"), 1)
                ch(dve.tensor_scalar(h[0:S, 0:FF // 2], h[0:S, 0:FF // 2], tk[0:S, 21:22], MAGIC, ALU.mult, ALU.add))
                dve.wait_ge(sem("t2"), after(b * 2))
                dve.tensor_scalar(hq[0:S, 0:FF // 2], h[0:S, 0:FF // 2], MAGIC, None, ALU.subtract)\
                   .then_inc(sem("hq0"), 1)
                for c in range(NT):
                    dve.wait_ge(sem("v_mm"), after(b * NT + c + 1))
                    dve.tensor_copy(vs(b)[0:TC, c * VW:(c + 1) * VW].rearrange("p (h w) -> p h w", h=HEADS)[:, :, 0:HD],
                                    ps[0:TC, c % 2, :].rearrange("p (h w) -> p h w", h=HEADS))\
                       .then_inc(sem("v_copied"), 1)
                dve.wait_ge(sem("t2"), after(b * 2 + 2))
                dve.tensor_copy(hqT[:, 8:16, :].rearrange("p k s -> p (k s)"), ps[:, 7, 0:4 * S].bitcast(BF16))\
                   .then_inc(sem("hqT1"), 1)
                ch(dve.tensor_scalar(tk[0:S, 22:23], tk[0:S, 19:20], wsc[0:S, 1, 1:2], 1.0 / QMAX, ALU.mult, ALU.mult))
                dve.wait_ge(sem("g2"), after(b + 1))
                dve.scalar_tensor_tensor(out=xr, in0=ps[0:S, 7, :], scalar=tk[0:S, 22:23], in1=xr,
                                         op0=ALU.mult, op1=ALU.add).then_inc(sem("x2"), 1)
                ch.end()
            dve.wait_ge(sem("x2"), after(B))
            dve.tensor_copy(cols[:, 22:23], cols[:, 0:1]).then_inc(sem("a_done_dve"), 1)

            for e in ("act", "pe", "pool"):
                dve.wait_ge(sem(f"a_done_{e}"), 1)
            ch = chain(dve, "dve_b_setup", 0)
            ch.turn(0)
            dve.wait_ge(sem("wqo_in"), 32)
            for w in range(2):
                for j in range(KC):
                    ins = dve.tensor_reduce(wsm[:, 0, w, j:j + 1], wst[:, w, j, :], AX.X, ALU.max,
                                            apply_absolute_value=True)
            ch(ins)
            dve.tensor_scalar(wsm[:, 1], wsm[:, 0], 1.0 / QMAX, 1e-8, ALU.mult, ALU.max).then_inc(sem("wscale"), 1)
            dve.wait_ge(sem("wscale"), 1)
            dve.reciprocal(wsm[:, 2], wsm[:, 1]).then_inc(sem("wscale"), 1)
            dve.wait_ge(sem("bq_in"), 16)
            inv = float(HD) ** -0.5
            for m in range(KC):
                dve.tensor_scalar(swqB[:, m, :], ones[:, 0:S], wsm[:, 1, 0, m:m + 1], inv, ALU.mult, ALU.mult)
                ch(dve.tensor_scalar(bqB[:, m, :], ones[:, 0:S], bqS[:, m:m + 1], inv, ALU.mult, ALU.mult))
            for i in range(8):
                dve.wait_ge(sem("wq_round"), i + 1)
                dve.tensor_scalar(wstb[:, i // KC, i % KC, :], wst[:, i // KC, i % KC, :], MAGIC, None, ALU.subtract)\
                   .then_inc(sem("wq_b"), 1)
            for i in range(1, 8, 2):
                dve.wait_ge(sem("wq_t"), i + 1)
                dve.tensor_copy(wqT[:, i // KC, i % KC, :], ps[:, i, 0:D // 2].bitcast(BF16)).then_inc(sem("wqT_dve"), 1)
            dve.wait_ge(sem("bvo_in"), 48)

            chp, chf = chain(dve, "dve_prep", 9), chain(dve, "dve_finish", 6)

            def quant(ch, rows, am, scale, inv_, rounded):
                ch(dve.tensor_reduce(am, rows, AX.X, ALU.max, apply_absolute_value=True))
                ch(dve.tensor_scalar(scale, am, 1.0 / QMAX, 1e-8, ALU.mult, ALU.max))
                ch(dve.reciprocal(inv_, scale))
                ch(dve.tensor_scalar(rounded, rows, inv_, MAGIC, ALU.mult, ALU.add))

            def prep1(b):
                chp.turn(b)
                chp(dve.bn_stats(st6b[0:S], XR[0:S, b, :]), True)
                dve.bn_aggr(mvb[0:S], st6b[0:S]).then_inc(sem("mvB"), 1)

            def prep2(b):
                dve.wait_ge(sem("rsB"), b + 1)
                chp(dve.tensor_scalar(g2[0:S], XR[0:S, b, :], mvb[0:S, 0:1], tb[0:S, 1:2], ALU.subtract, ALU.mult))
                quant(chp, g2[0:S], tb[0:S, 3:4], tb[0:S, 4:5], tb[0:S, 5:6], xq2[0:S])
                dve.tensor_scalar(xq2b[0:S], xq2[0:S], MAGIC, None, ALU.subtract).then_inc(sem("xq2b"), 1)

            def prep3(b, j, u):
                dve.wait_ge(sem("q_mm"), b + 1)
                chp(dve.tensor_copy(sxB[:], ps[:, 6, KC * S:(KC + 1) * S]))
                chp(dve.tensor_tensor(t1[:], ps[:, 6, 0:KC * S].rearrange("p (k s) -> p k s", k=KC),
                                      sxB[:].unsqueeze(1).to_broadcast([P, KC, S]), ALU.mult))
                chp(dve.tensor_tensor(t2[:], t1[:], swqB[:], ALU.mult))
                dve.tensor_tensor(t3[:], t2[:], bqB[:], ALU.add).then_inc(sem("qf"), 1)
                dve.wait_ge(sem("qf"), b + 1)
                scores_done(dve, b - 1)
                dve.tensor_copy(qH[j][:], t3[:]).then_inc(sem("qH"), 1)
                dve.wait_ge(sem("qH"), b + 1)
                dve.tensor_tensor(qL[j][:], t3[:], qH[j][:].bitcast(F32), ALU.subtract).then_inc(sem("q_ready"), 1)
                chp.end()

            def finish1(b):
                chf.turn(b)
                for r in range(2):
                    dve.wait_ge(sem(f"pv{r}"), after((b + 1) * 8))
                o = ps[0:S, 4:6, 0:8 * (HD + 1)].rearrange("p g (h w) -> p g h w", h=8)
                chf(dve.reciprocal(rinv[0:S].rearrange("p (g h) -> p g h", g=2), o[:, :, :, HD]))
                dve.tensor_tensor(oN[0:S].rearrange("p (g h w) -> p g h w", g=2, h=8), o[:, :, :, 0:HD],
                                  rinv[0:S].rearrange("p (g h) -> p g h", g=2).unsqueeze(3)
                                  .to_broadcast([S, 2, 8, HD]), ALU.mult).then_inc(sem("o_norm"), 1)

            def finish2(b):
                dve.wait_ge(sem("o_norm"), after(b + 1))
                chf(dve.tensor_tensor(oQ[0:S], oN[0:S], bvB[0:S], ALU.add))
                quant(chf, oQ[0:S], tb[0:S, 6:7], tb[0:S, 7:8], tb[0:S, 8:9], oN[0:S])
                dve.tensor_scalar(oQb[0:S], oN[0:S], MAGIC, None, ALU.subtract).then_inc(sem("oQb"), 1)
                chf.end()

            def finish3(b):
                dve.wait_ge(sem("wo_mm"), b + 1)
                dve.scalar_tensor_tensor(out=y2[0:S], in0=ps[0:S, 6, :], scalar=tb[0:S, 7:8], in1=swoB[0:S],
                                         op0=ALU.mult, op1=ALU.mult).then_inc(sem("y2"), 1)
                dve.wait_ge(sem("y2"), b + 1)
                dve.wait_ge(sem("xbo"), b + 1)
                dve.tensor_tensor(XR[0:S, b, :], y2[0:S], xbo[0:S], ALU.add).then_inc(sem("x3"), 1)

            def body(b, j, u, first, last):
                dve.wait_ge(sem(f"mask_in{j}"), 16 * u + 16)
                for h_ in range(HEADS + 1):
                    if h_ < HEADS:
                        r, n = h_ % 2, b * 8 + h_ // 2
                        alone(dve, (f"score{r}", after(n + 1)), (f"exp{r}", after(n)))
                        dve.tensor_tensor_reduce(out=sN[0:S, r, 0:T], in0=ps[0:S, r, 0:T], in1=maskS[0:S, j, 0:T],
                                                 scale=-1.0, scalar=3.4e38, op0=ALU.add, op1=ALU.min,
                                                 accum_out=nmx[0:S, h_:h_ + 1]).then_inc(sem(f"masked{r}"), 1)
                    if h_ and not copies_on_act(h_ - 1):
                        copy_p(dve, dve.tensor_copy, b, h_ - 1)
                    if not first:
                        if h_ == 2:
                            finish1(b - 1)
                        if h_ == 4:
                            finish2(b - 1)
                        if h_ == 9:
                            finish3(b - 1)
                    if not last:
                        if h_ == 6:
                            prep1(b + 1)
                        if h_ == 8:
                            prep2(b + 1)
                        if h_ == 15:
                            prep3(b + 1, 1 - j, u + j)
                dve.tensor_copy(cols[:, 24:25], cols[:, 0:1]).then_inc(sem("mask_used"), 1)

            prep1(0)
            prep2(0)
            prep3(0, 0, 0)
            batches(dve, body)
            finish1(B - 1)
            finish2(B - 1)
            finish3(B - 1)
            dve.wait_ge(sem("x3"), after(B))
            dve.tensor_copy(cols[:, 22:23], cols[:, 1:2]).then_inc(sem("b_done_dve"), 1)

            for e in ("act", "pe", "pool"):
                dve.wait_ge(sem(f"b_done_{e}"), 1)
            dve.wait_ge(sem("c_in"), 64)
            dve.wait_ge(sem("c_setup"), 5)
            ch = chain(dve, "dve_c", 13)
            with dve.Fori(0, B) as b:
                ch.turn(b)
                xr = XR[0:S, b, :]
                ch(dve.bn_stats(st6c[0:S], xr), True)
                dve.bn_aggr(mvc[0:S], st6c[0:S]).then_inc(sem("mvC"), 1)
                dve.wait_ge(sem("rsC"), b + 1)
                dve.tensor_scalar(z[0:S, 0], xr, mvc[0:S, 0:1], tc_[0:S, 1:2], ALU.subtract, ALU.mult)\
                   .then_inc(sem("z"), 1)
                dve.wait_ge(sem("logit"), b + 1)
                ch(dve.tensor_tensor(sc[0:S], ps[0:S, 1, 0:E], gbB[0:S, 0], ALU.add))
                ch(dve.tensor_tensor(comb[0:S], sc[0:S], gbB[0:S, 1], ALU.add), True)
                ch(dve.max(top[0:S], comb[0:S]), True)
                ch(dve.max_index(idx[0:S], top[0:S], comb[0:S]))
                ch(dve.tensor_copy(idf[0:S], idx[0:S]))
                dve.tensor_tensor(tc_[0:S, 2:3], top[0:S, 1:2], top[0:S, 0:1], ALU.subtract).then_inc(sem("gap"), 1)
                dve.wait_ge(sem("gap_exp"), b + 1)
                ch(dve.tensor_scalar(tc_[0:S, 4:5], tc_[0:S, 3:4], 1.0, None, ALU.add))
                ch(dve.reciprocal(tc_[0:S, 5:6], tc_[0:S, 4:5]))
                ch(dve.tensor_tensor(tc_[0:S, 6:7], tc_[0:S, 3:4], tc_[0:S, 5:6], ALU.mult))
                ch(dve.tensor_scalar(comb2[0:S], iot[0:S], idf[0:S, 0:1], tc_[0:S, 5:6], ALU.is_equal, ALU.mult))
                ch(dve.tensor_scalar(sc[0:S], iot[0:S], idf[0:S, 1:2], tc_[0:S, 6:7], ALU.is_equal, ALU.mult))
                ch(dve.tensor_tensor(comb[0:S], comb2[0:S], sc[0:S], ALU.add))
                ch(dve.tensor_copy(cols[:, 25:26], cols[:, 0:1]), True)
                ch.end()
                with dve.Fori(0, E) as e:
                    dve.wait_ge(sem("h_mm"), b * E + e + 1)
                    dve.wait_ge(sem("hs"), after(b * E + e))
                    dve.tensor_tensor(hb[0:S], ps[0:S, 2, 0:EH], b1B[0:S, e, :], ALU.add).then_inc(sem("hb"), 1)
                    dve.wait_ge(sem("y_mm"), b * E + e + 1)
                    dve.scalar_tensor_tensor(out=xr, in0=ps[0:S, 4, :], scalar=comb[0:S, bass.ds(e, 1)], in1=xr,
                                             op0=ALU.mult, op1=ALU.add).then_inc(sem("moe_done"), 1)
                    alone(dve, ("moe_done", after(b * E + e + 1)))


def kernel(**inputs):
    import numpy as np
    import concourse.bacc as bacc
    from concourse.bass_utils import run_bass_kernel_spmd

    a = {k: np.asarray(v) for k, v in inputs.items()}

    def chunked(w):
        return w.reshape(-1, P, w.shape[-1]).transpose(1, 0, 2)

    def column(v):
        return v.reshape(-1, P).T

    def pieces(w):
        return w.reshape(P, NW, -1).transpose(1, 0, 2)

    ctx = np.concatenate([a["ctx_2048"], np.zeros((B, TP - T, D), np.float32)], 1)
    w2e = np.concatenate([a["L1_ffn_w2"].transpose(0, 2, 1), a["L1_ffn_b2"][:, None, :],
                          np.zeros((E, 1, D), np.float32)], 1)
    laid = [
        ("x", a["x"].transpose(1, 0, 2)),
        ("ctxT", ctx.transpose(0, 2, 1).reshape(B, KC, P, TP).transpose(0, 2, 1, 3).reshape(B, P, KC * TP)),
        ("mask", a["mask_BxSxS2_ff0"]),
        ("decay", a["L0_xattn_decay"].reshape(1)),
        ("win", chunked(a["L0_xattn_W_in"].T).reshape(P, -1)),
        ("b_in", column(a["L0_xattn_b_in"])),
        ("wout", chunked(a["L0_xattn_W_out"].T).reshape(P, -1)),
        ("b_out", a["L0_xattn_b_out"]),
        ("gamma0", a["L0_xattn_gamma"]),
        ("beta0", a["L0_xattn_beta"]),
        ("w1", pieces(chunked(a["L0_ffn_w1"].T).reshape(P, -1))),
        ("w2", pieces(chunked(a["L0_ffn_w2"].T).reshape(P, -1))),
        ("gammaf", a["L0_ffn_gamma"]),
        ("wq", chunked(a["L1_xattn_wq"])),
        ("bq", column(a["L1_xattn_bq"])),
        ("wk", chunked(a["L1_xattn_wk"].T).reshape(P, -1)),
        ("bk", column(a["L1_xattn_bk"])),
        ("wv", chunked(a["L1_xattn_wv"].T).reshape(P, -1)),
        ("bv", a["L1_xattn_bv"]),
        ("wo", chunked(a["L1_xattn_wo"])),
        ("bo", a["L1_xattn_bo"]),
        ("gate_w", chunked(a["L1_ffn_gate_w"].T)),
        ("gate_b", a["L1_ffn_gate_b"]),
        ("gate_bias", a["L1_ffn_bias"]),
        ("ew1", a["L1_ffn_w1"].transpose(0, 2, 1).reshape(E, KC, P, EH).transpose(0, 2, 1, 3).reshape(E, P, KC * EH)),
        ("eb1", a["L1_ffn_b1"]),
        ("ew2", w2e.reshape(E, 3, EC, D).transpose(0, 2, 1, 3).reshape(E, EC, 3 * D)),
    ]
    nc = bacc.Bacc("TRN2", target_bir_lowering=False, num_devices=1)
    arrays, args = {}, []
    for name, v in laid:
        arrays[f"in_{name}"] = np.ascontiguousarray(v)
        args.append(nc.dram_tensor(f"in_{name}", v.shape, F32, kind="ExternalInput").ap())
    args.append(nc.dram_tensor("out_0", (B, S, D), F32, kind="ExternalOutput").ap())
    block_kernel(nc, *args)
    r = run_bass_kernel_spmd(nc, [arrays], core_ids=[0])
    return r.results[0]["out_0"]
```

```python
from contextlib import ExitStack

import concourse.bass as bass
from concourse import mybir

ALU = mybir.AluOpType
ACT = mybir.ActivationFunctionType
AX = mybir.AxisListType
F32 = mybir.dt.float32
F32R = mybir.dt.float32r
BF16 = mybir.dt.bfloat16
FP8 = mybir.dt.float8e4
I32 = mybir.dt.int32

B, S, D = 8, 100, 512
T = 361
P = 128
KC = D // P
NT = 3
TC = -(-T // NT)
TP = 364
HEADS, HD = 16, 32
HPC = P // HD
VW = HEADS * (HD + 1)
FF = 2048
FC = FF // P
NW = 4
WP = D * FF // P // NW
E, EH = 8, 352
EC = 118
EHP = 3 * EC
TOPK = 2
NBLK = (B * S * TOPK + E * (P - 1)) // P
LN_EPS, RMS_EPS = 1e-5, 1e-6
MAGIC = 1.5 * 2.0 ** 23
QMAX = 127.0


def block_kernel(nc, x, ctxT, mask, decay, win, b_in, wout, b_out, gamma0, beta0, w1, w2, gammaf,
                 wq, bq, wk, bk, wv, bv, wo, bo, gate_w, gate_b, gate_bias, ew1, eb1, ew2, out):
    with ExitStack() as whole:
        def sb(stack, name, shape, dt=F32):
            return stack.enter_context(nc.sbuf_tensor(name, shape, dt))

        sems = {}

        def sem(name):
            if name not in sems:
                sems[name] = whole.enter_context(nc.semaphore(name))
            return sems[name]

        credited = ("g1", "g2", "gelu", "hq0", "hq1", "hqT0", "k_copied", "oQT", "oQb",
                    "o_norm", "summ_used", "t1", "t2", "v_copied", "v_mm", "x1", "x2", "x3", "y_out0", "y_out1",
                    *(f"{name}{r}" for name in ("exp", "masked", "p_copied", "p_turned", "pv", "score")
                      for r in range(2)))

        def after(count):
            return count + 1

        summ_dram = nc.dram_tensor("summary_rows", [B, D], F32, kind="Internal").ap()
        slots_in = nc.dram_tensor("slots_in", [NBLK * P, D], F32, kind="Internal").ap()
        slots_out = nc.dram_tensor("slots_out", [NBLK * P, D], F32, kind="Internal").ap()
        swo_dram = nc.dram_tensor("wo_scales", [D], F32, kind="Internal").ap()

        CT = sb(whole, "CT", [P, B, KC * TP])
        VS = sb(whole, "VS", [P, B * NT * VW])
        XR = sb(whole, "XR", [P, B, D])
        ident = sb(whole, "ident", [P, P])
        identb = sb(whole, "identb", [P, P], BF16)
        ones = sb(whole, "ones", [P, P])
        before = sb(whole, "before", [P, P])
        zeros = sb(whole, "zeros", [P, P])
        cols = sb(whole, "cols", [P, 48])
        ps = whole.enter_context(nc.psum_tensor("ps", [P, 8, 512], F32))

        def vs(b):
            return VS[:, bass.ds(b * (NT * VW), NT * VW)]

        a = ExitStack()
        wkH, wkL = sb(a, "wkH", [P, KC, D], F32R), sb(a, "wkL", [P, KC, D], F32R)
        wvH, wvL = sb(a, "wvH", [P, KC, D], F32R), sb(a, "wvL", [P, KC, D], F32R)
        cxH, cxL = sb(a, "cxH", [P, KC, TP], F32R), sb(a, "cxL", [P, KC, TP], F32R)
        w1s = sb(a, "w1s", [P, KC * D])
        w2s = sb(a, "w2s", [P, KC * D])
        w1q = w1s[:].bitcast(FP8)
        w2q = w2s[:].bitcast(FP8)
        h = sb(a, "h", [P, FF])
        hq = sb(a, "hq", [P, FF], BF16)
        hqT = sb(a, "hqT", [P, FC, S], BF16)
        xq, y, xb = sb(a, "xq", [P, D]), sb(a, "y", [P, D]), sb(a, "xb", [P, D])
        xqb = sb(a, "xqb", [P, D], BF16)
        xqT = sb(a, "xqT", [P, KC, S], BF16)
        summB = sb(a, "summB", [P, D])
        gamma0B, beta0B, gammafB = sb(a, "gamma0B", [P, D]), sb(a, "beta0B", [P, D]), sb(a, "gammafB", [P, D])
        kvw, xm = sb(a, "kvw", [P, KC, B]), sb(a, "xm", [P, KC, B])
        biases = sb(a, "biases", [P, 3, KC])
        st6 = sb(a, "st6", [P, 6])
        mv = sb(a, "mv", [P, 2])
        mv0 = sb(a, "mv0", [P, B, 2])
        st0 = sb(a, "st0", [P, B, 6])
        rs0 = sb(a, "rs0", [P, B])
        tk = sb(a, "tk", [P, 24])
        asum = sb(a, "asum", [P, 2, NW])
        wsc = sb(a, "wsc", [P, 2, 4])
        cw, krow = h[:, 0:TP], h[:, TP:2 * TP]
        junk = [h[:, (2 + i) * TP:(2 + i) * TP + T] for i in range(3)]
        summ, boutB = xq[0:B, :], y[0:B, :]
        a.close()

        def stage(i):
            at = 2 * NT * VW + (i % NW) * WP
            return VS[:, at:at + WP]

        bb = ExitStack()
        staging = ExitStack()
        wst = sb(staging, "wst", [P, 2, KC, D])
        wstb = sb(staging, "wstb", [P, 2, KC, D], BF16)
        staging.close()
        KH = [sb(bb, f"KH{i}", [P, KC, TP], F32R) for i in range(2)]
        KL = [sb(bb, f"KL{i}", [P, KC, TP], F32R) for i in range(2)]
        qH = [sb(bb, f"qH{i}", [P, KC, S], F32R) for i in range(2)]
        qL = [sb(bb, f"qL{i}", [P, KC, S], F32R) for i in range(2)]
        maskS = sb(bb, "maskS", [P, 2, T + 1])
        sN = sb(bb, "sN", [P, 2, TP])
        pE = sb(bb, "pE", [P, 2, NT * TC + 1])
        pT = sb(bb, "pT", [P, 2, NT, S])
        nmx = sb(bb, "nmx", [P, HEADS])
        oN, oQ = sb(bb, "oN", [P, D]), sb(bb, "oQ", [P, D])
        oQb = sb(bb, "oQb", [P, D], BF16)
        oQT = sb(bb, "oQT", [P, KC, S], BF16)
        g2, xq2 = sb(bb, "g2", [P, D]), sb(bb, "xq2", [P, D])
        xq2b = sb(bb, "xq2b", [P, D], BF16)
        xq2T = sb(bb, "xq2T", [P, KC, S], BF16)
        xbo, y2 = sb(bb, "xbo", [P, D]), sb(bb, "y2", [P, D])
        sxB = sb(bb, "sxB", [P, S])
        t1, t2, t3 = (sb(bb, f"qt{i}", [P, KC, S]) for i in range(3))
        swqB, bqB = sb(bb, "swqB", [P, KC, S]), sb(bb, "bqB", [P, KC, S])
        bvB, boB, swoB = sb(bb, "bvB", [P, D]), sb(bb, "boB", [P, D]), sb(bb, "swoB", [P, D])
        wqT = sb(bb, "wqT", [P, 2, KC, D], BF16)
        wsm = sb(bb, "wsm", [P, 4, 2, KC])
        bqS = sb(bb, "bqS", [P, KC])
        st6b, mvb = sb(bb, "st6b", [P, 6]), sb(bb, "mvb", [P, 2])
        tb = sb(bb, "tb", [P, 24])
        rinv = sb(bb, "rinv", [P, HEADS])
        bb.close()

        cc = ExitStack()
        z, zT = sb(cc, "z", [P, B, D]), sb(cc, "zT", [P, 2, KC, S])
        st6c, mvc = sb(cc, "st6c", [P, B, 6]), sb(cc, "mvc", [P, B, 2])
        rsc = sb(cc, "rsc", [P, 2, B])
        gwT, gbB = sb(cc, "gwT", [P, KC, E]), sb(cc, "gbB", [P, 2, E])
        sc, sc2, cand = (sb(cc, n_, [P, B, E]) for n_ in ("sc", "sc2", "cand"))
        hot = sb(cc, "hot", [P, 3, B, E])
        best = sb(cc, "best", [P, 2, B])
        first_ = sb(cc, "first", [P, 2, B])
        iot = sb(cc, "iot", [P, B, E])
        gate = sb(cc, "gate", [P, 4, B])
        place, pick = sb(cc, "place", [P, B, E]), sb(cc, "pick", [P, B, E])
        slot, slotI = sb(cc, "slot", [P, 2, B]), sb(cc, "slotI", [P, 2, B], I32)
        need = sb(cc, "need", [P, 6, E])
        blk_e, blk_no = sb(cc, "blk_e", [1, NBLK, E]), sb(cc, "blk_no", [1, NBLK, E])
        blk_f, blk_x = sb(cc, "blk_f", [1, 2, NBLK]), sb(cc, "blk_x", [1, NBLK], I32)
        b1B = sb(cc, "b1B", [P, E, EH])
        xin, xT = sb(cc, "xin", [P, 2, D]), sb(cc, "xT", [P, 2, KC, P])
        hb, hs, hTe = sb(cc, "hb", [P, 2, EH]), sb(cc, "hs", [P, 2, EHP]), sb(cc, "hTe", [P, 2, 3, P])
        yb = sb(cc, "yb", [P, 2, D])
        picked = sb(cc, "picked", [P, 2, B, D])
        cc.close()

        C_MAGIC, C_NMAGIC, C_HALF, C_DEC, C_K, C_SUM = 0, 1, 2, 3, 4, 5
        C_EXP = 6

        def batches(eng, body):
            body(0, 0, 0, True, False)
            with eng.Fori(0, B // 2 - 1) as it:
                body(it * 2 + 1, 1, it, False, False)
                body(it * 2 + 2, 0, it + 1, False, False)
            body(B - 1, 1, B // 2 - 1, False, True)

        def blocks(eng, body, peeled=2):
            body(0, 0, 0)
            with eng.Fori(0, (NBLK - peeled) // 2) as it:
                body(it * 2 + 1, 1, it)
                body(it * 2 + 2, 0, it + 1)
            for s in range(NBLK + 1 - peeled, NBLK + 1):
                body(s, s % 2, s // 2)

        def started(s):
            return not isinstance(s, int) or s > 0

        def within(s, ahead):
            return not isinstance(s, int) or s + ahead < NBLK

        def block_expert(engine, s):
            return nc.values_load(blk_x[0:1, bass.ds(s, 1)], engines=[engine], min_val=0, max_val=E - 1,
                                  skip_runtime_bounds_check_because="it is a count held to E - 1 when made")

        def chain(eng, name, per):
            class Chain:
                def turn(self, t):
                    self.base, self.k = t * per, 0

                def __call__(self, ins, by_itself=False):
                    self.k += 1
                    ins.then_inc(sem(name), 1)
                    if by_itself:
                        alone(eng, (name, self.base + self.k))
                    else:
                        eng.wait_ge(sem(name), self.base + self.k)

                def end(self):
                    assert self.k == per, (name, self.k)
            return Chain()

        def scores_done(eng, b):
            if not isinstance(b, int) or b > 0:
                for r in range(2):
                    eng.wait_ge(sem(f"score{r}"), after(b * 8))

        def alone(eng, *waits):
            for name, v in waits:
                eng.wait_ge(sem(name), v)
            eng.sem_inc(sem("gone_on"), 1)

        def copies_on_act(h_):
            return h_ % 3 != 2

        def copy_p(eng, copy, b, h_):
            r, n = h_ % 2, b * 8 + h_ // 2
            eng.wait_ge(sem(f"p_turned{r}"), after(n + 1))
            eng.wait_ge(sem(f"pv{r}"), after(n))
            copy(pT[0:TC, r].rearrange("p c s -> p (c s)"), ps[0:TC, 2 + r, 0:NT * S]).then_inc(sem(f"p_copied{r}"), 1)

        block = whole.enter_context(nc.Block())

        @block.sync
        def _(sp):
            sp.dma_start(cols[:, C_DEC:C_DEC + 1], decay.partition_broadcast(P)).then_inc(sem("decay_in"), 16)
            sp.dma_start(biases[:, 0, :], b_in).then_inc(sem("biases_in"), 16)
            sp.dma_start(biases[:, 1, :], bk).then_inc(sem("biases_in"), 16)
            sp.dma_start(CT[:, 0, :], ctxT[0]).then_inc(sem("ctx_in0"), 16)
            sp.dma_start(stage(0), wk).then_inc(sem("stage_in0"), 16)
            sp.dma_start(stage(1), wv).then_inc(sem("stage_in1"), 16)
            for c in range(2):
                sp.dma_start(stage(2 + c), w1[c]).then_inc(sem(f"stage_in{2 + c}"), 16)
            for b in range(1, B):
                sp.dma_start(CT[:, b, :], ctxT[b]).then_inc(sem(f"ctx_in{b}"), 16)
            for c in range(2, NW):
                sp.wait_ge(sem("wkvL"), c - 1)
                sp.dma_start(stage(2 + c), w1[c]).then_inc(sem(f"stage_in{c - 2}"), 16)
            sp.dma_start(w1s[:], win).then_inc(sem("win_in"), 16)
            sp.dma_start(w2s[:], wout).then_inc(sem("win_in"), 16)
            sp.dma_start(boutB, b_out.partition_broadcast(B)).then_inc(sem("win_in"), 16)
            sp.dma_start(XR[0:S], x).then_inc(sem("vec_in"), 16)
            for t, src in ((gamma0B, gamma0), (beta0B, beta0), (gammafB, gammaf)):
                sp.dma_start(t[0:S, :], src.partition_broadcast(S)).then_inc(sem("vec_in"), 16)
            for c in range(NW):
                sp.wait_ge(sem("ternary"), c + 1)
                sp.dma_start(stage(2 + c), w2[c]).then_inc(sem(f"stage_in{(2 + c) % NW}"), 16)
            sp.wait_ge(sem("zeros"), 1)
            for i in range(NBLK // 4):
                sp.dma_start(slots_in[i * 4 * P:(i + 1) * 4 * P].rearrange("(p r) (q c) -> p (r q) c", r=4, c=P),
                             zeros[:].unsqueeze(1).to_broadcast([P, 4 * D // P, P])).then_inc(sem("slots_zero"), 16)
            sp.wait_ge(sem("summ_ready"), 1)
            sp.dma_start(summ_dram, summ).then_inc(sem("summ_out"), 16)
            sp.wait_ge(sem("summ_out"), 16)
            with sp.Fori(0, B) as b:
                sp.wait_ge(sem("summ_used"), after(b))
                sp.dma_start(summB[0:S], summ_dram[b].partition_broadcast(S)).then_inc(sem("summ_in"), 16)
            sp.wait_ge(sem("a_done"), 4)
            sp.dma_start(wst[:, 0], wq).then_inc(sem("wqo_in"), 16)
            sp.dma_start(wst[:, 1], wo).then_inc(sem("wqo_in"), 16)
            sp.dma_start(bqS[:], bq).then_inc(sem("wqo_in"), 16)
            for t, src in ((bvB, bv), (boB, bo)):
                sp.dma_start(t[0:S, :], src.partition_broadcast(S)).then_inc(sem("bvo_in"), 16)
            sp.wait_ge(sem("wscale"), 1)
            sp.dma_start(swo_dram.rearrange("(j p) -> p j", p=P), wsm[:, 1, 1, :], allow_slow_non_contiguous=True)\
              .then_inc(sem("swo_out"), 16)
            sp.wait_ge(sem("swo_out"), 16)
            sp.dma_start(swoB[0:S, :], swo_dram.partition_broadcast(S)).then_inc(sem("bvo_in"), 16)
            for j in range(2):
                sp.dma_start(maskS[0:S, j, 0:T], mask[j]).then_inc(sem(f"mask_in{j}"), 16)

            def expert_loads(b, j, more):
                sp.wait_ge(sem("kL"), b + 1)
                sp.dma_start(CT[:, b, 0:KC * EH], ew1[b]).then_inc(sem("ew1_in"), 16)
                sp.wait_ge(sem("o_norm"), after(b + 1))
                sp.dma_start(vs(b)[0:EC, 0:3 * D], ew2[b]).then_inc(sem("ew2_in"), 16)
                if more:
                    sp.wait_ge(sem("mask_used"), b + 1)
                    sp.dma_start(maskS[0:S, j, 0:T], mask[b + 2]).then_inc(sem(f"mask_in{j}"), 16)

            with sp.Fori(0, B // 2 - 1) as it:
                for j in range(2):
                    expert_loads(it * 2 + j, j, True)
            expert_loads(B - 2, 0, False)
            expert_loads(B - 1, 1, False)
            sp.wait_ge(sem("b_done"), 4)
            sp.dma_start(gwT[:], gate_w).then_inc(sem("c_in"), 16)
            sp.dma_start(gbB[0:S, 0, :], gate_b.partition_broadcast(S)).then_inc(sem("c_in"), 16)
            sp.dma_start(gbB[0:S, 1, :], gate_bias.partition_broadcast(S)).then_inc(sem("c_in"), 16)
            sp.dma_start(b1B[:], eb1.partition_broadcast(P)).then_inc(sem("c_in"), 16)

            def load_block(s, j, u):
                sp.dma_start(xin[:, j], slots_in[bass.ds(s * P, P)]).then_inc(sem(f"x_in{j}"), 16)

            sp.wait_ge(sem("sent"), 16 * TOPK * B)
            load_block(0, 0, 0)
            load_block(1, 1, 0)

            def step(s, j, u):
                if not started(s):
                    sp.wait_ge(sem("x_turned"), 1)
                    load_block(2, 0, 1)
                if within(s, 3):
                    sp.wait_ge(sem("x_turned"), s + 2)
                    load_block(s + 3, 1 - j, u + 1 + j)
                if started(s):
                    sp.wait_ge(sem("y_copied"), s)
                    sp.dma_start(slots_out[bass.ds((s - 1) * P, P)], yb[:, 1 - j]).then_inc(sem(f"y_out{1 - j}"), 16)

            blocks(sp, step, peeled=4)
            for b in range(B):
                sp.wait_ge(sem("combined"), b + 1)
                sp.dma_start(out[b], XR[0:S, b, :]).then_inc(sem("out"), 16)
            sp.wait_ge(sem("out"), 16 * B)

        @block.gpsimd
        def _(g):
            n = [0]

            def step(ins):
                n[0] += 1
                ins.then_inc(sem("pool_setup"), 1)
                g.wait_ge(sem("pool_setup"), n[0])

            step(g.iota(ident[:], [[1, P]], base=0, channel_multiplier=-1, allow_small_or_imprecise_dtypes=True))
            step(g.tensor_scalar(before[:], ident[:], 0.0, None, ALU.is_gt))
            step(g.tensor_scalar(ident[:], ident[:], 0.0, None, ALU.is_equal))
            step(g.tensor_copy(identb[:], ident[:]))
            step(g.memset(ones[:], 1.0))
            g.memset(zeros[:], 0.0).then_inc(sem("zeros"), 1)
            g.memset(cols[:, C_MAGIC:C_MAGIC + 1], MAGIC)
            g.memset(cols[:, C_NMAGIC:C_NMAGIC + 1], -MAGIC)
            g.memset(cols[:, C_HALF:C_HALF + 1], -0.5).then_inc(sem("consts"), 1)
            g.wait_ge(sem("consts"), 1)

            def rsqrt(dst, src, tmp, eps, tag, count, width=1):
                g.tensor_scalar(tmp, src, eps, None, ALU.add).then_inc(sem(tag + "_t"), 1)
                g.wait_ge(sem(tag + "_t"), count)
                half = cols[0:S, C_HALF:C_HALF + 1]
                half = half if width == 1 else half.to_broadcast([S, width])
                return g.tensor_tensor(dst, tmp, half, ALU.pow)

            g.wait_ge(sem("mv_all"), B)
            rsqrt(rs0[0:S, :], mv0[0:S, :, 1], rs0[0:S, :], LN_EPS, "rs_all", 1, B).then_inc(sem("rs_all"), 1)
            with g.Fori(0, B) as b:
                g.wait_ge(sem("cxH"), b + 1)
                g.tensor_tensor(cxL[:].rearrange("p k t -> p (k t)"), CT[:, b, :],
                                cxH[:].rearrange("p k t -> p (k t)").bitcast(F32), ALU.subtract)\
                 .then_inc(sem("cxL"), 1)
                g.wait_ge(sem("x1"), after(b))
                g.wait_ge(sem("vec_in"), 64)
                g.tensor_tensor(xb[0:S], XR[0:S, b, :], beta0B[0:S], ALU.add).then_inc(sem("xb"), 1)
                alone(g, ("mvA", b * 2 + 1))
                rsqrt(tk[0:S, 1:2], mv[0:S, 1:2], tk[0:S, 0:1], LN_EPS, "rsA", b * 2 + 1).then_inc(sem("rsA"), 1)
                alone(g, ("mvA", b * 2 + 2))
                rsqrt(tk[0:S, 3:4], mv[0:S, 1:2], tk[0:S, 2:3], LN_EPS, "rsA", b * 2 + 2).then_inc(sem("rsF"), 1)
                alone(g, ("rsF", b + 1))
                g.tensor_scalar(tk[0:S, 4:5], mv[0:S, 1:2], tk[0:S, 3:4], tk[0:S, 3:4], ALU.mult, ALU.mult)\
                 .then_inc(sem("msF"), 1)
                alone(g, ("msF", b + 1))
                rsqrt(tk[0:S, 6:7], tk[0:S, 4:5], tk[0:S, 5:6], RMS_EPS, "rms", b + 1).then_inc(sem("rms"), 1)
                alone(g, ("rms", b + 1))
                g.tensor_tensor(tk[0:S, 7:8], tk[0:S, 3:4], tk[0:S, 6:7], ALU.mult).then_inc(sem("uscale"), 1)
                g.wait_ge(sem("v_copied"), after((b + 1) * NT))
                g.tensor_copy(vs(b)[0:TC, :].rearrange("p (c h w) -> p c h w", c=NT, h=HEADS)[:, :, :, HD],
                              ones[0:TC, 0:NT * HEADS].rearrange("p (c h) -> p c h", c=NT))\
                 .then_inc(sem("v_ones"), 1)
                alone(g, ("h_round", b + 1), ("t2", after(b * 2)))
                g.tensor_scalar(hq[0:S, FF // 2:], h[0:S, FF // 2:], -MAGIC, 1.0, ALU.add, ALU.mult)\
                 .then_inc(sem("hq1"), 1)
            g.wait_ge(sem("hq1"), after(B))
            g.wait_ge(sem("v_ones"), B)
            g.tensor_copy(cols[:, 20:21], cols[:, 0:1]).then_inc(sem("a_done"), 1)
            g.wait_ge(sem("a_done"), 4)
            for i in range(2):
                g.memset(pE[0:S, i, T:NT * TC + 1], 0.0).then_inc(sem("p_pad"), 1)

            def low_keys(b, j, u):
                g.wait_ge(sem("kH"), b + 1)
                scores_done(g, b - 1)
                g.tensor_tensor(KL[j][:].rearrange("p k t -> p (k t)"), CT[:, b, :],
                                KH[j][:].rearrange("p k t -> p (k t)").bitcast(F32), ALU.subtract)\
                 .then_inc(sem("kL"), 1)

            def rstd_b(b):
                alone(g, ("mvB", b + 1))
                rsqrt(tb[0:S, 1:2], mvb[0:S, 1:2], tb[0:S, 0:1], LN_EPS, "rsB_t", b + 1).then_inc(sem("rsB"), 1)

            def with_bo(b):
                g.wait_ge(sem("x3"), after(b))
                g.tensor_tensor(xbo[0:S], XR[0:S, b, :], boB[0:S], ALU.add).then_inc(sem("xbo"), 1)

            def body(b, j, u, first, last):
                if not first:
                    with_bo(b - 1)
                if not last:
                    low_keys(b + 1, 1 - j, u + j)
                    rstd_b(b + 1)

            g.wait_ge(sem("bvo_in"), 48)
            low_keys(0, 0, 0)
            rstd_b(0)
            batches(g, body)
            with_bo(B - 1)
            g.wait_ge(sem("xbo"), B)
            g.tensor_copy(cols[:, 20:21], cols[:, 1:2]).then_inc(sem("b_done"), 1)
            g.wait_ge(sem("b_done"), 4)
            g.iota(iot[:], [[0, B], [1, E]], base=0, channel_multiplier=0, allow_small_or_imprecise_dtypes=True)\
             .then_inc(sem("c_setup"), 1)
            g.iota(blk_no[:], [[1, NBLK], [0, E]], base=0, channel_multiplier=0, allow_small_or_imprecise_dtypes=True)\
             .then_inc(sem("c_setup"), 1)
            for j in range(2):
                g.memset(hs[:, j, EH:EH + 1], 1.0).then_inc(sem("c_setup"), 1)
                g.memset(hs[:, j, EH + 1:EHP], 0.0).then_inc(sem("c_setup"), 1)
            g.wait_ge(sem("mv_all"), 2 * B)
            rsqrt(rsc[0:S, 1, :], mvc[0:S, :, 1], rsc[0:S, 0, :], LN_EPS, "rs_all", 2, B).then_inc(sem("rs_all"), 1)
            g.wait_ge(sem("slots"), 1)
            g.wait_ge(sem("slots_zero"), 16 * (NBLK // 4))
            for b in range(B):
                for k in range(TOPK):
                    g.indirect_dma_start(slots_in, bass.IndirectOffsetOnAxis(slotI[0:S, k, b:b + 1], 0), z[0:S, b, :], None,
                                         bounds_check=NBLK * P - 1).then_inc(sem("sent"), 16)
            g.wait_ge(sem("y_out0"), after(16 * (NBLK // 2)))
            g.wait_ge(sem("y_out1"), after(16 * (NBLK // 2)))
            for b in range(B):
                for k in range(TOPK):
                    g.indirect_dma_start(picked[0:S, k, b, :], None, slots_out,
                                         bass.IndirectOffsetOnAxis(slotI[0:S, k, b:b + 1], 0),
                                         bounds_check=NBLK * P - 1).then_inc(sem(f"back{b // 2}"), 16)

        @block.scalar
        def _(act):
            act.wait_ge(sem("decay_in"), 16)
            act.activation(cols[:, C_EXP:C_EXP + 1], cols[:, C_DEC:C_DEC + 1], ACT.Exp, scale=-1.0)\
               .then_inc(sem("decay_exp"), 1)
            act.wait_ge(sem("stage_in0"), 16)
            act.copy(wkH[:].rearrange("p k n -> p (k n)"), stage(0)).then_inc(sem("wkvH"), 1)
            act.wait_ge(sem("stage_in1"), 16)
            act.copy(wvH[:].rearrange("p k n -> p (k n)"), stage(1)).then_inc(sem("wkvH"), 1)
            act.wait_ge(sem("consts"), 1)
            for w in range(2):
                for c in range(NW):
                    slot = (2 + c) % NW
                    act.wait_ge(sem(f"stage_in{slot}"), 16 * (w + 1 + (slot < 2)))
                    if w + c:
                        act.wait_ge(sem("abs_sum"), NW * w + c)
                    act.activation(hq[:, 0:WP], stage(slot), ACT.Abs, accum_out=asum[:, w, c:c + 1])\
                       .then_inc(sem("abs_sum"), 1)
                act.wait_ge(sem("w_scale"), w + 1)
                for c in range(NW):
                    act.activation(stage(2 + c), stage(2 + c), ACT.Identity, bias=cols[:, C_MAGIC:C_MAGIC + 1],
                                   scale=wsc[:, w, 2:3]).then_inc(sem("w_round"), 1)
            for b in range(B):
                act.wait_ge(sem(f"ctx_in{b}"), 16)

            with act.Fori(0, B) as b:
                alone(act, ("v_mm", after(b * NT)))
                act.copy(cxH[:].rearrange("p k t -> p (k t)"), CT[:, b, :]).then_inc(sem("cxH"), 1)
                for m in range(KC):
                    alone(act, ("k_mm", b * KC + m + 1))
                    act.activation(CT[:, b, m * TP:(m + 1) * TP], ps[:, m % 2, 0:TP], ACT.Identity,
                                   bias=biases[:, 1, m:m + 1]).then_inc(sem("k_copied"), 1)
                act.wait_ge(sem("t1"), after(b + 1))
                act.wait_ge(sem("g1"), after(b * 4))
                act.copy(xqT[:].rearrange("p k s -> p (k s)"), ps[:, 6, 0:KC * S // 2].bitcast(BF16))\
                   .then_inc(sem("xqT"), 1)
                act.wait_ge(sem("dq1"), b + 1)
                act.wait_ge(sem("hq0"), after(b))
                act.wait_ge(sem("hq1"), after(b))
                for m in range(4):
                    act.wait_ge(sem("g1"), after(b * 4 + m + 1))
                    act.activation(h[0:S, m * 512:(m + 1) * 512], ps[0:S, 2 + m, :], ACT.Gelu,
                                   scale=tk[0:S, 12:13]).then_inc(sem("gelu"), 1)
                act.wait_ge(sem("t2"), after(b * 2 + 1))
                act.wait_ge(sem("g2"), after(b))
                act.copy(hqT[:, 0:8, :].rearrange("p k s -> p (k s)"), ps[:, 6, 0:4 * S].bitcast(BF16))\
                   .then_inc(sem("hqT0"), 1)
            act.wait_ge(sem("hqT0"), after(B))
            act.copy(cols[:, 21:22], cols[:, 0:1]).then_inc(sem("a_done"), 1)
            act.wait_ge(sem("a_done"), 4)
            act.wait_ge(sem("wscale"), 2)
            for w in range(2):
                for j in range(KC):
                    act.activation(wst[:, w, j, :], wst[:, w, j, :], ACT.Identity, bias=cols[:, C_MAGIC:C_MAGIC + 1],
                                   scale=wsm[:, 2, w, j:j + 1]).then_inc(sem("wq_round"), 1)
            for i in range(0, 8, 2):
                act.wait_ge(sem("wq_t"), i + 1)
                act.copy(wqT[:, i // KC, i % KC, :], ps[:, i, 0:D // 2].bitcast(BF16)).then_inc(sem("wqT_act"), 1)

            def high_keys(b, j, u):
                scores_done(act, b - 1)
                act.copy(KH[j][:].rearrange("p k t -> p (k t)"), CT[:, b, :]).then_inc(sem("kH"), 1)

            def turned_x(b):
                act.wait_ge(sem("xq2_t"), b + 1)
                act.copy(xq2T[:].rearrange("p k s -> p (k s)"), ps[:, 7, 0:KC * S // 2].bitcast(BF16))\
                   .then_inc(sem("xq2T"), 1)

            def turned_o(b):
                act.wait_ge(sem("oq_t"), b + 1)
                act.copy(oQT[:].rearrange("p k s -> p (k s)"), ps[:, 7, 0:KC * S // 2].bitcast(BF16))\
                   .then_inc(sem("oQT"), 1)

            def body(b, j, u, first, last):
                for h_ in range(HEADS + 1):
                    if h_ < HEADS:
                        r, n = h_ % 2, b * 8 + h_ // 2
                        act.wait_ge(sem(f"masked{r}"), after(n + 1))
                        act.wait_ge(sem(f"p_turned{r}"), after(n))
                        act.activation(pE[0:S, r, 0:T], sN[0:S, r, 0:T], ACT.Exp, scale=-1.0,
                                       bias=nmx[0:S, h_:h_ + 1]).then_inc(sem(f"exp{r}"), 1)
                    if h_ and copies_on_act(h_ - 1):
                        copy_p(act, act.copy, b, h_ - 1)
                    if h_ == 3 and not last:
                        high_keys(b + 1, 1 - j, u + j)
                    if h_ == 7 and not first:
                        turned_o(b - 1)
                    if h_ == 13 and not last:
                        turned_x(b + 1)

            act.wait_ge(sem("wq_t"), 8)
            high_keys(0, 0, 0)
            turned_x(0)
            batches(act, body)
            turned_o(B - 1)
            act.wait_ge(sem("oQT"), after(B))
            act.copy(cols[:, 21:22], cols[:, 1:2]).then_inc(sem("b_done"), 1)
            act.wait_ge(sem("b_done"), 4)
            for b in range(B):
                act.wait_ge(sem("z_t"), b + 1)
                act.copy(zT[:, b % 2].rearrange("p k s -> p (k s)"), ps[:, b % 2, 0:KC * S]).then_inc(sem("zT"), 1)
            act.wait_ge(sem("gap"), 1)
            act.activation(gate[0:S, 1], gate[0:S, 0], ACT.Exp).then_inc(sem("gap_exp"), 1)

            def step(s, j, u):
                if started(s):
                    act.wait_ge(sem("h_turned"), s)
                    act.copy(hTe[0:EC, 1 - j].rearrange("p c s -> p (c s)"), ps[0:EC, 5 - j, 0:3 * P])\
                       .then_inc(sem("hT"), 1)
                if within(s, 0):
                    act.wait_ge(sem("h_biased"), s + 1)
                    act.activation(hs[:, j, 0:EH], hb[:, j], ACT.Silu).then_inc(sem("h_act"), 1)
                if started(s):
                    act.wait_ge(sem("y_mm"), s)
                    act.wait_ge(sem(f"y_out{1 - j}"), after((u + j - 1) * 16))
                    act.copy(yb[:, 1 - j], ps[:, 7 - j, :]).then_inc(sem("y_copied"), 1)

            act.wait_ge(sem("c_setup"), 6)
            blocks(act, step)

        @block.tensor
        def _(pe):
            for name in credited:
                pe.sem_inc(sem(name), 1)
            pe.wait_ge(sem("consts"), 1)
            pe.wait_ge(sem("kvw"), KC * B)
            pe.wait_ge(sem("win_in"), 48)
            for m in range(KC):
                for k in range(KC):
                    mm = pe.matmul(ps[:, 7, m * B:(m + 1) * B], w1s[:, k * D + m * P:k * D + (m + 1) * P], kvw[:, k, :],
                                   start=(k == 0), stop=(k == KC - 1))
            mm.then_inc(sem("xm_mm"), 1)
            pe.wait_ge(sem("xm"), 1)
            for k in range(KC):
                mm = pe.matmul(ps[0:B, 6, :], xm[:, k, :], w2s[:, k * D:(k + 1) * D], start=(k == 0), stop=(k == KC - 1))
            mm.then_inc(sem("summ_mm"), 1)
            for w in range(2):
                pe.wait_ge(sem("abs_sum"), NW * (w + 1))
                pe.matmul(ps[:, 5, 0:NW], ones[:, :], asum[:, w, :], start=True, stop=True).then_inc(sem("w_total"), 1)
            pe.wait_ge(sem("w_scale"), 2)
            pe.wait_ge(sem("summ_ready"), 1)
            pe.wait_ge(sem("wkvL"), 2)
            with pe.Fori(0, B) as b:
                pe.wait_ge(sem("cxL"), b + 1)
                for m in range(KC):
                    if m < 2:
                        pe.wait_ge(sem("v_copied"), after(b * NT))
                    else:
                        pe.wait_ge(sem("k_copied"), after(b * KC + m - 1))
                    n = 0
                    for wt, cx in ((wkH, cxH), (wkH, cxL), (wkL, cxH)):
                        for k in range(KC):
                            mm = pe.matmul(ps[:, m % 2, 0:TP], wt[:, k, m * P:(m + 1) * P], cx[:, k, :],
                                           start=(n == 0), stop=(n == 3 * KC - 1))
                            n += 1
                    mm.then_inc(sem("k_mm"), 1)
                pe.wait_ge(sem("xqb"), b + 1)
                pe.wait_ge(sem("hqT0"), after(b))
                for k in range(KC):
                    mm = pe.transpose(ps[:, 6, k * S // 2:(k + 1) * S // 2].bitcast(BF16), xqb[0:S, k * P:(k + 1) * P],
                                      identb[0:S, 0:S])
                mm.then_inc(sem("t1"), 1)
                alone(pe, ("xqT", b + 1), ("ternary", NW), ("gelu", after(b * 4)))
                for m in range(4):
                    for k in range(KC):
                        mm = pe.matmul(ps[0:S, 2 + m, :], xqT[:, k, :], w1q[:, k * FF + m * 512:k * FF + (m + 1) * 512],
                                       start=(k == 0), stop=(k == KC - 1))
                    mm.then_inc(sem("g1"), 1)
                for c in range(NT):
                    if c < 2:
                        pe.wait_ge(sem("k_copied"), after(b * KC + c + 3))
                    else:
                        pe.wait_ge(sem("v_copied"), after(b * NT + 1))
                    n = 0
                    for cx, wt in ((cxH, wvH), (cxH, wvL), (cxL, wvH)):
                        for k in range(KC):
                            mm = pe.matmul(ps[0:TC, c % 2, :], cx[:, k, c * TC:(c + 1) * TC], wt[:, k, :],
                                           start=(n == 0), stop=(n == 3 * KC - 1))
                            n += 1
                    mm.then_inc(sem("v_mm"), 1)
                pe.wait_ge(sem("hq0"), after(b + 1))
                pe.wait_ge(sem("hq1"), after(b + 1))
                pe.wait_ge(sem("x2"), after(b))
                for half in range(2):
                    for k in range(8):
                        mm = pe.transpose(ps[:, 6 + half, k * S // 2:(k + 1) * S // 2].bitcast(BF16),
                                          hq[0:S, (half * 8 + k) * P:(half * 8 + k + 1) * P], identb[0:S, 0:S])
                    mm.then_inc(sem("t2"), 1)
                alone(pe, ("hqT0", after(b + 1)), ("hqT1", b + 1), ("ternary", 2 * NW))
                for k in range(FC):
                    mm = pe.matmul(ps[0:S, 7, :], hqT[:, k, :], w2q[:, k * D:(k + 1) * D],
                                   start=(k == 0), stop=(k == FC - 1))
                mm.then_inc(sem("g2"), 1)
            pe.wait_ge(sem("x2"), after(B))
            pe.matmul(ps[:, 0, 0:1], ones[:, :], ones[:, 0:1], start=True, stop=True).then_inc(sem("a_done"), 1)
            pe.wait_ge(sem("a_done"), 4)
            for i in range(8):
                w, k = divmod(i, KC)
                pe.wait_ge(sem("wq_b"), (w + 1) * KC)
                for j in range(KC):
                    mm = pe.transpose(ps[:, i, j * P // 2:(j + 1) * P // 2].bitcast(BF16),
                                      wstb[:, w, j, k * P:(k + 1) * P], identb[:, :])
                mm.then_inc(sem("wq_t"), 1)
            pe.wait_ge(sem("wqT_act"), 4)
            pe.wait_ge(sem("wqT_dve"), 4)

            def turn_rows(src, name, b):
                for k in range(KC):
                    mm = pe.transpose(ps[:, 7, k * S // 2:(k + 1) * S // 2].bitcast(BF16), src[0:S, k * P:(k + 1) * P],
                                      identb[0:S, 0:S])
                mm.then_inc(sem(name), 1)

            def queries(b):
                pe.wait_ge(sem("xq2T"), b + 1)
                pe.transpose(ps[:, 6, KC * S:(KC + 1) * S], tb[0:S, 4:5].to_broadcast([S, P]), ident[0:S, 0:S])
                for m in range(KC):
                    for k in range(KC):
                        mm = pe.matmul(ps[:, 6, m * S:(m + 1) * S], wqT[:, 0, k, m * P:(m + 1) * P], xq2T[:, k, :],
                                       start=(k == 0), stop=(k == KC - 1))
                mm.then_inc(sem("q_mm"), 1)

            def out_rows(b):
                pe.wait_ge(sem("oQT"), after(b + 1))
                for k in range(KC):
                    mm = pe.matmul(ps[0:S, 6, :], oQT[:, k, :], wqT[:, 1, k, :], start=(k == 0), stop=(k == KC - 1))
                mm.then_inc(sem("wo_mm"), 1)

            def body(b, j, u, first, last):
                pe.wait_ge(sem("q_ready"), b + 1)
                pe.wait_ge(sem("kL"), b + 1)
                for h_ in range(HEADS + 2):
                    if h_ < HEADS:
                        r, n, m, at = h_ % 2, b * 8 + h_ // 2, h_ // HPC, h_ % HPC * HD
                        pe.wait_ge(sem(f"masked{r}"), after(n))
                        for i, (q, kk) in enumerate(((qH[j], KH[j]), (qH[j], KL[j]), (qL[j], KH[j]))):
                            mm = pe.matmul(ps[0:S, r, 0:TP], q[at:at + HD, m, :], kk[at:at + HD, m, :],
                                           start=(i == 0), stop=(i == 2))
                        mm.then_inc(sem(f"score{r}"), 1)
                    if 1 <= h_ <= HEADS:
                        r, n = (h_ - 1) % 2, b * 8 + (h_ - 1) // 2
                        pe.wait_ge(sem(f"exp{r}"), after(n + 1))
                        pe.wait_ge(sem(f"p_copied{r}"), after(n))
                        for c in range(NT):
                            mm = pe.transpose(ps[0:TC, 2 + r, c * S:(c + 1) * S], pE[0:S, r, c * TC:(c + 1) * TC],
                                              ident[0:S, 0:S])
                        mm.then_inc(sem(f"p_turned{r}"), 1)
                    if h_ >= 2:
                        hh = h_ - 2
                        r, n = hh % 2, b * 8 + hh // 2
                        pe.wait_ge(sem(f"p_copied{r}"), after(n + 1))
                        if hh == 0:
                            pe.wait_ge(sem("o_norm"), after(b))
                        for c in range(NT):
                            at = c * VW + hh * (HD + 1)
                            mm = pe.matmul(ps[0:S, 4 + hh // 8, hh % 8 * (HD + 1):(hh % 8 + 1) * (HD + 1)],
                                           pT[0:TC, r, c, :], vs(b)[0:TC, at:at + HD + 1],
                                           start=(c == 0), stop=(c == NT - 1))
                        mm.then_inc(sem(f"pv{r}"), 1)
                    if h_ == 6 and not first:
                        pe.wait_ge(sem("oQb"), after(b))
                        turn_rows(oQb, "oq_t", b - 1)
                    if h_ == 8 and not first:
                        out_rows(b - 1)
                    if h_ == 12 and not last:
                        pe.wait_ge(sem("xq2b"), b + 2)
                        pe.wait_ge(sem("oQT"), after(b))
                        turn_rows(xq2b, "xq2_t", b + 1)
                    if h_ == 14 and not last:
                        pe.wait_ge(sem("x3"), after(b))
                        queries(b + 1)

            pe.wait_ge(sem("xq2b"), 1)
            turn_rows(xq2b, "xq2_t", 0)
            queries(0)
            batches(pe, body)
            pe.wait_ge(sem("oQb"), after(B))
            turn_rows(oQb, "oq_t", B - 1)
            out_rows(B - 1)
            pe.wait_ge(sem("x3"), after(B))
            pe.matmul(ps[:, 0, 0:1], ones[:, :], ones[:, 0:1], start=True, stop=True).then_inc(sem("b_done"), 1)
            pe.wait_ge(sem("b_done"), 4)
            pe.wait_ge(sem("ew1_in"), 16 * E)
            pe.wait_ge(sem("ew2_in"), 16 * E)
            pe.wait_ge(sem("c_in"), 64)
            for b in range(B + 1):
                if b < B:
                    pe.wait_ge(sem("z"), b + 1)
                    for k in range(KC):
                        mm = pe.transpose(ps[:, b % 2, k * S:(k + 1) * S], z[0:S, b, k * P:(k + 1) * P],
                                          ident[0:S, 0:S])
                    mm.then_inc(sem("z_t"), 1)
                if b:
                    pe.wait_ge(sem("zT"), b)
                    for k in range(KC):
                        mm = pe.matmul(ps[0:S, 2, (b - 1) * E:b * E], zT[:, (b - 1) % 2, k, :], gwT[:, k, :],
                                       start=(k == 0), stop=(k == KC - 1))
                    mm.then_inc(sem("logit"), 1)
            pe.wait_ge(sem("hot"), 1)
            both = hot[0:S, 2].rearrange("p b e -> p (b e)")
            pe.matmul(ps[0:S, 3, 0:B * E], before[0:S, 0:S], both, start=True, stop=False)
            for d in range(1, B):
                pe.matmul(ps[0:S, 3, d * E:B * E], ones[0:S, 0:S], both[:, 0:(B - d) * E],
                          start=False, stop=(d == B - 1))
            for b in range(B):
                mm = pe.matmul(ps[:, 4, 0:E], ones[0:S, :], both[:, b * E:(b + 1) * E], start=(b == 0), stop=(b == B - 1))
            mm.then_inc(sem("counts"), 1)

            def turn_x(s, j, u):
                pe.wait_ge(sem(f"x_in{j}"), u * 16 + 16)
                for k in range(KC):
                    mm = pe.transpose(ps[:, j, k * P:(k + 1) * P], xin[:, j, k * P:(k + 1) * P], ident[:, :])
                mm.then_inc(sem("x_turned"), 1)

            def step(s, j, u):
                if within(s, 0):
                    e = block_expert(mybir.EngineType.PE, s)
                    pe.wait_ge(sem("xT"), s + 1)
                    for k in range(KC):
                        mm = pe.matmul(ps[:, 2 + j, 0:EH], xT[:, j, k, :], CT[:, e, k * EH:(k + 1) * EH],
                                       start=(k == 0), stop=(k == KC - 1))
                    mm.then_inc(sem("h_mm"), 1)
                if started(s):
                    pe.wait_ge(sem("h_act"), s)
                    for c in range(3):
                        mm = pe.transpose(ps[0:EC, 5 - j, c * P:(c + 1) * P], hs[:, 1 - j, c * EC:(c + 1) * EC], ident[:, :])
                    mm.then_inc(sem("h_turned"), 1)
                if within(s, 1):
                    turn_x(s + 1, 1 - j, u + j)
                if started(s):
                    e = block_expert(mybir.EngineType.PE, s - 1)
                    pe.wait_ge(sem("hT"), s)
                    for c in range(3):
                        mm = pe.matmul(ps[:, 7 - j, :], hTe[0:EC, 1 - j, c, :], vs(e)[0:EC, c * D:(c + 1) * D],
                                       start=(c == 0), stop=(c == 2))
                    mm.then_inc(sem("y_mm"), 1)

            pe.wait_ge(sem("block_experts"), 1)
            turn_x(0, 0, 0)
            blocks(pe, step)

        @block.vector
        def _(dve):
            ch = once = chain(dve, "dve_once", 0)
            ch.turn(0)
            ch(dve.memset(krow, 1.0))
            dve.wait_ge(sem("decay_exp"), 1)
            ch(dve.tensor_scalar(cols[:, C_K:C_K + 1], cols[:, C_EXP:C_EXP + 1], 1.0, None, ALU.add))
            ch(dve.reciprocal(cols[:, C_K + 2:C_K + 3], cols[:, C_K:C_K + 1]))
            ch(dve.tensor_scalar(y[:, 0:T], krow[:, 0:T], cols[:, C_K + 2:C_K + 3], None, ALU.mult))
            ch(dve.tensor_tensor_scan(out=xq[:, T - 1::-1], data0=y[:, 0:T], data1=krow[:, 0:T],
                                      initial=0.0, op0=ALU.mult, op1=ALU.add))
            ch(dve.tensor_scalar(cw[:, 0:T], xq[:, 0:T], 1.0 / T, None, ALU.mult))
            ch(dve.tensor_reduce(cols[:, C_SUM:C_SUM + 1], cw[:, 0:T], AX.X, ALU.add))
            dve.wait_ge(sem("biases_in"), 32)
            ch(dve.tensor_scalar(biases[:, 2, :], biases[:, 0, :], cols[:, C_SUM:C_SUM + 1], None, ALU.mult))
            for i, (hi, lo) in enumerate(((wkH, wkL), (wvH, wvL))):
                dve.wait_ge(sem("wkvH"), i + 1)
                dve.tensor_tensor(lo[:].rearrange("p k n -> p (k n)"), stage(i),
                                  hi[:].rearrange("p k n -> p (k n)").bitcast(F32), ALU.subtract)\
                   .then_inc(sem("wkvL"), 1)
            for b in range(B):
                dve.wait_ge(sem(f"ctx_in{b}"), 16)
                for k in range(KC):
                    i = b * KC + k
                    if i >= 3:
                        dve.wait_ge(sem("kvw"), i - 2)
                    dve.tensor_tensor_reduce(out=junk[i % 3], in0=CT[:, b, k * TP:k * TP + T], in1=cw[:, 0:T],
                                             scale=1.0, scalar=0.0, op0=ALU.mult, op1=ALU.add,
                                             accum_out=kvw[:, k, b:b + 1]).then_inc(sem("kvw"), 1)
            dve.wait_ge(sem("xm_mm"), 1)
            dve.tensor_tensor(xm[:], ps[:, 7, 0:KC * B].rearrange("p (k b) -> p k b", k=KC),
                              biases[:, 2, :].unsqueeze(2).to_broadcast([P, KC, B]), ALU.add).then_inc(sem("xm"), 1)
            dve.wait_ge(sem("summ_mm"), 1)
            dve.wait_ge(sem("win_in"), 48)
            dve.tensor_tensor(summ, ps[0:B, 6, :], boutB, ALU.add).then_inc(sem("summ_ready"), 1)

            def w_scale(w):
                dve.wait_ge(sem("w_total"), w + 1)
                ch(dve.tensor_reduce(wsc[:, w, 0:1], ps[:, 5, 0:NW], AX.X, ALU.add))
                ch(dve.tensor_scalar(wsc[:, w, 1:2], wsc[:, w, 0:1], 1.0 / (D * FF), 1e-5, ALU.mult, ALU.max))
                dve.reciprocal(wsc[:, w, 2:3], wsc[:, w, 1:2]).then_inc(sem("w_scale"), 1)

            def ternary(w):
                dst = (w1q, w2q)[w]
                for c in range(NW):
                    dve.wait_ge(sem("w_round"), NW * w + c + 1)
                    ch(dve.tensor_scalar(stage(2 + c), stage(2 + c), MAGIC - 1.0, MAGIC + 1.0, ALU.max, ALU.min))
                    dve.tensor_scalar(dst[:, c * WP:(c + 1) * WP], stage(2 + c), MAGIC, None, ALU.subtract,
                                      saturate=False).then_inc(sem("ternary"), 1)

            w_scale(0)
            ternary(0)
            w_scale(1)
            ternary(1)
            dve.wait_ge(sem("w_scale"), 2)
            dve.wait_ge(sem("vec_in"), 64)
            for b in range(B):
                ch(dve.bn_stats(st0[0:S, b, :], XR[0:S, b, :]))
                dve.bn_aggr(mv0[0:S, b, :], st0[0:S, b, :]).then_inc(sem("mv_all"), 1)
            dve.wait_ge(sem("rs_all"), 1)
            dve.wait_ge(sem("vec_in"), 64)

            ch = chain(dve, "dve_a", 16)
            with dve.Fori(0, B) as b:
                ch.turn(b)
                xr = XR[0:S, b, :]
                dve.wait_ge(sem("summ_in"), 16 * b + 16)
                dve.scalar_tensor_tensor(out=y[0:S], in0=xr, scalar=rs0[0:S, bass.ds(b, 1)], in1=summB[0:S],
                                         op0=ALU.mult, op1=ALU.add).then_inc(sem("summ_used"), 1)
                dve.wait_ge(sem("summ_used"), after(b + 1))
                ch(dve.bn_stats(st6[0:S], y[0:S]), True)
                dve.bn_aggr(mv[0:S], st6[0:S]).then_inc(sem("mvA"), 1)
                dve.wait_ge(sem("mvA"), b * 2 + 1)
                ch(dve.scalar_tensor_tensor(out=xq[0:S], in0=y[0:S], scalar=mv[0:S, 0:1], in1=gamma0B[0:S],
                                            op0=ALU.subtract, op1=ALU.mult))
                dve.wait_ge(sem("rsA"), b + 1)
                dve.wait_ge(sem("xb"), b + 1)
                dve.scalar_tensor_tensor(out=xr, in0=xq[0:S], scalar=tk[0:S, 1:2], in1=xb[0:S],
                                         op0=ALU.mult, op1=ALU.add).then_inc(sem("x1"), 1)
                alone(dve, ("x1", after(b + 1)))
                ch(dve.bn_stats(st6[0:S], xr), True)
                dve.bn_aggr(mv[0:S], st6[0:S]).then_inc(sem("mvA"), 1)
                dve.wait_ge(sem("mvA"), b * 2 + 2)
                ch(dve.scalar_tensor_tensor(out=y[0:S], in0=xr, scalar=mv[0:S, 0:1], in1=gammafB[0:S],
                                            op0=ALU.subtract, op1=ALU.mult))
                ch(dve.tensor_reduce(tk[0:S, 8:9], y[0:S], AX.X, ALU.max, apply_absolute_value=True))
                dve.wait_ge(sem("uscale"), b + 1)
                ch(dve.tensor_scalar(tk[0:S, 9:10], tk[0:S, 8:9], tk[0:S, 7:8], 1e-5, ALU.mult, ALU.max))
                ch(dve.reciprocal(tk[0:S, 10:11], tk[0:S, 9:10]))
                ch(dve.tensor_scalar(tk[0:S, 11:12], tk[0:S, 10:11], tk[0:S, 7:8], QMAX, ALU.mult, ALU.mult))
                ch(dve.tensor_scalar(xq[0:S], y[0:S], tk[0:S, 11:12], MAGIC, ALU.mult, ALU.add))
                dve.wait_ge(sem("t1"), after(b))
                dve.tensor_scalar(xqb[0:S], xq[0:S], MAGIC, None, ALU.subtract).then_inc(sem("xqb"), 1)
                dve.wait_ge(sem("gelu"), after(b * 4))
                dve.tensor_scalar(tk[0:S, 12:13], tk[0:S, 9:10], wsc[0:S, 0, 1:2], 1.0 / QMAX, ALU.mult, ALU.mult)\
                   .then_inc(sem("dq1"), 1)
                for m in range(4):
                    dve.wait_ge(sem("gelu"), after(b * 4 + m + 1))
                    ins = dve.tensor_reduce(tk[0:S, 14 + m:15 + m], h[0:S, m * 512:(m + 1) * 512], AX.X, ALU.max,
                                            apply_absolute_value=True)
                ch(ins)
                ch(dve.tensor_reduce(tk[0:S, 18:19], tk[0:S, 14:18], AX.X, ALU.max))
                ch(dve.tensor_scalar(tk[0:S, 19:20], tk[0:S, 18:19], 1e-5, None, ALU.max))
                ch(dve.reciprocal(tk[0:S, 20:21], tk[0:S, 19:20]))
                ch(dve.tensor_scalar(tk[0:S, 21:22], tk[0:S, 20:21], QMAX, None, ALU.mult))
                dve.tensor_scalar(h[0:S, FF // 2:], h[0:S, FF // 2:], tk[0:S, 21:22], MAGIC, ALU.mult, ALU.add)\
                   .then_inc(sem("h_round"), 1)
                ch(dve.tensor_scalar(h[0:S, 0:FF // 2], h[0:S, 0:FF // 2], tk[0:S, 21:22], MAGIC, ALU.mult, ALU.add))
                dve.wait_ge(sem("t2"), after(b * 2))
                dve.tensor_scalar(hq[0:S, 0:FF // 2], h[0:S, 0:FF // 2], MAGIC, None, ALU.subtract)\
                   .then_inc(sem("hq0"), 1)
                for c in range(NT):
                    dve.wait_ge(sem("v_mm"), after(b * NT + c + 1))
                    dve.tensor_copy(vs(b)[0:TC, c * VW:(c + 1) * VW].rearrange("p (h w) -> p h w", h=HEADS)[:, :, 0:HD],
                                    ps[0:TC, c % 2, :].rearrange("p (h w) -> p h w", h=HEADS))\
                       .then_inc(sem("v_copied"), 1)
                dve.wait_ge(sem("t2"), after(b * 2 + 2))
                dve.tensor_copy(hqT[:, 8:16, :].rearrange("p k s -> p (k s)"), ps[:, 7, 0:4 * S].bitcast(BF16))\
                   .then_inc(sem("hqT1"), 1)
                ch(dve.tensor_scalar(tk[0:S, 22:23], tk[0:S, 19:20], wsc[0:S, 1, 1:2], 1.0 / QMAX, ALU.mult, ALU.mult))
                dve.wait_ge(sem("g2"), after(b + 1))
                dve.scalar_tensor_tensor(out=xr, in0=ps[0:S, 7, :], scalar=tk[0:S, 22:23], in1=xr,
                                         op0=ALU.mult, op1=ALU.add).then_inc(sem("x2"), 1)
                ch.end()
            dve.wait_ge(sem("x2"), after(B))
            dve.tensor_copy(cols[:, 22:23], cols[:, 0:1]).then_inc(sem("a_done"), 1)

            dve.wait_ge(sem("a_done"), 4)
            ch = once
            dve.wait_ge(sem("wqo_in"), 48)
            for w in range(2):
                for j in range(KC):
                    ins = dve.tensor_reduce(wsm[:, 0, w, j:j + 1], wst[:, w, j, :], AX.X, ALU.max,
                                            apply_absolute_value=True)
            ch(ins)
            dve.tensor_scalar(wsm[:, 1], wsm[:, 0], 1.0 / QMAX, 1e-8, ALU.mult, ALU.max).then_inc(sem("wscale"), 1)
            dve.wait_ge(sem("wscale"), 1)
            dve.reciprocal(wsm[:, 2], wsm[:, 1]).then_inc(sem("wscale"), 1)
            dve.wait_ge(sem("wqo_in"), 48)
            inv = float(HD) ** -0.5
            for m in range(KC):
                dve.tensor_scalar(swqB[:, m, :], ones[:, 0:S], wsm[:, 1, 0, m:m + 1], inv, ALU.mult, ALU.mult)
                ch(dve.tensor_scalar(bqB[:, m, :], ones[:, 0:S], bqS[:, m:m + 1], inv, ALU.mult, ALU.mult))
            for i in range(8):
                dve.wait_ge(sem("wq_round"), i + 1)
                dve.tensor_scalar(wstb[:, i // KC, i % KC, :], wst[:, i // KC, i % KC, :], MAGIC, None, ALU.subtract)\
                   .then_inc(sem("wq_b"), 1)
            for i in range(1, 8, 2):
                dve.wait_ge(sem("wq_t"), i + 1)
                dve.tensor_copy(wqT[:, i // KC, i % KC, :], ps[:, i, 0:D // 2].bitcast(BF16)).then_inc(sem("wqT_dve"), 1)
            dve.wait_ge(sem("bvo_in"), 48)

            chp, chf = chain(dve, "dve_prep", 9), chain(dve, "dve_finish", 6)

            def quant(ch, rows, am, scale, inv_, rounded):
                ch(dve.tensor_reduce(am, rows, AX.X, ALU.max, apply_absolute_value=True))
                ch(dve.tensor_scalar(scale, am, 1.0 / QMAX, 1e-8, ALU.mult, ALU.max))
                ch(dve.reciprocal(inv_, scale))
                ch(dve.tensor_scalar(rounded, rows, inv_, MAGIC, ALU.mult, ALU.add))

            def prep1(b):
                chp.turn(b)
                chp(dve.bn_stats(st6b[0:S], XR[0:S, b, :]), True)
                dve.bn_aggr(mvb[0:S], st6b[0:S]).then_inc(sem("mvB"), 1)

            def prep2(b):
                dve.wait_ge(sem("rsB"), b + 1)
                chp(dve.tensor_scalar(g2[0:S], XR[0:S, b, :], mvb[0:S, 0:1], tb[0:S, 1:2], ALU.subtract, ALU.mult))
                quant(chp, g2[0:S], tb[0:S, 3:4], tb[0:S, 4:5], tb[0:S, 5:6], xq2[0:S])
                dve.tensor_scalar(xq2b[0:S], xq2[0:S], MAGIC, None, ALU.subtract).then_inc(sem("xq2b"), 1)

            def prep3(b, j, u):
                dve.wait_ge(sem("q_mm"), b + 1)
                chp(dve.tensor_copy(sxB[:], ps[:, 6, KC * S:(KC + 1) * S]))
                chp(dve.tensor_tensor(t1[:], ps[:, 6, 0:KC * S].rearrange("p (k s) -> p k s", k=KC),
                                      sxB[:].unsqueeze(1).to_broadcast([P, KC, S]), ALU.mult))
                chp(dve.tensor_tensor(t2[:], t1[:], swqB[:], ALU.mult))
                dve.tensor_tensor(t3[:], t2[:], bqB[:], ALU.add).then_inc(sem("qf"), 1)
                dve.wait_ge(sem("qf"), b + 1)
                scores_done(dve, b - 1)
                dve.tensor_copy(qH[j][:], t3[:]).then_inc(sem("qH"), 1)
                dve.wait_ge(sem("qH"), b + 1)
                dve.tensor_tensor(qL[j][:], t3[:], qH[j][:].bitcast(F32), ALU.subtract).then_inc(sem("q_ready"), 1)
                chp.end()

            def finish1(b):
                chf.turn(b)
                for r in range(2):
                    dve.wait_ge(sem(f"pv{r}"), after((b + 1) * 8))
                o = ps[0:S, 4:6, 0:8 * (HD + 1)].rearrange("p g (h w) -> p g h w", h=8)
                chf(dve.reciprocal(rinv[0:S].rearrange("p (g h) -> p g h", g=2), o[:, :, :, HD]))
                dve.tensor_tensor(oN[0:S].rearrange("p (g h w) -> p g h w", g=2, h=8), o[:, :, :, 0:HD],
                                  rinv[0:S].rearrange("p (g h) -> p g h", g=2).unsqueeze(3)
                                  .to_broadcast([S, 2, 8, HD]), ALU.mult).then_inc(sem("o_norm"), 1)

            def finish2(b):
                dve.wait_ge(sem("o_norm"), after(b + 1))
                chf(dve.tensor_tensor(oQ[0:S], oN[0:S], bvB[0:S], ALU.add))
                quant(chf, oQ[0:S], tb[0:S, 6:7], tb[0:S, 7:8], tb[0:S, 8:9], oN[0:S])
                dve.tensor_scalar(oQb[0:S], oN[0:S], MAGIC, None, ALU.subtract).then_inc(sem("oQb"), 1)
                chf.end()

            def finish3(b):
                dve.wait_ge(sem("wo_mm"), b + 1)
                dve.scalar_tensor_tensor(out=y2[0:S], in0=ps[0:S, 6, :], scalar=tb[0:S, 7:8], in1=swoB[0:S],
                                         op0=ALU.mult, op1=ALU.mult).then_inc(sem("y2"), 1)
                dve.wait_ge(sem("y2"), b + 1)
                dve.wait_ge(sem("xbo"), b + 1)
                dve.tensor_tensor(XR[0:S, b, :], y2[0:S], xbo[0:S], ALU.add).then_inc(sem("x3"), 1)

            def body(b, j, u, first, last):
                dve.wait_ge(sem(f"mask_in{j}"), 16 * u + 16)
                for h_ in range(HEADS + 1):
                    if h_ < HEADS:
                        r, n = h_ % 2, b * 8 + h_ // 2
                        alone(dve, (f"score{r}", after(n + 1)), (f"exp{r}", after(n)))
                        dve.tensor_tensor_reduce(out=sN[0:S, r, 0:T], in0=ps[0:S, r, 0:T], in1=maskS[0:S, j, 0:T],
                                                 scale=-1.0, scalar=3.4e38, op0=ALU.add, op1=ALU.min,
                                                 accum_out=nmx[0:S, h_:h_ + 1]).then_inc(sem(f"masked{r}"), 1)
                    if h_ and not copies_on_act(h_ - 1):
                        copy_p(dve, dve.tensor_copy, b, h_ - 1)
                    if not first:
                        if h_ == 2:
                            finish1(b - 1)
                        if h_ == 4:
                            finish2(b - 1)
                        if h_ == 9:
                            finish3(b - 1)
                    if not last:
                        if h_ == 6:
                            prep1(b + 1)
                        if h_ == 8:
                            prep2(b + 1)
                        if h_ == 15:
                            prep3(b + 1, 1 - j, u + j)
                dve.tensor_copy(cols[:, 24:25], cols[:, 0:1]).then_inc(sem("mask_used"), 1)

            prep1(0)
            prep2(0)
            prep3(0, 0, 0)
            batches(dve, body)
            finish1(B - 1)
            finish2(B - 1)
            finish3(B - 1)
            dve.wait_ge(sem("x3"), after(B))
            dve.tensor_copy(cols[:, 22:23], cols[:, 1:2]).then_inc(sem("b_done"), 1)

            dve.wait_ge(sem("b_done"), 4)
            dve.wait_ge(sem("c_in"), 64)
            dve.wait_ge(sem("c_setup"), 6)
            ch = once
            for b in range(B):
                ch(dve.bn_stats(st6c[0:S, b, :], XR[0:S, b, :]))
                dve.bn_aggr(mvc[0:S, b, :], st6c[0:S, b, :]).then_inc(sem("mv_all"), 1)
            dve.wait_ge(sem("rs_all"), 2)
            for b in range(B):
                dve.tensor_scalar(z[0:S, b], XR[0:S, b, :], mvc[0:S, b, 0:1], rsc[0:S, 1, b:b + 1],
                                  ALU.subtract, ALU.mult).then_inc(sem("z"), 1)
            dve.wait_ge(sem("logit"), B)

            def over_b(v):
                return v.unsqueeze(1).to_broadcast([S, B, E])

            def over_e(v):
                return v.unsqueeze(2).to_broadcast([S, B, E])

            ch(dve.tensor_tensor(sc2[0:S], ps[0:S, 2, 0:B * E].rearrange("p (b e) -> p b e", b=B),
                                 over_b(gbB[0:S, 0]), ALU.add))
            ch(dve.tensor_tensor(sc[0:S], sc2[0:S], over_b(gbB[0:S, 1]), ALU.add))
            for k in range(TOPK):
                s_ = (sc, sc2)[k]
                ch(dve.tensor_reduce(best[0:S, k], s_[0:S], AX.X, ALU.max))
                ch(dve.tensor_tensor(cand[0:S], s_[0:S], over_e(best[0:S, k]), ALU.is_ge))
                ch(dve.scalar_tensor_tensor(out=pick[0:S], in0=cand[0:S], scalar=-float(2 * E), in1=iot[0:S],
                                            op0=ALU.mult, op1=ALU.add))
                ch(dve.tensor_reduce(first_[0:S, k], pick[0:S], AX.X, ALU.min))
                ch(dve.tensor_tensor(hot[0:S, k], pick[0:S], over_e(first_[0:S, k]), ALU.is_equal))
                if k == 0:
                    ch(dve.scalar_tensor_tensor(out=sc2[0:S], in0=hot[0:S, 0], scalar=-3e38, in1=sc[0:S],
                                                op0=ALU.mult, op1=ALU.add))
            dve.tensor_tensor(hot[0:S, 2], hot[0:S, 0], hot[0:S, 1], ALU.add).then_inc(sem("hot"), 1)
            dve.tensor_tensor(gate[0:S, 0], best[0:S, 1], best[0:S, 0], ALU.subtract).then_inc(sem("gap"), 1)
            dve.wait_ge(sem("counts"), 1)
            ch(dve.tensor_scalar(need[:, 0], ps[:, 4, 0:E], 1.0 / P, 0.5 - 0.5 / P, ALU.mult, ALU.add))
            ch(dve.tensor_scalar(need[:, 1], need[:, 0], MAGIC, None, ALU.add))
            ch(dve.tensor_scalar(need[:, 2], need[:, 1], MAGIC, None, ALU.subtract))
            ch(dve.tensor_tensor_scan(out=need[:, 3], data0=ones[:, 0:E], data1=need[:, 2], initial=0.0,
                                      op0=ALU.mult, op1=ALU.add))
            ch(dve.tensor_tensor(need[:, 4], need[:, 3], need[:, 2], ALU.subtract))
            ch(dve.scalar_tensor_tensor(out=place[0:S], in0=over_b(need[0:S, 4]), scalar=float(P),
                                        in1=ps[0:S, 3, 0:B * E].rearrange("p (b e) -> p b e", b=B),
                                        op0=ALU.mult, op1=ALU.add))
            for k in range(TOPK):
                ch(dve.tensor_tensor(pick[0:S], hot[0:S, k], place[0:S], ALU.mult))
                ch(dve.tensor_reduce(slot[0:S, k], pick[0:S], AX.X, ALU.add))
            dve.tensor_copy(slotI[0:S], slot[0:S]).then_inc(sem("slots"), 1)
            ch(dve.tensor_tensor(blk_e[:], blk_no[:], need[0:1, 3].unsqueeze(1).to_broadcast([1, NBLK, E]), ALU.is_ge))
            ch(dve.tensor_reduce(blk_f[:, 0], blk_e[:], AX.X, ALU.add))
            ch(dve.tensor_scalar(blk_f[:, 1], blk_f[:, 0], float(E - 1), None, ALU.min))
            dve.tensor_copy(blk_x[:], blk_f[:, 1]).then_inc(sem("block_experts"), 1)
            dve.wait_ge(sem("gap_exp"), 1)
            ch(dve.tensor_scalar(gate[0:S, 0], gate[0:S, 1], 1.0, None, ALU.add))
            ch(dve.reciprocal(gate[0:S, 2], gate[0:S, 0]))
            ch(dve.tensor_tensor(gate[0:S, 3], gate[0:S, 1], gate[0:S, 2], ALU.mult))
            dve.wait_ge(sem("block_experts"), 1)

            def copy_x(s, j):
                dve.wait_ge(sem("x_turned"), s + 1)
                dve.tensor_copy(xT[:, j].rearrange("p k s -> p (k s)"), ps[:, j, :]).then_inc(sem("xT"), 1)

            def step(s, j, u):
                if within(s, 0):
                    e = block_expert(mybir.EngineType.DVE, s)
                    alone(dve, ("h_mm", s + 1))
                    dve.tensor_tensor(hb[:, j], ps[:, 2 + j, 0:EH], b1B[:, e, :], ALU.add).then_inc(sem("h_biased"), 1)
                if within(s, 1):
                    copy_x(s + 1, 1 - j)

            copy_x(0, 0)
            blocks(dve, step)
            for b in range(B):
                dve.wait_ge(sem(f"back{b // 2}"), 2 * TOPK * 16)
                for k in range(TOPK):
                    ins = dve.scalar_tensor_tensor(out=XR[0:S, b, :], in0=picked[0:S, k, b, :],
                                                   scalar=gate[0:S, 2 + k, b:b + 1], in1=XR[0:S, b, :],
                                                   op0=ALU.mult, op1=ALU.add)
                    if k == 0:
                        ch(ins)
                ins.then_inc(sem("combined"), 1)


def kernel(**inputs):
    import numpy as np
    import concourse.bacc as bacc
    from concourse.bass_utils import run_bass_kernel_spmd

    a = {k: np.asarray(v) for k, v in inputs.items()}

    def chunked(w):
        return w.reshape(-1, P, w.shape[-1]).transpose(1, 0, 2)

    def column(v):
        return v.reshape(-1, P).T

    def pieces(w):
        return w.reshape(P, NW, -1).transpose(1, 0, 2)

    ctx = np.concatenate([a["ctx_2048"], np.zeros((B, TP - T, D), np.float32)], 1)
    w2e = np.concatenate([a["L1_ffn_w2"].transpose(0, 2, 1), a["L1_ffn_b2"][:, None, :],
                          np.zeros((E, 1, D), np.float32)], 1)
    laid = [
        ("x", a["x"].transpose(1, 0, 2)),
        ("ctxT", ctx.transpose(0, 2, 1).reshape(B, KC, P, TP).transpose(0, 2, 1, 3).reshape(B, P, KC * TP)),
        ("mask", a["mask_BxSxS2_ff0"]),
        ("decay", a["L0_xattn_decay"].reshape(1)),
        ("win", chunked(a["L0_xattn_W_in"].T).reshape(P, -1)),
        ("b_in", column(a["L0_xattn_b_in"])),
        ("wout", chunked(a["L0_xattn_W_out"].T).reshape(P, -1)),
        ("b_out", a["L0_xattn_b_out"]),
        ("gamma0", a["L0_xattn_gamma"]),
        ("beta0", a["L0_xattn_beta"]),
        ("w1", pieces(chunked(a["L0_ffn_w1"].T).reshape(P, -1))),
        ("w2", pieces(chunked(a["L0_ffn_w2"].T).reshape(P, -1))),
        ("gammaf", a["L0_ffn_gamma"]),
        ("wq", chunked(a["L1_xattn_wq"])),
        ("bq", column(a["L1_xattn_bq"])),
        ("wk", chunked(a["L1_xattn_wk"].T).reshape(P, -1)),
        ("bk", column(a["L1_xattn_bk"])),
        ("wv", chunked(a["L1_xattn_wv"].T).reshape(P, -1)),
        ("bv", a["L1_xattn_bv"]),
        ("wo", chunked(a["L1_xattn_wo"])),
        ("bo", a["L1_xattn_bo"]),
        ("gate_w", chunked(a["L1_ffn_gate_w"].T)),
        ("gate_b", a["L1_ffn_gate_b"]),
        ("gate_bias", a["L1_ffn_bias"]),
        ("ew1", a["L1_ffn_w1"].transpose(0, 2, 1).reshape(E, KC, P, EH).transpose(0, 2, 1, 3).reshape(E, P, KC * EH)),
        ("eb1", a["L1_ffn_b1"]),
        ("ew2", w2e.reshape(E, 3, EC, D).transpose(0, 2, 1, 3).reshape(E, EC, 3 * D)),
    ]
    nc = bacc.Bacc("TRN2", target_bir_lowering=False, num_devices=1)
    arrays, args = {}, []
    for name, v in laid:
        arrays[f"in_{name}"] = np.ascontiguousarray(v)
        args.append(nc.dram_tensor(f"in_{name}", v.shape, F32, kind="ExternalInput").ap())
    args.append(nc.dram_tensor("out_0", (B, S, D), F32, kind="ExternalOutput").ap())
    block_kernel(nc, *args)
    r = run_bass_kernel_spmd(nc, [arrays], core_ids=[0])
    return r.results[0]["out_0"]
```

```python
from contextlib import ExitStack

import concourse.bass as bass
from concourse import mybir

ALU = mybir.AluOpType
ACT = mybir.ActivationFunctionType
AX = mybir.AxisListType
F32 = mybir.dt.float32
F32R = mybir.dt.float32r
BF16 = mybir.dt.bfloat16
FP8 = mybir.dt.float8e4
I32 = mybir.dt.int32

B, S, D = 8, 100, 512
T = 361
P = 128
KC = D // P
NT = 3
TC = -(-T // NT)
TP = 364
HEADS, HD = 16, 32
HPC = P // HD
VW = HEADS * (HD + 1)
FF = 2048
FC = FF // P
NW = 4
WP = D * FF // P // NW
E, EH = 8, 352
EC = 118
EHP = 3 * EC
TOPK = 2
NBLK = (B * S * TOPK + E * (P - 1)) // P
LN_EPS, RMS_EPS = 1e-5, 1e-6
MAGIC = 1.5 * 2.0 ** 23
QMAX = 127.0


def block_kernel(nc, x, ctxT, mask, decay, win, b_in, wout, b_out, gamma0, beta0, w1, w2, gammaf,
                 wq, bq, wk, bk, wv, bv, wo, bo, gate_w, gate_b, gate_bias, ew1, eb1, ew2, out):
    with ExitStack() as whole:
        def sb(stack, name, shape, dt=F32):
            return stack.enter_context(nc.sbuf_tensor(name, shape, dt))

        sems = {}

        def sem(name):
            if name not in sems:
                sems[name] = whole.enter_context(nc.semaphore(name))
            return sems[name]

        credited = ("g1", "g2", "gelu", "hq0", "hq1", "hqT0", "k_copied", "oQT", "oQb",
                    "o_norm", "summ_used", "t1", "t2", "v_copied", "v_mm", "x1", "x2", "x3", "y_out0", "y_out1",
                    *(f"{name}{r}" for name in ("exp", "masked", "p_copied", "p_turned", "pv", "score")
                      for r in range(2)))

        def after(count):
            return count + 1

        summ_dram = nc.dram_tensor("summary_rows", [B, D], F32, kind="Internal").ap()
        slots_in = nc.dram_tensor("slots_in", [NBLK * P, D], F32, kind="Internal").ap()
        slots_out = nc.dram_tensor("slots_out", [NBLK * P, D], F32, kind="Internal").ap()
        swo_dram = nc.dram_tensor("wo_scales", [D], F32, kind="Internal").ap()

        CT = sb(whole, "CT", [P, B, KC * TP])
        VS = sb(whole, "VS", [P, B * NT * VW])
        XR = sb(whole, "XR", [P, B, D])
        ident = sb(whole, "ident", [P, P])
        identb = sb(whole, "identb", [P, P], BF16)
        ones = sb(whole, "ones", [P, P])
        before = sb(whole, "before", [P, P])
        zeros = sb(whole, "zeros", [P, P])
        cols = sb(whole, "cols", [P, 48])
        ps = whole.enter_context(nc.psum_tensor("ps", [P, 8, 512], F32))

        def vs(b):
            return VS[:, bass.ds(b * (NT * VW), NT * VW)]

        a = ExitStack()
        wkH, wkL = sb(a, "wkH", [P, KC, D], F32R), sb(a, "wkL", [P, KC, D], F32R)
        wvH, wvL = sb(a, "wvH", [P, KC, D], F32R), sb(a, "wvL", [P, KC, D], F32R)
        cxH, cxL = sb(a, "cxH", [P, KC, TP], F32R), sb(a, "cxL", [P, KC, TP], F32R)
        w1s = sb(a, "w1s", [P, KC * D])
        w2s = sb(a, "w2s", [P, KC * D])
        w1q = w1s[:].bitcast(FP8)
        w2q = w2s[:].bitcast(FP8)
        h = sb(a, "h", [P, FF])
        hq = sb(a, "hq", [P, FF], BF16)
        hqT = sb(a, "hqT", [P, FC, S], BF16)
        xq, y, xb = sb(a, "xq", [P, D]), sb(a, "y", [P, D]), sb(a, "xb", [P, D])
        xqb = sb(a, "xqb", [P, D], BF16)
        xqT = sb(a, "xqT", [P, KC, S], BF16)
        summB = sb(a, "summB", [P, D])
        gamma0B, beta0B, gammafB = sb(a, "gamma0B", [P, D]), sb(a, "beta0B", [P, D]), sb(a, "gammafB", [P, D])
        kvw, xm = sb(a, "kvw", [P, KC, B]), sb(a, "xm", [P, KC, B])
        biases = sb(a, "biases", [P, 3, KC])
        st6 = sb(a, "st6", [P, 6])
        mv = sb(a, "mv", [P, 2])
        mv0 = sb(a, "mv0", [P, B, 2])
        st0 = sb(a, "st0", [P, B, 6])
        rs0 = sb(a, "rs0", [P, B])
        tk = sb(a, "tk", [P, 24])
        asum = sb(a, "asum", [P, 2, NW])
        wsc = sb(a, "wsc", [P, 2, 4])
        cw, krow = h[:, 0:TP], h[:, TP:2 * TP]
        junk = [h[:, (2 + i) * TP:(2 + i) * TP + T] for i in range(3)]
        summ, boutB = xq[0:B, :], y[0:B, :]
        a.close()

        def stage(i):
            at = 2 * NT * VW + (i % NW) * WP
            return VS[:, at:at + WP]

        bb = ExitStack()
        staging = ExitStack()
        wst = sb(staging, "wst", [P, 2, KC, D])
        wstb = sb(staging, "wstb", [P, 2, KC, D], BF16)
        staging.close()
        KH = sb(bb, "KH", [P, KC, TP], F32R)
        qH, qL = sb(bb, "qH", [P, KC, S], F32R), sb(bb, "qL", [P, KC, S], F32R)
        K3 = sb(bb, "K3", [3 * HD, HEADS, TP], F32R)
        q3 = sb(bb, "q3", [3 * HD, HEADS, S], F32R)
        maskS = sb(bb, "maskS", [P, 2, T + 1])
        sN = sb(bb, "sN", [P, 2, TP])
        pE = sb(bb, "pE", [P, 2, NT * TC + 1])
        pT = sb(bb, "pT", [P, 2, NT, S])
        nmx = sb(bb, "nmx", [P, HEADS])
        oN = sb(bb, "oN", [P, D])
        oQb = sb(bb, "oQb", [P, D], BF16)
        oQT = sb(bb, "oQT", [P, KC, S], BF16)
        g2 = sb(bb, "g2", [P, D])
        xq2b = sb(bb, "xq2b", [P, D], BF16)
        xq2T = oQT
        xbo = sb(bb, "xbo", [P, D])
        y2 = sb(bb, "y2", [P, D])
        sxB = sb(bb, "sxB", [P, S])
        t1 = sb(bb, "qt", [P, KC, S])
        swqB, bqB = sb(bb, "swqB", [P, KC, S]), sb(bb, "bqB", [P, KC, S])
        bvB, boB, swoB = sb(bb, "bvB", [P, D]), sb(bb, "boB", [P, D]), sb(bb, "swoB", [P, D])
        wqT = sb(bb, "wqT", [P, 2, KC, D], BF16)
        wsm = sb(bb, "wsm", [P, 4, 2, KC])
        bqS = sb(bb, "bqS", [P, KC])
        st6b, mvb = sb(bb, "st6b", [P, 6]), sb(bb, "mvb", [P, 2])
        tb = sb(bb, "tb", [P, 24])
        rinv = sb(bb, "rinv", [P, HEADS])
        bb.close()

        cc = ExitStack()
        z, zT = sb(cc, "z", [P, B, D]), sb(cc, "zT", [P, 2, KC, S])
        st6c, mvc = sb(cc, "st6c", [P, B, 6]), sb(cc, "mvc", [P, B, 2])
        rsc = sb(cc, "rsc", [P, 2, B])
        gwT, gbB = sb(cc, "gwT", [P, KC, E]), sb(cc, "gbB", [P, 2, E])
        sc, sc2, cand = (sb(cc, n_, [P, B, E]) for n_ in ("sc", "sc2", "cand"))
        hot = sb(cc, "hot", [P, 3, B, E])
        best = sb(cc, "best", [P, 2, B])
        first_ = sb(cc, "first", [P, 2, B])
        iot = sb(cc, "iot", [P, B, E])
        gate = sb(cc, "gate", [P, 4, B])
        place, pick = sb(cc, "place", [P, B, E]), sb(cc, "pick", [P, B, E])
        slot, slotI = sb(cc, "slot", [P, 2, B]), sb(cc, "slotI", [P, 2, B], I32)
        need = sb(cc, "need", [P, 6, E])
        blk_e, blk_no = sb(cc, "blk_e", [1, NBLK, E]), sb(cc, "blk_no", [1, NBLK, E])
        blk_f, blk_x = sb(cc, "blk_f", [1, 2, NBLK]), sb(cc, "blk_x", [1, NBLK], I32)
        b1B = sb(cc, "b1B", [P, E, EH])
        xin, xT = sb(cc, "xin", [P, 2, D]), sb(cc, "xT", [P, 2, KC, P])
        hb, hs, hTe = sb(cc, "hb", [P, 2, EH]), sb(cc, "hs", [P, 2, EHP]), sb(cc, "hTe", [P, 2, 3, P])
        yb = sb(cc, "yb", [P, 2, D])
        picked = sb(cc, "picked", [P, 2, B, D])
        cc.close()

        C_MAGIC, C_NMAGIC, C_HALF, C_DEC, C_K, C_SUM = 0, 1, 2, 3, 4, 5
        C_EXP = 6

        def batches(eng, body):
            body(0, 0, 0, True, False)
            with eng.Fori(0, B // 2 - 1) as it:
                body(it * 2 + 1, 1, it, False, False)
                body(it * 2 + 2, 0, it + 1, False, False)
            body(B - 1, 1, B // 2 - 1, False, True)

        def passes(eng, body):
            with eng.Fori(0, B - 1) as b:
                body(b, False)
            body(B - 1, True)

        def blocks(eng, body, peeled=2):
            body(0, 0, 0)
            with eng.Fori(0, (NBLK - peeled) // 2) as it:
                body(it * 2 + 1, 1, it)
                body(it * 2 + 2, 0, it + 1)
            for s in range(NBLK + 1 - peeled, NBLK + 1):
                body(s, s % 2, s // 2)

        def started(s):
            return not isinstance(s, int) or s > 0

        def within(s, ahead):
            return not isinstance(s, int) or s + ahead < NBLK

        def block_expert(engine, s):
            return nc.values_load(blk_x[0:1, bass.ds(s, 1)], engines=[engine], min_val=0, max_val=E - 1,
                                  skip_runtime_bounds_check_because="it is a count held to E - 1 when made")

        def chain(eng, name, per):
            class Chain:
                def turn(self, t):
                    self.base, self.k = t * per, 0

                def __call__(self, ins, by_itself=False):
                    self.k += 1
                    ins.then_inc(sem(name), 1)
                    if by_itself:
                        alone(eng, (name, self.base + self.k))
                    else:
                        eng.wait_ge(sem(name), self.base + self.k)

                def end(self):
                    assert self.k == per, (name, self.k)
            return Chain()

        def head(i):
            return i % KC, i // KC, i % KC * HPC + i // KC

        TURN, MIX = 2, 3

        def behind(b, i, first):
            if i >= 0:
                return b, i
            return None if first else (b - 1, i + HEADS)

        def turn_done(eng, name, b, r):
            for q in range(2):
                eng.wait_ge(sem(f"{name}{q}"), after(b * 8 + 2 * r + 2))

        def stacked(eng, b):
            for r in range(HPC):
                eng.wait_ge(sem(f"kq_in{r}"), (b + 1) * 96)

        def alone(eng, *waits):
            for name, v in waits:
                eng.wait_ge(sem(name), v)
            eng.sem_inc(sem("gone_on"), 1)

        block = whole.enter_context(nc.Block())

        @block.sync
        def _(sp):
            sp.dma_start(cols[:, C_DEC:C_DEC + 1], decay.partition_broadcast(P)).then_inc(sem("biases_in"), 16)
            sp.dma_start(biases[:, 0, :], b_in).then_inc(sem("biases_in"), 16)
            sp.dma_start(biases[:, 1, :], bk).then_inc(sem("biases_in"), 16)
            sp.dma_start(CT[:, 0, :], ctxT[0]).then_inc(sem("ctx_in0"), 16)
            sp.dma_start(stage(0), wk).then_inc(sem("stage_in0"), 16)
            sp.dma_start(stage(1), wv).then_inc(sem("stage_in1"), 16)
            for c in range(2):
                sp.dma_start(stage(2 + c), w1[c]).then_inc(sem(f"stage_in{2 + c}"), 16)
            for b in range(1, B):
                sp.dma_start(CT[:, b, :], ctxT[b]).then_inc(sem(f"ctx_in{b}"), 16)
            sp.dma_start(w1s[:], win).then_inc(sem("win_in"), 16)
            sp.dma_start(w2s[:], wout).then_inc(sem("win_in"), 16)
            for c in range(2, NW):
                sp.wait_ge(sem("wkvL"), c - 1)
                sp.dma_start(stage(2 + c), w1[c]).then_inc(sem(f"stage_in{c - 2}"), 16)
            sp.dma_start(boutB, b_out.partition_broadcast(B)).then_inc(sem("win_in"), 16)
            sp.dma_start(XR[0:S], x).then_inc(sem("vec_in"), 16)
            for t, src in ((gamma0B, gamma0), (beta0B, beta0), (gammafB, gammaf)):
                sp.dma_start(t[0:S, :], src.partition_broadcast(S)).then_inc(sem("vec_in"), 16)
            for c in range(NW):
                sp.wait_ge(sem("ternary"), c + 1)
                sp.dma_start(stage(2 + c), w2[c]).then_inc(sem(f"stage_in{(2 + c) % NW}"), 16)
            sp.wait_ge(sem("consts"), 1)
            for i in range(NBLK // 4):
                sp.dma_start(slots_in[i * 4 * P:(i + 1) * 4 * P].rearrange("(p r) (q c) -> p (r q) c", r=4, c=P),
                             zeros[:].unsqueeze(1).to_broadcast([P, 4 * D // P, P])).then_inc(sem("slots_zero"), 16)
            sp.wait_ge(sem("summ_ready"), 1)
            sp.dma_start(summ_dram, summ).then_inc(sem("scratch_out"), 16)
            sp.wait_ge(sem("scratch_out"), 16)
            with sp.Fori(0, B) as b:
                sp.wait_ge(sem("summ_used"), after(b))
                sp.dma_start(summB[0:S], summ_dram[b].partition_broadcast(S)).then_inc(sem("summ_in"), 16)
            sp.wait_ge(sem("a_done"), 4)
            sp.dma_start(wst[:, 0], wq).then_inc(sem("wqo_in"), 16)
            sp.dma_start(wst[:, 1], wo).then_inc(sem("wqo_in"), 16)
            sp.dma_start(bqS[:], bq).then_inc(sem("wqo_in"), 16)
            for t, src in ((bvB, bv), (boB, bo)):
                sp.dma_start(t[0:S, :], src.partition_broadcast(S)).then_inc(sem("bvo_in"), 16)
            sp.wait_ge(sem("wscale"), 1)
            sp.dma_start(swo_dram.rearrange("(j p) -> p j", p=P), wsm[:, 1, 1, :], allow_slow_non_contiguous=True)\
              .then_inc(sem("scratch_out"), 16)
            sp.wait_ge(sem("scratch_out"), 32)
            sp.dma_start(swoB[0:S, :], swo_dram.partition_broadcast(S)).then_inc(sem("bvo_in"), 16)
            for j in range(2):
                sp.dma_start(maskS[0:S, j, 0:T], mask[j]).then_inc(sem(f"mask_in{j}"), 16)

            def expert_loads(b, j, more):
                stacked(sp, b)
                sp.dma_start(CT[:, b, 0:KC * EH], ew1[b]).then_inc(sem("experts_in"), 16)
                sp.wait_ge(sem("o_norm"), after(b + 1))
                sp.dma_start(vs(b)[0:EC, 0:3 * D], ew2[b]).then_inc(sem("experts_in"), 16)
                if more:
                    sp.wait_ge(sem("mask_used"), b + 1)
                    sp.dma_start(maskS[0:S, j, 0:T], mask[b + 2]).then_inc(sem(f"mask_in{j}"), 16)

            def stack(dst, parts, r):
                for i, src in enumerate(parts):
                    sp.dma_start(dst[i * HD:(i + 1) * HD, r::HPC, :].bitcast(F32), src[r * HD:(r + 1) * HD].bitcast(F32))\
                      .then_inc(sem(f"kq_in{r}"), 16)

            def stack_batch(b, first):
                low = CT[:, b, :].bitcast(F32R).rearrange("p (k t) -> p k t", k=KC)
                sp.wait_ge(sem("kL"), b + 1)
                for r in range(HPC):
                    if r == HPC - 1:
                        sp.wait_ge(sem("q_ready"), b + 1)
                        for q in range(HPC - 1):
                            stack(q3, (qH, qL, qH), q)
                    if not first:
                        turn_done(sp, "score", b - 1, r)
                    stack(K3, (KH, KH, low), r)
                stack(q3, (qH, qL, qH), HPC - 1)

            stack_batch(0, True)
            stack_batch(1, False)
            with sp.Fori(0, B // 2 - 1) as it:
                for j in range(2):
                    expert_loads(it * 2 + j, j, True)
                    stack_batch(it * 2 + j + 2, False)
            expert_loads(B - 2, 0, False)
            expert_loads(B - 1, 1, False)
            sp.wait_ge(sem("b_done"), 4)
            sp.dma_start(gwT[:], gate_w).then_inc(sem("c_in"), 16)
            sp.dma_start(gbB[0:S, 0, :], gate_b.partition_broadcast(S)).then_inc(sem("c_in"), 16)
            sp.dma_start(gbB[0:S, 1, :], gate_bias.partition_broadcast(S)).then_inc(sem("c_in"), 16)
            sp.dma_start(b1B[:], eb1.partition_broadcast(P)).then_inc(sem("c_in"), 16)

            def load_block(s, j, u):
                sp.dma_start(xin[:, j], slots_in[bass.ds(s * P, P)]).then_inc(sem(f"x_in{j}"), 16)

            sp.wait_ge(sem("sent"), 16 * TOPK * B)
            load_block(0, 0, 0)
            load_block(1, 1, 0)

            def step(s, j, u):
                if not started(s):
                    sp.wait_ge(sem("x_turned"), 1)
                    load_block(2, 0, 1)
                if within(s, 3):
                    sp.wait_ge(sem("x_turned"), s + 2)
                    load_block(s + 3, 1 - j, u + 1 + j)
                if started(s):
                    sp.wait_ge(sem("y_copied"), s)
                    sp.dma_start(slots_out[bass.ds((s - 1) * P, P)], yb[:, 1 - j]).then_inc(sem(f"y_out{1 - j}"), 16)

            blocks(sp, step, peeled=4)
            for b in range(B):
                sp.wait_ge(sem("combined"), b + 1)
                sp.dma_start(out[b], XR[0:S, b, :]).then_inc(sem("out"), 16)
            sp.wait_ge(sem("out"), 16 * B)

        @block.gpsimd
        def _(g):
            n = [0]

            def step(ins):
                n[0] += 1
                ins.then_inc(sem("pool_setup"), 1)
                g.wait_ge(sem("pool_setup"), n[0])

            step(g.iota(ident[:], [[1, P]], base=0, channel_multiplier=-1, allow_small_or_imprecise_dtypes=True))
            step(g.tensor_scalar(before[:], ident[:], 0.0, None, ALU.is_gt))
            step(g.tensor_scalar(ident[:], ident[:], 0.0, None, ALU.is_equal))
            step(g.tensor_copy(identb[:], ident[:]))
            step(g.memset(ones[:], 1.0))
            step(g.memset(zeros[:], 0.0))
            g.memset(cols[:, C_MAGIC:C_MAGIC + 1], MAGIC)
            g.memset(cols[:, C_NMAGIC:C_NMAGIC + 1], -MAGIC)
            g.memset(cols[:, C_HALF:C_HALF + 1], -0.5).then_inc(sem("consts"), 1)
            g.wait_ge(sem("consts"), 1)

            def rsqrt(dst, src, tmp, eps, tag, count, width=1):
                g.tensor_scalar(tmp, src, eps, None, ALU.add).then_inc(sem(tag + "_t"), 1)
                g.wait_ge(sem(tag + "_t"), count)
                half = cols[0:S, C_HALF:C_HALF + 1]
                half = half if width == 1 else half.to_broadcast([S, width])
                return g.tensor_tensor(dst, tmp, half, ALU.pow)

            g.wait_ge(sem("mv_all"), B)
            rsqrt(rs0[0:S, :], mv0[0:S, :, 1], rs0[0:S, :], LN_EPS, "rs_all", 1, B).then_inc(sem("rs_all"), 1)
            def norms(b):
                g.wait_ge(sem("x1"), after(b))
                g.tensor_tensor(xb[0:S], XR[0:S, b, :], beta0B[0:S], ALU.add).then_inc(sem("xb"), 1)
                alone(g, ("mvA", b * 2 + 1))
                rsqrt(tk[0:S, 1:2], mv[0:S, 1:2], tk[0:S, 0:1], LN_EPS, "rsA", b * 3 + 1).then_inc(sem("rsA"), 1)
                alone(g, ("mvA", b * 2 + 2))
                rsqrt(tk[0:S, 3:4], mv[0:S, 1:2], tk[0:S, 2:3], LN_EPS, "rsA", b * 3 + 2).then_inc(sem("rsF"), 1)
                alone(g, ("rsF", b + 1))
                g.tensor_scalar(tk[0:S, 4:5], mv[0:S, 1:2], tk[0:S, 3:4], tk[0:S, 3:4], ALU.mult, ALU.mult)\
                 .then_inc(sem("msF"), 1)
                alone(g, ("msF", b + 1))
                rsqrt(tk[0:S, 6:7], tk[0:S, 4:5], tk[0:S, 5:6], RMS_EPS, "rsA", b * 3 + 3).then_inc(sem("rms"), 1)
                alone(g, ("rms", b + 1))
                g.tensor_tensor(tk[0:S, 7:8], tk[0:S, 3:4], tk[0:S, 6:7], ALU.mult).then_inc(sem("uscale"), 1)

            def body(b, last):
                alone(g, ("h_round", b + 1), ("t2", after(b * 2)))
                g.tensor_scalar(hq[0:S, FF // 2:], h[0:S, FF // 2:], -MAGIC, 1.0, ALU.add, ALU.mult)\
                 .then_inc(sem("hq1"), 1)
                if not last:
                    norms(b + 1)
                g.wait_ge(sem("v_copied"), after((b + 1) * NT))
                g.tensor_copy(vs(b)[0:TC, :].rearrange("p (c h w) -> p c h w", c=NT, h=HEADS)[:, :, :, HD],
                              ones[0:TC, 0:NT * HEADS].rearrange("p (c h) -> p c h", c=NT))\
                 .then_inc(sem("v_ones"), 1)

            g.wait_ge(sem("vec_in"), 64)
            norms(0)
            passes(g, body)
            g.wait_ge(sem("hq1"), after(B))
            g.wait_ge(sem("v_ones"), B)
            g.tensor_copy(cols[:, 20:21], cols[:, 0:1]).then_inc(sem("a_done"), 1)
            g.wait_ge(sem("a_done"), 4)
            for i in range(2):
                g.memset(pE[0:S, i, T:NT * TC + 1], 0.0).then_inc(sem("pool_setup"), 1)

            def low_keys(b):
                g.wait_ge(sem("kH"), b + 1)
                g.tensor_tensor(CT[:, b, :].bitcast(F32R), CT[:, b, :],
                                KH[:].rearrange("p k t -> p (k t)").bitcast(F32), ALU.subtract)\
                 .then_inc(sem("kL"), 1)

            def rstd_b(b):
                alone(g, ("mvB", b + 1))
                rsqrt(tb[0:S, 1:2], mvb[0:S, 1:2], tb[0:S, 0:1], LN_EPS, "rsB_t", b + 1).then_inc(sem("rsB"), 1)

            def with_bo(b):
                g.wait_ge(sem("x3"), after(b))
                g.tensor_tensor(xbo[0:S], XR[0:S, b, :], boB[0:S], ALU.add).then_inc(sem("xbo"), 1)

            def body(b, j, u, first, last):
                if not first:
                    with_bo(b - 1)
                if not last:
                    rstd_b(b + 1)
                    low_keys(b + 1)

            low_keys(0)
            rstd_b(0)
            g.wait_ge(sem("bvo_in"), 48)
            batches(g, body)
            with_bo(B - 1)
            g.wait_ge(sem("xbo"), B)
            g.tensor_copy(cols[:, 20:21], cols[:, 1:2]).then_inc(sem("b_done"), 1)
            g.wait_ge(sem("b_done"), 4)
            g.iota(iot[:], [[0, B], [1, E]], base=0, channel_multiplier=0, allow_small_or_imprecise_dtypes=True)\
             .then_inc(sem("c_setup"), 1)
            g.iota(blk_no[:], [[1, NBLK], [0, E]], base=0, channel_multiplier=0, allow_small_or_imprecise_dtypes=True)\
             .then_inc(sem("c_setup"), 1)
            for j in range(2):
                g.memset(hs[:, j, EH:EH + 1], 1.0).then_inc(sem("c_setup"), 1)
                g.memset(hs[:, j, EH + 1:EHP], 0.0).then_inc(sem("c_setup"), 1)
            g.wait_ge(sem("mv_all"), 2 * B)
            rsqrt(rsc[0:S, 1, :], mvc[0:S, :, 1], rsc[0:S, 0, :], LN_EPS, "rs_all", 2, B).then_inc(sem("rs_all"), 1)
            g.wait_ge(sem("slots"), 1)
            g.wait_ge(sem("slots_zero"), 16 * (NBLK // 4))
            for b in range(B):
                for k in range(TOPK):
                    g.indirect_dma_start(slots_in, bass.IndirectOffsetOnAxis(slotI[0:S, k, b:b + 1], 0), z[0:S, b, :], None,
                                         bounds_check=NBLK * P - 1).then_inc(sem("sent"), 16)
            g.wait_ge(sem("y_out0"), after(16 * (NBLK // 2)))
            g.wait_ge(sem("y_out1"), after(16 * (NBLK // 2)))
            for b in range(B):
                for k in range(TOPK):
                    g.indirect_dma_start(picked[0:S, k, b, :], None, slots_out,
                                         bass.IndirectOffsetOnAxis(slotI[0:S, k, b:b + 1], 0),
                                         bounds_check=NBLK * P - 1).then_inc(sem(f"back{b // 2}"), 16)

        @block.scalar
        def _(act):
            act.wait_ge(sem("biases_in"), 48)
            act.activation(cols[:, C_EXP:C_EXP + 1], cols[:, C_DEC:C_DEC + 1], ACT.Exp, scale=-1.0)\
               .then_inc(sem("decay_exp"), 1)
            act.wait_ge(sem("stage_in0"), 16)
            act.copy(wkH[:].rearrange("p k n -> p (k n)"), stage(0)).then_inc(sem("wkvH"), 1)
            act.wait_ge(sem("stage_in1"), 16)
            act.copy(wvH[:].rearrange("p k n -> p (k n)"), stage(1)).then_inc(sem("wkvH"), 1)
            act.wait_ge(sem("consts"), 1)
            def high_context(b):
                act.copy(cxH[:].rearrange("p k t -> p (k t)"), CT[:, b, :]).then_inc(sem("cxH"), 1)

            for w in range(2):
                for c in range(NW):
                    slot = (2 + c) % NW
                    act.wait_ge(sem(f"stage_in{slot}"), 16 * (w + 1 + (slot < 2)))
                    if w + c:
                        act.wait_ge(sem("abs_sum"), NW * w + c)
                    act.activation(hq[:, 0:WP], stage(slot), ACT.Abs, accum_out=asum[:, w, c:c + 1])\
                       .then_inc(sem("abs_sum"), 1)
                if w == 1:
                    for b in range(B):
                        act.wait_ge(sem(f"ctx_in{b}"), 16)
                    high_context(0)
                act.wait_ge(sem("w_scale"), w + 1)
                for c in range(NW):
                    act.activation(stage(2 + c), stage(2 + c), ACT.Identity, bias=cols[:, C_MAGIC:C_MAGIC + 1],
                                   scale=wsc[:, w, 2:3]).then_inc(sem("w_round"), 1)

            def body(b, last):
                for m in range(KC):
                    if m == KC - 1:
                        act.wait_ge(sem("t1"), after(b + 1))
                        act.copy(xqT[:].rearrange("p k s -> p (k s)"), ps[:, 6, 0:KC * S // 2].bitcast(BF16))\
                           .then_inc(sem("xqT"), 1)
                    alone(act, ("k_mm", b * KC + m + 1))
                    act.activation(CT[:, b, m * TP:(m + 1) * TP], ps[:, m % 2, 0:TP], ACT.Identity,
                                   bias=biases[:, 1, m:m + 1]).then_inc(sem("k_copied"), 1)
                act.wait_ge(sem("dq1"), b + 1)
                act.wait_ge(sem("hq0"), after(b))
                act.wait_ge(sem("hq1"), after(b))
                for m in range(4):
                    act.wait_ge(sem("g1"), after(b * 4 + m + 1))
                    act.activation(h[0:S, m * 512:(m + 1) * 512], ps[0:S, 2 + m, :], ACT.Gelu,
                                   scale=tk[0:S, 12:13]).then_inc(sem("gelu"), 1)
                for half in range(2):
                    act.wait_ge(sem("t2"), after(b * 2 + 1 + half))
                    act.copy(hqT[:, half * 8:half * 8 + 8, :].rearrange("p k s -> p (k s)"),
                             ps[:, 6 + half, 0:4 * S].bitcast(BF16)).then_inc(sem("hqT0"), 1)
                if not last:
                    alone(act, ("v_mm", after((b + 1) * NT)))
                    high_context(b + 1)

            passes(act, body)
            act.wait_ge(sem("hqT0"), after(2 * B))
            act.copy(cols[:, 21:22], cols[:, 0:1]).then_inc(sem("a_done"), 1)
            act.wait_ge(sem("a_done"), 4)
            act.wait_ge(sem("wscale"), 2)
            for w in range(2):
                for j in range(KC):
                    act.activation(wst[:, w, j, :], wst[:, w, j, :], ACT.Identity, bias=cols[:, C_MAGIC:C_MAGIC + 1],
                                   scale=wsm[:, 2, w, j:j + 1]).then_inc(sem("wq_round"), 1)
            for i in range(0, 8, 2):
                act.wait_ge(sem("wq_t"), i + 1)
                act.copy(wqT[:, i // KC, i % KC, :], ps[:, i, 0:D // 2].bitcast(BF16)).then_inc(sem("wqT_act"), 1)

            def high_keys(b, first):
                if not first:
                    stacked(act, b - 1)
                act.copy(KH[:].rearrange("p k t -> p (k t)"), CT[:, b, :]).then_inc(sem("kH"), 1)

            def turned_x(b):
                act.wait_ge(sem("xq2_t"), b + 1)
                act.copy(xq2T[:].rearrange("p k s -> p (k s)"), ps[:, 7, 0:KC * S // 2].bitcast(BF16))\
                   .then_inc(sem("xq2T"), 1)

            def turned_o(b):
                act.wait_ge(sem("oq_t"), b + 1)
                act.copy(oQT[:].rearrange("p k s -> p (k s)"), ps[:, 7, 0:KC * S // 2].bitcast(BF16))\
                   .then_inc(sem("oQT"), 1)

            def body(b, j, u, first, last):
                for h_ in range(HEADS + (TURN if last else 0)):
                    if h_ < HEADS:
                        r, n = h_ % 2, b * 8 + h_ // 2
                        act.wait_ge(sem(f"masked{r}"), after(n + 1))
                        act.wait_ge(sem(f"p_turned{r}"), after(n))
                        act.activation(pE[0:S, r, 0:T], sN[0:S, r, 0:T], ACT.Exp, scale=-1.0,
                                       bias=nmx[0:S, h_:h_ + 1]).then_inc(sem(f"exp{r}"), 1)
                    at_turn = behind(b, h_ - TURN, first)
                    if at_turn:
                        bt, ht = at_turn
                        r, n = ht % 2, bt * 8 + ht // 2
                        act.wait_ge(sem(f"p_turned{r}"), after(n + 1))
                        act.wait_ge(sem(f"pv{r}"), after(n))
                        act.copy(pT[0:TC, r].rearrange("p c s -> p (c s)"), ps[0:TC, 2 + r, 0:NT * S])\
                           .then_inc(sem(f"p_copied{r}"), 1)
                    if h_ == 5 and not last:
                        high_keys(b + 1, False)
                    if h_ == 6 and not last:
                        turned_x(b + 1)
                    if h_ == 10 and not first:
                        turned_o(b - 1)

            act.wait_ge(sem("wq_t"), 8)
            high_keys(0, True)
            turned_x(0)
            batches(act, body)
            turned_o(B - 1)
            act.wait_ge(sem("oQT"), after(B))
            act.copy(cols[:, 21:22], cols[:, 1:2]).then_inc(sem("b_done"), 1)
            act.wait_ge(sem("b_done"), 4)
            for b in range(B):
                act.wait_ge(sem("z_t"), b + 1)
                act.copy(zT[:, b % 2].rearrange("p k s -> p (k s)"), ps[:, b % 2, 0:KC * S]).then_inc(sem("zT"), 1)
            act.wait_ge(sem("gap"), 1)
            act.activation(gate[0:S, 1], gate[0:S, 0], ACT.Exp).then_inc(sem("gap_exp"), 1)

            def step(s, j, u):
                if started(s):
                    act.wait_ge(sem("h_turned"), s)
                    act.copy(hTe[0:EC, 1 - j].rearrange("p c s -> p (c s)"), ps[0:EC, 5 - j, 0:3 * P])\
                       .then_inc(sem("hT"), 1)
                if within(s, 0):
                    act.wait_ge(sem("h_biased"), s + 1)
                    act.activation(hs[:, j, 0:EH], hb[:, j], ACT.Silu).then_inc(sem("h_act"), 1)
                if started(s):
                    act.wait_ge(sem("y_mm"), s)
                    act.wait_ge(sem(f"y_out{1 - j}"), after((u + j - 1) * 16))
                    act.copy(yb[:, 1 - j], ps[:, 7 - j, :]).then_inc(sem("y_copied"), 1)

            act.wait_ge(sem("c_setup"), 6)
            blocks(act, step)

        @block.tensor
        def _(pe):
            for name in credited:
                pe.sem_inc(sem(name), 1)
            pe.wait_ge(sem("consts"), 1)
            def weight_total(w):
                pe.wait_ge(sem("abs_sum"), NW * (w + 1))
                pe.matmul(ps[:, 5, w * NW:(w + 1) * NW], ones[:, :], asum[:, w, :], start=True, stop=True)\
                  .then_inc(sem("pe_once"), 1)

            pe.wait_ge(sem("kvw"), KC * B)
            pe.wait_ge(sem("win_in"), 48)
            for m in range(KC):
                for k in range(KC):
                    mm = pe.matmul(ps[:, 7, m * B:(m + 1) * B], w1s[:, k * D + m * P:k * D + (m + 1) * P], kvw[:, k, :],
                                   start=(k == 0), stop=(k == KC - 1))
            mm.then_inc(sem("pe_once"), 1)
            weight_total(0)
            pe.wait_ge(sem("xm"), 1)
            for k in range(KC):
                mm = pe.matmul(ps[0:B, 6, :], xm[:, k, :], w2s[:, k * D:(k + 1) * D], start=(k == 0), stop=(k == KC - 1))
            mm.then_inc(sem("pe_once"), 1)
            weight_total(1)
            pe.wait_ge(sem("summ_ready"), 1)
            pe.wait_ge(sem("wkvL"), 2)

            def keys(b, m):
                if m < 2:
                    pe.wait_ge(sem("v_copied"), after(b * NT))
                else:
                    pe.wait_ge(sem("k_copied"), after(b * KC + m - 1))
                n = 0
                for wt, cx in ((wkH, cxH), (wkL, cxH), (wkH, cxL)):
                    for k in range(KC):
                        mm = pe.matmul(ps[:, m % 2, 0:TP], wt[:, k, m * P:(m + 1) * P], cx[:, k, :],
                                       start=(n == 0), stop=(n == 3 * KC - 1))
                        n += 1
                mm.then_inc(sem("k_mm"), 1)

            def values(b, c):
                if c < 2:
                    pe.wait_ge(sem("k_copied"), after(b * KC + c + 3))
                else:
                    pe.wait_ge(sem("v_copied"), after(b * NT + 1))
                n = 0
                for cx, wt in ((cxH, wvH), (cxH, wvL), (cxL, wvH)):
                    for k in range(KC):
                        mm = pe.matmul(ps[0:TC, c % 2, :], cx[:, k, c * TC:(c + 1) * TC], wt[:, k, :],
                                       start=(n == 0), stop=(n == 3 * KC - 1))
                        n += 1
                mm.then_inc(sem("v_mm"), 1)

            def body(b, last):
                pe.wait_ge(sem("cxL"), b + 1)
                for m in range(KC - 1):
                    keys(b, m)
                pe.wait_ge(sem("xqb"), b + 1)
                pe.wait_ge(sem("hqT0"), after(b * 2))
                for k in range(KC):
                    mm = pe.transpose(ps[:, 6, k * S // 2:(k + 1) * S // 2].bitcast(BF16), xqb[0:S, k * P:(k + 1) * P],
                                      identb[0:S, 0:S])
                mm.then_inc(sem("t1"), 1)
                keys(b, KC - 1)
                alone(pe, ("xqT", b + 1), ("ternary", NW), ("gelu", after(b * 4)))
                for m in range(4):
                    for k in range(KC):
                        mm = pe.matmul(ps[0:S, 2 + m, :], xqT[:, k, :], w1q[:, k * FF + m * 512:k * FF + (m + 1) * 512],
                                       start=(k == 0), stop=(k == KC - 1))
                    mm.then_inc(sem("g1"), 1)
                values(b, 0)
                values(b, 1)
                pe.wait_ge(sem("hq0"), after(b + 1))
                pe.wait_ge(sem("hq1"), after(b + 1))
                pe.wait_ge(sem("x2"), after(b))
                for half in range(2):
                    for k in range(8):
                        mm = pe.transpose(ps[:, 6 + half, k * S // 2:(k + 1) * S // 2].bitcast(BF16),
                                          hq[0:S, (half * 8 + k) * P:(half * 8 + k + 1) * P], identb[0:S, 0:S])
                    mm.then_inc(sem("t2"), 1)
                values(b, 2)
                alone(pe, ("hqT0", after(b * 2 + 2)), ("ternary", 2 * NW))
                for k in range(FC):
                    mm = pe.matmul(ps[0:S, 7, :], hqT[:, k, :], w2q[:, k * D:(k + 1) * D],
                                   start=(k == 0), stop=(k == FC - 1))
                mm.then_inc(sem("g2"), 1)

            passes(pe, body)
            pe.wait_ge(sem("x2"), after(B))
            pe.matmul(ps[:, 0, 0:1], ones[:, :], ones[:, 0:1], start=True, stop=True).then_inc(sem("a_done"), 1)
            pe.wait_ge(sem("a_done"), 4)
            for i in range(8):
                w, k = divmod(i, KC)
                pe.wait_ge(sem("wq_b"), (w + 1) * KC)
                for j in range(KC):
                    mm = pe.transpose(ps[:, i, j * P // 2:(j + 1) * P // 2].bitcast(BF16),
                                      wstb[:, w, j, k * P:(k + 1) * P], identb[:, :])
                mm.then_inc(sem("wq_t"), 1)
            pe.wait_ge(sem("wqT_act"), 4)
            pe.wait_ge(sem("wqT_dve"), 4)

            def turn_rows(src, name, b):
                for k in range(KC):
                    mm = pe.transpose(ps[:, 7, k * S // 2:(k + 1) * S // 2].bitcast(BF16), src[0:S, k * P:(k + 1) * P],
                                      identb[0:S, 0:S])
                mm.then_inc(sem(name), 1)

            def queries(b):
                pe.wait_ge(sem("xq2T"), b + 1)
                pe.transpose(ps[:, 6, KC * S:(KC + 1) * S], tb[0:S, 4:5].to_broadcast([S, P]), ident[0:S, 0:S])
                for m in range(KC):
                    for k in range(KC):
                        mm = pe.matmul(ps[:, 6, m * S:(m + 1) * S], wqT[:, 0, k, m * P:(m + 1) * P], xq2T[:, k, :],
                                       start=(k == 0), stop=(k == KC - 1))
                mm.then_inc(sem("q_mm"), 1)

            def out_rows(b):
                pe.wait_ge(sem("oQT"), after(b + 1))
                for k in range(KC):
                    mm = pe.matmul(ps[0:S, 6, :], oQT[:, k, :], wqT[:, 1, k, :], start=(k == 0), stop=(k == KC - 1))
                mm.then_inc(sem("wo_mm"), 1)

            def body(b, j, u, first, last):
                for h_ in range(HEADS + (MIX if last else 0)):
                    if h_ < HEADS:
                        r, n, hd = h_ % 2, b * 8 + h_ // 2, head(h_)[2]
                        if h_ % KC == 0:
                            pe.wait_ge(sem(f"kq_in{h_ // KC}"), (b + 1) * 96)
                        pe.wait_ge(sem(f"masked{r}"), after(n))
                        pe.matmul(ps[0:S, r, 0:TP], q3[:, hd, :], K3[:, hd, :], start=True, stop=True)\
                          .then_inc(sem(f"score{r}"), 1)
                    at_turn = behind(b, h_ - TURN, first)
                    if at_turn and at_turn[1] < HEADS:
                        bt, ht = at_turn
                        r, n = ht % 2, bt * 8 + ht // 2
                        pe.wait_ge(sem(f"exp{r}"), after(n + 1))
                        pe.wait_ge(sem(f"p_copied{r}"), after(n))
                        for c in range(NT):
                            mm = pe.transpose(ps[0:TC, 2 + r, c * S:(c + 1) * S], pE[0:S, r, c * TC:(c + 1) * TC],
                                              ident[0:S, 0:S])
                        mm.then_inc(sem(f"p_turned{r}"), 1)
                    at_mix = behind(b, h_ - MIX, first)
                    if at_mix:
                        bm, hh = at_mix
                        r, n, hd = hh % 2, bm * 8 + hh // 2, head(hh)[2]
                        pe.wait_ge(sem(f"p_copied{r}"), after(n + 1))
                        if hh == 0:
                            pe.wait_ge(sem("o_norm"), after(bm))
                        for c in range(NT):
                            at = c * VW + hd * (HD + 1)
                            mm = pe.matmul(ps[0:S, 4 + hd // 8, hd % 8 * (HD + 1):(hd % 8 + 1) * (HD + 1)],
                                           pT[0:TC, r, c, :], vs(bm)[0:TC, at:at + HD + 1],
                                           start=(c == 0), stop=(c == NT - 1))
                        mm.then_inc(sem(f"pv{r}"), 1)
                    if h_ == 5 and not last:
                        pe.wait_ge(sem("xq2b"), b + 2)
                        if not first:
                            pe.wait_ge(sem("oQT"), after(b - 1))
                        turn_rows(xq2b, "xq2_t", b + 1)
                    if h_ == 7 and not last:
                        if not first:
                            pe.wait_ge(sem("x3"), after(b - 1))
                        queries(b + 1)
                    if h_ == 9 and not first:
                        if not last:
                            pe.wait_ge(sem("xq2T"), b + 2)
                        pe.wait_ge(sem("oQb"), after(b))
                        turn_rows(oQb, "oq_t", b - 1)
                    if h_ == 11 and not first:
                        if not last:
                            pe.wait_ge(sem("q_ready"), b + 2)
                        out_rows(b - 1)

            pe.wait_ge(sem("xq2b"), 1)
            turn_rows(xq2b, "xq2_t", 0)
            queries(0)
            batches(pe, body)
            pe.wait_ge(sem("oQb"), after(B))
            turn_rows(oQb, "oq_t", B - 1)
            out_rows(B - 1)
            pe.wait_ge(sem("x3"), after(B))
            pe.matmul(ps[:, 0, 0:1], ones[:, :], ones[:, 0:1], start=True, stop=True).then_inc(sem("b_done"), 1)
            pe.wait_ge(sem("b_done"), 4)
            pe.wait_ge(sem("experts_in"), 32 * E)
            pe.wait_ge(sem("c_in"), 64)
            for b in range(B + 1):
                if b < B:
                    pe.wait_ge(sem("z"), b + 1)
                    for k in range(KC):
                        mm = pe.transpose(ps[:, b % 2, k * S:(k + 1) * S], z[0:S, b, k * P:(k + 1) * P],
                                          ident[0:S, 0:S])
                    mm.then_inc(sem("z_t"), 1)
                if b:
                    pe.wait_ge(sem("zT"), b)
                    for k in range(KC):
                        mm = pe.matmul(ps[0:S, 2, (b - 1) * E:b * E], zT[:, (b - 1) % 2, k, :], gwT[:, k, :],
                                       start=(k == 0), stop=(k == KC - 1))
                    mm.then_inc(sem("logit"), 1)
            pe.wait_ge(sem("hot"), 1)
            both = hot[0:S, 2].rearrange("p b e -> p (b e)")
            pe.matmul(ps[0:S, 3, 0:B * E], before[0:S, 0:S], both, start=True, stop=False)
            for d in range(1, B):
                pe.matmul(ps[0:S, 3, d * E:B * E], ones[0:S, 0:S], both[:, 0:(B - d) * E],
                          start=False, stop=(d == B - 1))
            for b in range(B):
                mm = pe.matmul(ps[:, 4, 0:E], ones[0:S, :], both[:, b * E:(b + 1) * E], start=(b == 0), stop=(b == B - 1))
            mm.then_inc(sem("counts"), 1)

            def turn_x(s, j, u):
                pe.wait_ge(sem(f"x_in{j}"), u * 16 + 16)
                for k in range(KC):
                    mm = pe.transpose(ps[:, j, k * P:(k + 1) * P], xin[:, j, k * P:(k + 1) * P], ident[:, :])
                mm.then_inc(sem("x_turned"), 1)

            def step(s, j, u):
                if within(s, 0):
                    e = block_expert(mybir.EngineType.PE, s)
                    pe.wait_ge(sem("xT"), s + 1)
                    for k in range(KC):
                        mm = pe.matmul(ps[:, 2 + j, 0:EH], xT[:, j, k, :], CT[:, e, k * EH:(k + 1) * EH],
                                       start=(k == 0), stop=(k == KC - 1))
                    mm.then_inc(sem("h_mm"), 1)
                if started(s):
                    pe.wait_ge(sem("h_act"), s)
                    for c in range(3):
                        mm = pe.transpose(ps[0:EC, 5 - j, c * P:(c + 1) * P], hs[:, 1 - j, c * EC:(c + 1) * EC], ident[:, :])
                    mm.then_inc(sem("h_turned"), 1)
                if within(s, 1):
                    turn_x(s + 1, 1 - j, u + j)
                if started(s):
                    e = block_expert(mybir.EngineType.PE, s - 1)
                    pe.wait_ge(sem("hT"), s)
                    for c in range(3):
                        mm = pe.matmul(ps[:, 7 - j, :], hTe[0:EC, 1 - j, c, :], vs(e)[0:EC, c * D:(c + 1) * D],
                                       start=(c == 0), stop=(c == 2))
                    mm.then_inc(sem("y_mm"), 1)

            pe.wait_ge(sem("block_experts"), 1)
            turn_x(0, 0, 0)
            blocks(pe, step)

        @block.vector
        def _(dve):
            ch = once = chain(dve, "dve_once", 0)
            ch.turn(0)
            ch(dve.memset(krow, 1.0))
            dve.wait_ge(sem("decay_exp"), 1)
            ch(dve.tensor_scalar(cols[:, C_K:C_K + 1], cols[:, C_EXP:C_EXP + 1], 1.0, None, ALU.add))
            ch(dve.reciprocal(cols[:, C_K + 2:C_K + 3], cols[:, C_K:C_K + 1]))
            ch(dve.tensor_scalar(y[:, 0:T], krow[:, 0:T], cols[:, C_K + 2:C_K + 3], None, ALU.mult))
            ch(dve.tensor_tensor_scan(out=xq[:, T - 1::-1], data0=y[:, 0:T], data1=krow[:, 0:T],
                                      initial=0.0, op0=ALU.mult, op1=ALU.add))
            ch(dve.tensor_scalar(cw[:, 0:T], xq[:, 0:T], 1.0 / T, None, ALU.mult))
            ch(dve.tensor_reduce(cols[:, C_SUM:C_SUM + 1], cw[:, 0:T], AX.X, ALU.add))
            dve.wait_ge(sem("biases_in"), 48)
            ch(dve.tensor_scalar(biases[:, 2, :], biases[:, 0, :], cols[:, C_SUM:C_SUM + 1], None, ALU.mult))
            for i, (hi, lo) in enumerate(((wkH, wkL), (wvH, wvL))):
                dve.wait_ge(sem("wkvH"), i + 1)
                dve.tensor_tensor(lo[:].rearrange("p k n -> p (k n)"), stage(i),
                                  hi[:].rearrange("p k n -> p (k n)").bitcast(F32), ALU.subtract)\
                   .then_inc(sem("wkvL"), 1)
            for b in range(B):
                dve.wait_ge(sem(f"ctx_in{b}"), 16)
                for k in range(KC):
                    i = b * KC + k
                    if i >= 3:
                        dve.wait_ge(sem("kvw"), i - 2)
                    dve.tensor_tensor_reduce(out=junk[i % 3], in0=CT[:, b, k * TP:k * TP + T], in1=cw[:, 0:T],
                                             scale=1.0, scalar=0.0, op0=ALU.mult, op1=ALU.add,
                                             accum_out=kvw[:, k, b:b + 1]).then_inc(sem("kvw"), 1)
            def w_scale(w):
                dve.wait_ge(sem("pe_once"), 2 * w + 2)
                ch(dve.tensor_reduce(wsc[:, w, 0:1], ps[:, 5, w * NW:(w + 1) * NW], AX.X, ALU.add))
                ch(dve.tensor_scalar(wsc[:, w, 1:2], wsc[:, w, 0:1], 1.0 / (D * FF), 1e-5, ALU.mult, ALU.max))
                dve.reciprocal(wsc[:, w, 2:3], wsc[:, w, 1:2]).then_inc(sem("w_scale"), 1)

            def ternary(w):
                dst = (w1q, w2q)[w]
                for c in range(NW):
                    dve.wait_ge(sem("w_round"), NW * w + c + 1)
                    ch(dve.tensor_scalar(stage(2 + c), stage(2 + c), MAGIC - 1.0, MAGIC + 1.0, ALU.max, ALU.min))
                    dve.tensor_scalar(dst[:, c * WP:(c + 1) * WP], stage(2 + c), MAGIC, None, ALU.subtract,
                                      saturate=False).then_inc(sem("ternary"), 1)

            dve.wait_ge(sem("pe_once"), 1)
            dve.tensor_tensor(xm[:], ps[:, 7, 0:KC * B].rearrange("p (k b) -> p k b", k=KC),
                              biases[:, 2, :].unsqueeze(2).to_broadcast([P, KC, B]), ALU.add).then_inc(sem("xm"), 1)
            w_scale(0)
            ternary(0)
            dve.wait_ge(sem("vec_in"), 64)
            for b in range(B):
                ch(dve.bn_stats(st0[0:S, b, :], XR[0:S, b, :]))
                dve.bn_aggr(mv0[0:S, b, :], st0[0:S, b, :]).then_inc(sem("mv_all"), 1)
            dve.wait_ge(sem("pe_once"), 3)
            dve.wait_ge(sem("win_in"), 48)
            dve.tensor_tensor(summ, ps[0:B, 6, :], boutB, ALU.add).then_inc(sem("summ_ready"), 1)

            def low_context(b):
                dve.wait_ge(sem("cxH"), b + 1)
                dve.tensor_tensor(cxL[:].rearrange("p k t -> p (k t)"), CT[:, b, :],
                                  cxH[:].rearrange("p k t -> p (k t)").bitcast(F32), ALU.subtract)\
                   .then_inc(sem("cxL"), 1)

            low_context(0)
            w_scale(1)
            ternary(1)
            dve.wait_ge(sem("w_scale"), 2)
            dve.wait_ge(sem("rs_all"), 1)

            chr_, ch = chain(dve, "dve_rows", 8), chain(dve, "dve_a", 7)

            def rows(b):
                chr_.turn(b)
                xr = XR[0:S, b, :]
                dve.wait_ge(sem("summ_in"), 16 * b + 16)
                dve.scalar_tensor_tensor(out=y[0:S], in0=xr, scalar=rs0[0:S, bass.ds(b, 1)], in1=summB[0:S],
                                         op0=ALU.mult, op1=ALU.add).then_inc(sem("summ_used"), 1)
                dve.wait_ge(sem("summ_used"), after(b + 1))
                chr_(dve.bn_stats(st6[0:S], y[0:S]), True)
                dve.bn_aggr(mv[0:S], st6[0:S]).then_inc(sem("mvA"), 1)
                dve.wait_ge(sem("mvA"), b * 2 + 1)
                chr_(dve.scalar_tensor_tensor(out=xq[0:S], in0=y[0:S], scalar=mv[0:S, 0:1], in1=gamma0B[0:S],
                                              op0=ALU.subtract, op1=ALU.mult))
                dve.wait_ge(sem("rsA"), b + 1)
                dve.wait_ge(sem("xb"), b + 1)
                dve.scalar_tensor_tensor(out=xr, in0=xq[0:S], scalar=tk[0:S, 1:2], in1=xb[0:S],
                                         op0=ALU.mult, op1=ALU.add).then_inc(sem("x1"), 1)

            def ffn_rows(b):
                xr = XR[0:S, b, :]
                alone(dve, ("x1", after(b + 1)))
                chr_(dve.bn_stats(st6[0:S], xr), True)
                dve.bn_aggr(mv[0:S], st6[0:S]).then_inc(sem("mvA"), 1)
                dve.wait_ge(sem("mvA"), b * 2 + 2)
                chr_(dve.scalar_tensor_tensor(out=y[0:S], in0=xr, scalar=mv[0:S, 0:1], in1=gammafB[0:S],
                                              op0=ALU.subtract, op1=ALU.mult))
                chr_(dve.tensor_reduce(tk[0:S, 8:9], y[0:S], AX.X, ALU.max, apply_absolute_value=True))
                dve.wait_ge(sem("uscale"), b + 1)
                dve.tensor_scalar(tk[0:S, 9:10], tk[0:S, 8:9], tk[0:S, 7:8], 1e-5, ALU.mult, ALU.max)\
                   .then_inc(sem("u_max"), 1)
                dve.wait_ge(sem("u_max"), b + 1)
                chr_(dve.reciprocal(tk[0:S, 10:11], tk[0:S, 9:10]))
                chr_(dve.tensor_scalar(tk[0:S, 11:12], tk[0:S, 10:11], tk[0:S, 7:8], QMAX, ALU.mult, ALU.mult))
                chr_(dve.tensor_scalar(xq[0:S], y[0:S], tk[0:S, 11:12], MAGIC, ALU.mult, ALU.add))
                dve.wait_ge(sem("t1"), after(b))
                dve.tensor_scalar(xqb[0:S], xq[0:S], MAGIC, None, ALU.subtract).then_inc(sem("xqb"), 1)
                chr_.end()

            def body(b, last):
                ch.turn(b)
                xr = XR[0:S, b, :]
                dve.wait_ge(sem("gelu"), after(b * 4))
                dve.tensor_scalar(tk[0:S, 12:13], tk[0:S, 9:10], wsc[0:S, 0, 1:2], 1.0 / QMAX, ALU.mult, ALU.mult)\
                   .then_inc(sem("dq1"), 1)
                for m in range(4):
                    dve.wait_ge(sem("gelu"), after(b * 4 + m + 1))
                    ins = dve.tensor_reduce(tk[0:S, 14 + m:15 + m], h[0:S, m * 512:(m + 1) * 512], AX.X, ALU.max,
                                            apply_absolute_value=True)
                ch(ins)
                ch(dve.tensor_reduce(tk[0:S, 18:19], tk[0:S, 14:18], AX.X, ALU.max))
                ch(dve.tensor_scalar(tk[0:S, 19:20], tk[0:S, 18:19], 1e-5, None, ALU.max))
                ch(dve.reciprocal(tk[0:S, 20:21], tk[0:S, 19:20]))
                ch(dve.tensor_scalar(tk[0:S, 21:22], tk[0:S, 20:21], QMAX, None, ALU.mult))
                dve.tensor_scalar(h[0:S, FF // 2:], h[0:S, FF // 2:], tk[0:S, 21:22], MAGIC, ALU.mult, ALU.add)\
                   .then_inc(sem("h_round"), 1)
                ch(dve.tensor_scalar(h[0:S, 0:FF // 2], h[0:S, 0:FF // 2], tk[0:S, 21:22], MAGIC, ALU.mult, ALU.add))
                dve.wait_ge(sem("t2"), after(b * 2))
                dve.tensor_scalar(hq[0:S, 0:FF // 2], h[0:S, 0:FF // 2], MAGIC, None, ALU.subtract)\
                   .then_inc(sem("hq0"), 1)
                for c in range(NT):
                    if c == NT - 1 and not last:
                        rows(b + 1)
                    dve.wait_ge(sem("v_mm"), after(b * NT + c + 1))
                    dve.tensor_copy(vs(b)[0:TC, c * VW:(c + 1) * VW].rearrange("p (h w) -> p h w", h=HEADS)[:, :, 0:HD],
                                    ps[0:TC, c % 2, :].rearrange("p (h w) -> p h w", h=HEADS))\
                       .then_inc(sem("v_copied"), 1)
                if not last:
                    low_context(b + 1)
                ch(dve.tensor_scalar(tk[0:S, 22:23], tk[0:S, 19:20], wsc[0:S, 1, 1:2], 1.0 / QMAX, ALU.mult, ALU.mult))
                if not last:
                    ffn_rows(b + 1)
                dve.wait_ge(sem("g2"), after(b + 1))
                dve.scalar_tensor_tensor(out=xr, in0=ps[0:S, 7, :], scalar=tk[0:S, 22:23], in1=xr,
                                         op0=ALU.mult, op1=ALU.add).then_inc(sem("x2"), 1)
                ch.end()

            rows(0)
            ffn_rows(0)
            passes(dve, body)
            dve.wait_ge(sem("x2"), after(B))
            dve.tensor_copy(cols[:, 22:23], cols[:, 0:1]).then_inc(sem("a_done"), 1)

            dve.wait_ge(sem("a_done"), 4)
            ch = once
            dve.wait_ge(sem("wqo_in"), 48)
            for w in range(2):
                for j in range(KC):
                    ins = dve.tensor_reduce(wsm[:, 0, w, j:j + 1], wst[:, w, j, :], AX.X, ALU.max,
                                            apply_absolute_value=True)
            ch(ins)
            dve.tensor_scalar(wsm[:, 1], wsm[:, 0], 1.0 / QMAX, 1e-8, ALU.mult, ALU.max).then_inc(sem("wscale"), 1)
            dve.wait_ge(sem("wscale"), 1)
            dve.reciprocal(wsm[:, 2], wsm[:, 1]).then_inc(sem("wscale"), 1)
            dve.wait_ge(sem("wqo_in"), 48)
            inv = float(HD) ** -0.5
            for m in range(KC):
                dve.tensor_scalar(swqB[:, m, :], ones[:, 0:S], wsm[:, 1, 0, m:m + 1], inv, ALU.mult, ALU.mult)
                ch(dve.tensor_scalar(bqB[:, m, :], ones[:, 0:S], bqS[:, m:m + 1], inv, ALU.mult, ALU.mult))
            for i in range(8):
                dve.wait_ge(sem("wq_round"), i + 1)
                dve.tensor_scalar(wstb[:, i // KC, i % KC, :], wst[:, i // KC, i % KC, :], MAGIC, None, ALU.subtract)\
                   .then_inc(sem("wq_b"), 1)
            for i in range(1, 8, 2):
                dve.wait_ge(sem("wq_t"), i + 1)
                dve.tensor_copy(wqT[:, i // KC, i % KC, :], ps[:, i, 0:D // 2].bitcast(BF16)).then_inc(sem("wqT_dve"), 1)
            dve.wait_ge(sem("bvo_in"), 48)

            chp, chf = chain(dve, "dve_prep", 11), chain(dve, "dve_finish", 7)

            def row_scale(ch, rows, am, scale, inv_):
                ch(dve.tensor_reduce(am, rows, AX.X, ALU.max, apply_absolute_value=True))
                ch(dve.tensor_scalar(scale, am, 1.0 / QMAX, 1e-8, ALU.mult, ALU.max))
                ch(dve.reciprocal(inv_, scale))

            def prep_stats(b):
                chp.turn(b)
                chp(dve.bn_stats(st6b[0:S], XR[0:S, b, :]), True)
                dve.bn_aggr(mvb[0:S], st6b[0:S]).then_inc(sem("mvB"), 1)

            def prep_norm(b):
                dve.wait_ge(sem("rsB"), b + 1)
                chp(dve.tensor_scalar(g2[0:S], XR[0:S, b, :], mvb[0:S, 0:1], tb[0:S, 1:2], ALU.subtract, ALU.mult))

            def prep_scale(b):
                row_scale(chp, g2[0:S], tb[0:S, 3:4], tb[0:S, 4:5], tb[0:S, 5:6])

            def prep_round(b):
                chp(dve.tensor_scalar(g2[0:S], g2[0:S], tb[0:S, 5:6], MAGIC, ALU.mult, ALU.add))
                dve.tensor_scalar(xq2b[0:S], g2[0:S], MAGIC, None, ALU.subtract).then_inc(sem("xq2b"), 1)

            def prep_rescale(b):
                dve.wait_ge(sem("q_mm"), b + 1)
                chp(dve.tensor_copy(sxB[:], ps[:, 6, KC * S:(KC + 1) * S]))
                chp(dve.tensor_tensor(t1[:], ps[:, 6, 0:KC * S].rearrange("p (k s) -> p k s", k=KC),
                                      sxB[:].unsqueeze(1).to_broadcast([P, KC, S]), ALU.mult))

            def prep_bias(b):
                chp(dve.tensor_tensor(t1[:], t1[:], swqB[:], ALU.mult))
                chp(dve.tensor_tensor(t1[:], t1[:], bqB[:], ALU.add))

            def prep_split(b, first):
                if not first:
                    stacked(dve, b - 1)
                chp(dve.tensor_copy(qH[:], t1[:]))
                dve.tensor_tensor(qL[:], t1[:], qH[:].bitcast(F32), ALU.subtract).then_inc(sem("q_ready"), 1)
                chp.end()

            def finish1(b):
                chf.turn(b)
                for r in range(2):
                    dve.wait_ge(sem(f"pv{r}"), after((b + 1) * 8))
                o = ps[0:S, 4:6, 0:8 * (HD + 1)].rearrange("p g (h w) -> p g h w", h=8)
                chf(dve.reciprocal(rinv[0:S].rearrange("p (g h) -> p g h", g=2), o[:, :, :, HD]))
                dve.tensor_tensor(oN[0:S].rearrange("p (g h w) -> p g h w", g=2, h=8), o[:, :, :, 0:HD],
                                  rinv[0:S].rearrange("p (g h) -> p g h", g=2).unsqueeze(3)
                                  .to_broadcast([S, 2, 8, HD]), ALU.mult).then_inc(sem("o_norm"), 1)

            def finish2(b):
                dve.wait_ge(sem("o_norm"), after(b + 1))
                chf(dve.tensor_tensor(oN[0:S], oN[0:S], bvB[0:S], ALU.add))

            def finish3(b):
                row_scale(chf, oN[0:S], tb[0:S, 6:7], tb[0:S, 7:8], tb[0:S, 8:9])

            def finish4(b):
                chf(dve.tensor_scalar(oN[0:S], oN[0:S], tb[0:S, 8:9], MAGIC, ALU.mult, ALU.add))
                dve.tensor_scalar(oQb[0:S], oN[0:S], MAGIC, None, ALU.subtract).then_inc(sem("oQb"), 1)

            def finish5(b):
                dve.wait_ge(sem("wo_mm"), b + 1)
                chf(dve.scalar_tensor_tensor(out=y2[0:S], in0=ps[0:S, 6, :], scalar=tb[0:S, 7:8], in1=swoB[0:S],
                                             op0=ALU.mult, op1=ALU.mult))
                chf.end()
                dve.wait_ge(sem("xbo"), b + 1)
                dve.tensor_tensor(XR[0:S, b, :], y2[0:S], xbo[0:S], ALU.add).then_inc(sem("x3"), 1)

            def body(b, j, u, first, last):
                dve.wait_ge(sem(f"mask_in{j}"), 16 * u + 16)
                for h_ in range(HEADS + 1):
                    if h_ < HEADS:
                        r, n = h_ % 2, b * 8 + h_ // 2
                        alone(dve, (f"score{r}", after(n + 1)), (f"exp{r}", after(n)))
                        dve.tensor_tensor_reduce(out=sN[0:S, r, 0:T], in0=ps[0:S, r, 0:T], in1=maskS[0:S, j, 0:T],
                                                 scale=-1.0, scalar=3.4e38, op0=ALU.add, op1=ALU.min,
                                                 accum_out=nmx[0:S, h_:h_ + 1]).then_inc(sem(f"masked{r}"), 1)
                    if not first and h_ in finish_at:
                        finish_at[h_](b - 1)
                    if not last and h_ in prep_at:
                        prep_at[h_](b + 1)
                dve.tensor_copy(cols[:, 24:25], cols[:, 0:1]).then_inc(sem("mask_used"), 1)

            finish_at = {2: finish1, 5: finish2, 6: finish3, 7: finish4, 13: finish5}
            prep_at = {0: prep_stats, 2: prep_norm, 3: prep_scale, 4: prep_round,
                       8: prep_rescale, 9: prep_bias, 10: lambda b: prep_split(b, False)}
            prep_stats(0)
            prep_norm(0)
            prep_scale(0)
            prep_round(0)
            prep_rescale(0)
            prep_bias(0)
            prep_split(0, True)
            batches(dve, body)
            for step in finish_at.values():
                step(B - 1)
            dve.wait_ge(sem("x3"), after(B))
            dve.tensor_copy(cols[:, 22:23], cols[:, 1:2]).then_inc(sem("b_done"), 1)

            dve.wait_ge(sem("b_done"), 4)
            dve.wait_ge(sem("c_in"), 64)
            dve.wait_ge(sem("c_setup"), 6)
            ch = once
            for b in range(B):
                ch(dve.bn_stats(st6c[0:S, b, :], XR[0:S, b, :]))
                dve.bn_aggr(mvc[0:S, b, :], st6c[0:S, b, :]).then_inc(sem("mv_all"), 1)
            dve.wait_ge(sem("rs_all"), 2)
            for b in range(B):
                dve.tensor_scalar(z[0:S, b], XR[0:S, b, :], mvc[0:S, b, 0:1], rsc[0:S, 1, b:b + 1],
                                  ALU.subtract, ALU.mult).then_inc(sem("z"), 1)
            dve.wait_ge(sem("logit"), B)

            def over_b(v):
                return v.unsqueeze(1).to_broadcast([S, B, E])

            def over_e(v):
                return v.unsqueeze(2).to_broadcast([S, B, E])

            ch(dve.tensor_tensor(sc2[0:S], ps[0:S, 2, 0:B * E].rearrange("p (b e) -> p b e", b=B),
                                 over_b(gbB[0:S, 0]), ALU.add))
            ch(dve.tensor_tensor(sc[0:S], sc2[0:S], over_b(gbB[0:S, 1]), ALU.add))
            for k in range(TOPK):
                s_ = (sc, sc2)[k]
                ch(dve.tensor_reduce(best[0:S, k], s_[0:S], AX.X, ALU.max))
                ch(dve.tensor_tensor(cand[0:S], s_[0:S], over_e(best[0:S, k]), ALU.is_ge))
                ch(dve.scalar_tensor_tensor(out=pick[0:S], in0=cand[0:S], scalar=-float(2 * E), in1=iot[0:S],
                                            op0=ALU.mult, op1=ALU.add))
                ch(dve.tensor_reduce(first_[0:S, k], pick[0:S], AX.X, ALU.min))
                ch(dve.tensor_tensor(hot[0:S, k], pick[0:S], over_e(first_[0:S, k]), ALU.is_equal))
                if k == 0:
                    ch(dve.scalar_tensor_tensor(out=sc2[0:S], in0=hot[0:S, 0], scalar=-3e38, in1=sc[0:S],
                                                op0=ALU.mult, op1=ALU.add))
            dve.tensor_tensor(hot[0:S, 2], hot[0:S, 0], hot[0:S, 1], ALU.add).then_inc(sem("hot"), 1)
            dve.tensor_tensor(gate[0:S, 0], best[0:S, 1], best[0:S, 0], ALU.subtract).then_inc(sem("gap"), 1)
            dve.wait_ge(sem("counts"), 1)
            ch(dve.tensor_scalar(need[:, 0], ps[:, 4, 0:E], 1.0 / P, 0.5 - 0.5 / P, ALU.mult, ALU.add))
            ch(dve.tensor_scalar(need[:, 1], need[:, 0], MAGIC, None, ALU.add))
            ch(dve.tensor_scalar(need[:, 2], need[:, 1], MAGIC, None, ALU.subtract))
            ch(dve.tensor_tensor_scan(out=need[:, 3], data0=ones[:, 0:E], data1=need[:, 2], initial=0.0,
                                      op0=ALU.mult, op1=ALU.add))
            ch(dve.tensor_tensor(need[:, 4], need[:, 3], need[:, 2], ALU.subtract))
            ch(dve.scalar_tensor_tensor(out=place[0:S], in0=over_b(need[0:S, 4]), scalar=float(P),
                                        in1=ps[0:S, 3, 0:B * E].rearrange("p (b e) -> p b e", b=B),
                                        op0=ALU.mult, op1=ALU.add))
            for k in range(TOPK):
                ch(dve.tensor_tensor(pick[0:S], hot[0:S, k], place[0:S], ALU.mult))
                ch(dve.tensor_reduce(slot[0:S, k], pick[0:S], AX.X, ALU.add))
            dve.tensor_copy(slotI[0:S], slot[0:S]).then_inc(sem("slots"), 1)
            ch(dve.tensor_tensor(blk_e[:], blk_no[:], need[0:1, 3].unsqueeze(1).to_broadcast([1, NBLK, E]), ALU.is_ge))
            ch(dve.tensor_reduce(blk_f[:, 0], blk_e[:], AX.X, ALU.add))
            ch(dve.tensor_scalar(blk_f[:, 1], blk_f[:, 0], float(E - 1), None, ALU.min))
            dve.tensor_copy(blk_x[:], blk_f[:, 1]).then_inc(sem("block_experts"), 1)
            dve.wait_ge(sem("gap_exp"), 1)
            ch(dve.tensor_scalar(gate[0:S, 0], gate[0:S, 1], 1.0, None, ALU.add))
            ch(dve.reciprocal(gate[0:S, 2], gate[0:S, 0]))
            ch(dve.tensor_tensor(gate[0:S, 3], gate[0:S, 1], gate[0:S, 2], ALU.mult))
            dve.wait_ge(sem("block_experts"), 1)

            def copy_x(s, j):
                dve.wait_ge(sem("x_turned"), s + 1)
                dve.tensor_copy(xT[:, j].rearrange("p k s -> p (k s)"), ps[:, j, :]).then_inc(sem("xT"), 1)

            def step(s, j, u):
                if within(s, 0):
                    e = block_expert(mybir.EngineType.DVE, s)
                    alone(dve, ("h_mm", s + 1))
                    dve.tensor_tensor(hb[:, j], ps[:, 2 + j, 0:EH], b1B[:, e, :], ALU.add).then_inc(sem("h_biased"), 1)
                if within(s, 1):
                    copy_x(s + 1, 1 - j)

            copy_x(0, 0)
            blocks(dve, step)
            for b in range(B):
                dve.wait_ge(sem(f"back{b // 2}"), 2 * TOPK * 16)
                for k in range(TOPK):
                    ins = dve.scalar_tensor_tensor(out=XR[0:S, b, :], in0=picked[0:S, k, b, :],
                                                   scalar=gate[0:S, 2 + k, b:b + 1], in1=XR[0:S, b, :],
                                                   op0=ALU.mult, op1=ALU.add)
                    if k == 0:
                        ch(ins)
                ins.then_inc(sem("combined"), 1)


def kernel(**inputs):
    import numpy as np
    import concourse.bacc as bacc
    from concourse.bass_utils import run_bass_kernel_spmd

    a = {k: np.asarray(v) for k, v in inputs.items()}

    def chunked(w):
        return w.reshape(-1, P, w.shape[-1]).transpose(1, 0, 2)

    def column(v):
        return v.reshape(-1, P).T

    def pieces(w):
        return w.reshape(P, NW, -1).transpose(1, 0, 2)

    ctx = np.concatenate([a["ctx_2048"], np.zeros((B, TP - T, D), np.float32)], 1)
    w2e = np.concatenate([a["L1_ffn_w2"].transpose(0, 2, 1), a["L1_ffn_b2"][:, None, :],
                          np.zeros((E, 1, D), np.float32)], 1)
    laid = [
        ("x", a["x"].transpose(1, 0, 2)),
        ("ctxT", ctx.transpose(0, 2, 1).reshape(B, KC, P, TP).transpose(0, 2, 1, 3).reshape(B, P, KC * TP)),
        ("mask", a["mask_BxSxS2_ff0"]),
        ("decay", a["L0_xattn_decay"].reshape(1)),
        ("win", chunked(a["L0_xattn_W_in"].T).reshape(P, -1)),
        ("b_in", column(a["L0_xattn_b_in"])),
        ("wout", chunked(a["L0_xattn_W_out"].T).reshape(P, -1)),
        ("b_out", a["L0_xattn_b_out"]),
        ("gamma0", a["L0_xattn_gamma"]),
        ("beta0", a["L0_xattn_beta"]),
        ("w1", pieces(chunked(a["L0_ffn_w1"].T).reshape(P, -1))),
        ("w2", pieces(chunked(a["L0_ffn_w2"].T).reshape(P, -1))),
        ("gammaf", a["L0_ffn_gamma"]),
        ("wq", chunked(a["L1_xattn_wq"])),
        ("bq", column(a["L1_xattn_bq"])),
        ("wk", chunked(a["L1_xattn_wk"].T).reshape(P, -1)),
        ("bk", column(a["L1_xattn_bk"])),
        ("wv", chunked(a["L1_xattn_wv"].T).reshape(P, -1)),
        ("bv", a["L1_xattn_bv"]),
        ("wo", chunked(a["L1_xattn_wo"])),
        ("bo", a["L1_xattn_bo"]),
        ("gate_w", chunked(a["L1_ffn_gate_w"].T)),
        ("gate_b", a["L1_ffn_gate_b"]),
        ("gate_bias", a["L1_ffn_bias"]),
        ("ew1", a["L1_ffn_w1"].transpose(0, 2, 1).reshape(E, KC, P, EH).transpose(0, 2, 1, 3).reshape(E, P, KC * EH)),
        ("eb1", a["L1_ffn_b1"]),
        ("ew2", w2e.reshape(E, 3, EC, D).transpose(0, 2, 1, 3).reshape(E, EC, 3 * D)),
    ]
    nc = bacc.Bacc("TRN2", target_bir_lowering=False, num_devices=1)
    arrays, args = {}, []
    for name, v in laid:
        arrays[f"in_{name}"] = np.ascontiguousarray(v)
        args.append(nc.dram_tensor(f"in_{name}", v.shape, F32, kind="ExternalInput").ap())
    args.append(nc.dram_tensor("out_0", (B, S, D), F32, kind="ExternalOutput").ap())
    block_kernel(nc, *args)
    r = run_bass_kernel_spmd(nc, [arrays], core_ids=[0])
    return r.results[0]["out_0"]
```
